# Optimizing a Trainium2 kernel written in Bass

```python
import numpy as np
import jax
import jax.numpy as jnp

def _softmax(x, axis=-1):
    return jax.nn.softmax(x, axis=axis)

def _gelu(x):
    return jax.nn.gelu(x, approximate=True)

def _silu(x):
    return jax.nn.silu(x)

def _sigmoid(x):
    return jax.nn.sigmoid(x)

def _layernorm(x, axis=-1, eps=1e-05):
    m = jnp.mean(x, axis=axis, keepdims=True)
    v = jnp.var(x, axis=axis, keepdims=True)
    return (x - m) / jnp.sqrt(v + eps)

def _scatter_add(tgt, idx, src, axis=0):
    return tgt.at[idx].add(src)

def _segment_sum(src, seg, n):
    return jax.ops.segment_sum(src, seg, n)
kernel_name = 'mk_adaln_ffn_d4_seqx_r8_c23475'

def setup_inputs(seed: int=0):
    np.random.seed(seed)
    _w = jnp.asarray

    def _rec_inputs():
        import jax
        import jax.numpy as jnp
        _rk = jax.random.key(seed)
        x = -7.109e-05 + 0.9999 * jax.random.normal(jax.random.fold_in(_rk, 1), (32, 32, 128), jnp.float32)
        _lenS = 32 - jax.random.randint(jax.random.fold_in(_rk, 7), (32,), 0, max(1, 32 // 4) + 1, jnp.int32)
        _lenS2 = 32 - jax.random.randint(jax.random.fold_in(_rk, 8), (32,), 0, max(1, 32 // 4) + 1, jnp.int32)
        itok_B_0_8 = jax.random.randint(jax.random.fold_in(_rk, 11), (32,), 0, 9, jnp.int32)
        itok_B_0_2 = jax.random.randint(jax.random.fold_in(_rk, 12), (32,), 0, 3, jnp.int32)
        condB_tauraws = -5.74692 + 0.777674 * jax.random.normal(jax.random.fold_in(_rk, 13), (32,), jnp.float32)
        cond_256 = -0.000235209 + 0.019331 * jax.random.normal(jax.random.fold_in(_rk, 14), (32, 32), jnp.float32)
        condB_bn2 = jnp.zeros((32,), jnp.float32)
        cond_1024 = -4.10585e-05 + 0.0199478 * jax.random.normal(jax.random.fold_in(_rk, 16), (32, 128), jnp.float32)
        itok_B_0_7 = jax.random.randint(jax.random.fold_in(_rk, 17), (32,), 0, 8, jnp.int32)
        return (x, itok_B_0_8, itok_B_0_2, condB_tauraws, cond_256, condB_bn2, cond_1024, itok_B_0_7)
    x, itok_B_0_8, itok_B_0_2, condB_tauraws, cond_256, condB_bn2, cond_1024, itok_B_0_7 = _rec_inputs()

    def _L0_cond_setup():
        import jax, jax.numpy as jnp
        import numpy as np
        LN_EPS = 1e-05
        key = jax.random.key(seed)
        ks = jax.random.split(key, 8)
        B, S, H, A, L = (32, 256, 128, 32, 10)
        return {'hidden_states': jax.random.normal(ks[0], (B, S, H), dtype=jnp.float32), 'language_ids': jax.random.randint(ks[1], (B,), 0, L, dtype=jnp.int64), 'W1': jax.random.normal(ks[2], (L, H, A), dtype=jnp.float32) * (1.0 / np.sqrt(H)), 'b1': jnp.zeros((L, A), dtype=jnp.float32), 'W2': jax.random.normal(ks[3], (L, A, H), dtype=jnp.float32) * (1.0 / np.sqrt(A)), 'b2': jnp.zeros((L, H), dtype=jnp.float32), 'gamma': jnp.ones((L, H), dtype=jnp.float32), 'beta': jnp.zeros((L, H), dtype=jnp.float32)}
    _L0_cond_all = _L0_cond_setup()
    _L0_cond_in = {k: v for k, v in _L0_cond_all.items() if k in ('W1', 'b1', 'W2', 'b2', 'gamma', 'beta')}
    del _L0_cond_all

    def _L0_ffn_setup():
        import jax, jax.numpy as jnp
        import numpy as np
        E = 16
        K = 2
        LOAD = 1.0

        def _dispatch(xb, pb, cap):
            T, C = xb.shape
            top_k_probs, ei = jax.lax.top_k(pb, K)
            flat = ei.swapaxes(0, 1).ravel()
            one_hot = jax.nn.one_hot(flat, E, dtype=jnp.int32)
            pos = jnp.cumsum(one_hot, axis=0) * one_hot
            pos = pos.reshape(K, T, E).swapaxes(0, 1)
            pos = jnp.max(pos, axis=-1) - 1
            ei2 = flat.reshape(K, T).swapaxes(0, 1)
            xr = jnp.repeat(xb, K, axis=0)
            buf = jnp.zeros((E, cap, C), xb.dtype)
            buf = buf.at[ei2.ravel(), pos.ravel()].set(xr, mode='drop')
            return (top_k_probs, pos, ei2, buf)

        def _collect(eo_b, ei_b, pos_b, tk_b):
            out = eo_b[ei_b, pos_b]
            return jnp.sum(tk_b[..., None] * out, axis=1)
        key = jax.random.key(seed)
        k1, k2, k3, k4, k5 = jax.random.split(key, 5)
        B, T, C, H = (8, 512, 128, 64)
        n_layer = 12
        x = jax.random.normal(k1, (B, T, C), dtype=jnp.float32)
        w_router = jax.random.normal(k2, (C, E), dtype=jnp.float32) * 0.02
        w_fc = jax.random.normal(k3, (E, C, H), dtype=jnp.float32) * 0.02
        w_gate = jax.random.normal(k4, (E, C, H), dtype=jnp.float32) * 0.02
        w_proj = jax.random.normal(k5, (E, H, C), dtype=jnp.float32) * (0.02 * (2 * n_layer) ** (-0.5))
        return {'x': x, 'w_router': w_router, 'w_fc': w_fc, 'w_gate': w_gate, 'w_proj': w_proj}
    _L0_ffn_all = _L0_ffn_setup()
    _L0_ffn_in = {k: v for k, v in _L0_ffn_all.items() if k in ('w_router', 'w_fc', 'w_gate', 'w_proj')}
    del _L0_ffn_all

    def _L1_cond_setup():
        import jax, jax.numpy as jnp
        import numpy as np
        NEG_INF = -1e+30
        key = jax.random.key(seed)
        k1, k2, k3, k4, k5 = jax.random.split(key, 5)
        B, S, D, A = (16, 128, 128, 32)
        hidden = jax.random.normal(k1, (B, S, D), dtype=jnp.float32)
        W1 = jax.random.normal(k2, (D, A), dtype=jnp.float32) / np.sqrt(D)
        b1 = jax.random.normal(k3, (A,), dtype=jnp.float32) * 0.01
        v = jax.random.normal(k4, (A,), dtype=jnp.float32) / np.sqrt(A)
        prompt_type_ids = jax.random.randint(k5, (B,), 0, 3, dtype=jnp.int32)
        return {'hidden': hidden, 'W1': W1, 'b1': b1, 'v': v, 'prompt_type_ids': prompt_type_ids}
    _L1_cond_all = _L1_cond_setup()
    _L1_cond_in = {k: v for k, v in _L1_cond_all.items() if k in ('W1', 'b1', 'v')}
    del _L1_cond_all

    def _L1_ffn_setup():
        import jax, jax.numpy as jnp
        import numpy as np
        B, L, H, E, FF, C = (4, 256, 128, 8, 512, 2)
        key = jax.random.key(seed)
        ks = jax.random.split(key, 6)
        s = 0.02
        return {'x': jax.random.normal(ks[0], (B, L, H), dtype=jnp.float32), 'Wg': jax.random.normal(ks[1], (H, E), dtype=jnp.float32) * s, 'W1': jax.random.normal(ks[2], (E, H, FF), dtype=jnp.float32) * s, 'b1': jnp.zeros((E, FF), dtype=jnp.float32), 'W2': jax.random.normal(ks[3], (E, FF, H), dtype=jnp.float32) * s, 'b2': jnp.zeros((E, H), dtype=jnp.float32)}
    _L1_ffn_all = _L1_ffn_setup()
    _L1_ffn_in = {k: v for k, v in _L1_ffn_all.items() if k in ('Wg', 'W1', 'b1', 'W2', 'b2')}
    del _L1_ffn_all

    def _L2_cond_setup():
        import jax, jax.numpy as jnp
        import numpy as np
        import math
        B, T, E, D = (4, 256, 128, 4)

        def _tau_init(t):
            a = 0.1 ** (1.0 / max(t - 1, 1))
            tt = -math.log(max(a, 1e-10))
            return math.log(math.exp(tt) - 1 + 1e-10)

        def causal_ema(b, tau_raw):
            alpha = jnp.exp(-jax.nn.softplus(tau_raw)).astype(b.dtype)

            def step(h, bt):
                h = alpha * h + bt
                return (h, h)
            h0 = jnp.zeros((b.shape[0], b.shape[2]), b.dtype)
            _, hs = jax.lax.scan(step, h0, jnp.swapaxes(b, 0, 1))
            return jnp.swapaxes(hs, 0, 1)
        key = jax.random.key(seed)
        ks = jax.random.split(key, 10)
        s = 0.02
        return {'x': jax.random.normal(ks[0], (B, T, E), jnp.float32), 'tau_ctx': jnp.float32(_tau_init(max(T // 2, 4))), 'tau_raws': jnp.array([_tau_init(max(T // 2 ** i, 2)) for i in range(D)], jnp.float32), 'Wg': jax.random.normal(ks[1], (E, 2 * E), jnp.float32) * s, 'bg': jnp.full((E,), -0.5, jnp.float32), 'Wn1': jax.random.normal(ks[2], (E // 4, E), jnp.float32) * s, 'bn1': jnp.zeros((E // 4,), jnp.float32), 'Wn2': jax.random.normal(ks[3], (D, E // 4), jnp.float32) * s, 'bn2': jnp.zeros((D,), jnp.float32), 'blend': jax.random.normal(ks[4], (D, E), jnp.float32) * s, 'Wsoma': jax.random.normal(ks[5], (E, E), jnp.float32) * s, 'bsoma': jnp.zeros((E,), jnp.float32), 'Wtemp': jax.random.normal(ks[6], (E, E), jnp.float32) * s, 'btemp': jnp.zeros((E,), jnp.float32), 'Wout': jax.random.normal(ks[7], (E, E), jnp.float32) * s, 'gamma': jnp.ones((E,), jnp.float32), 'beta': jnp.zeros((E,), jnp.float32)}
    _L2_cond_all = _L2_cond_setup()
    _L2_cond_in = {k: v for k, v in _L2_cond_all.items() if k in ('tau_ctx', 'Wg', 'bg', 'Wn1', 'bn1', 'Wsoma', 'bsoma', 'Wtemp', 'btemp', 'Wout', 'gamma', 'beta')}
    del _L2_cond_all

    def _L2_ffn_setup():
        import jax, jax.numpy as jnp
        import numpy as np
        D_MODEL, D_FF, RANK = (128, 512, 32)
        B, S = (4, 512)
        key = jax.random.key(seed)
        ks = jax.random.split(key, 7)
        return {'x': jax.random.normal(ks[0], (B, S, D_MODEL), dtype=jnp.float32), 'U1': jax.random.normal(ks[1], (D_MODEL, RANK), dtype=jnp.float32) * 0.02, 'V1': jax.random.normal(ks[2], (RANK, D_FF), dtype=jnp.float32) * 0.02, 'b1': jnp.zeros((D_FF,), dtype=jnp.float32), 'U2': jax.random.normal(ks[3], (D_FF, RANK), dtype=jnp.float32) * 0.02, 'V2': jax.random.normal(ks[4], (RANK, D_MODEL), dtype=jnp.float32) * 0.02, 'b2': jnp.zeros((D_MODEL,), dtype=jnp.float32)}
    _L2_ffn_all = _L2_ffn_setup()
    _L2_ffn_in = {k: v for k, v in _L2_ffn_all.items() if k in ('U1', 'V1', 'b1', 'U2', 'V2', 'b2')}
    del _L2_ffn_all

    def _L3_cond_setup():
        import jax, jax.numpy as jnp
        import numpy as np
        S, O, H = (8, 128, 128)
        B, N = (32, 64)
        key = jax.random.key(seed)
        k1, k2, k3, k4 = jax.random.split(key, 4)
        x = jax.random.normal(k1, (B, N, H), dtype=jnp.float32)
        subject_id = jax.random.randint(k2, (B,), 0, S)
        wbound = jnp.sqrt(2.0 / 6.0) * jnp.sqrt(3.0 / H)
        weight = jax.random.uniform(k3, (S, O, H), minval=-wbound, maxval=wbound, dtype=jnp.float32)
        bbound = 1.0 / jnp.sqrt(H)
        bias = jax.random.uniform(k4, (S, O), minval=-bbound, maxval=bbound, dtype=jnp.float32)
        return {'x': x, 'subject_id': subject_id, 'weight': weight, 'bias': bias}
    _L3_cond_all = _L3_cond_setup()
    _L3_cond_in = {k: v for k, v in _L3_cond_all.items() if k in ('weight', 'bias')}
    del _L3_cond_all

    def _L3_ffn_setup():
        import jax, jax.numpy as jnp
        import numpy as np
        D_MODEL, D_FF, N_EXPERTS, TOP_K = (128, 256, 8, 2)
        B, S = (2, 256)
        key = jax.random.key(seed)
        ks = jax.random.split(key, 6)
        sd = 1.0 / np.sqrt(D_MODEL)
        sf = 1.0 / np.sqrt(D_FF)
        return {'x': jax.random.normal(ks[0], (B, S, D_MODEL), jnp.float32), 'router_w': jax.random.normal(ks[1], (N_EXPERTS, D_MODEL), jnp.float32) * sd, 'gate_w': jax.random.normal(ks[2], (N_EXPERTS, D_MODEL, D_FF), jnp.float32) * sd, 'gate_b': jnp.zeros((N_EXPERTS, D_FF), jnp.float32), 'up_w': jax.random.normal(ks[3], (N_EXPERTS, D_MODEL, D_FF), jnp.float32) * sd, 'up_b': jnp.zeros((N_EXPERTS, D_FF), jnp.float32), 'down_w': jax.random.normal(ks[4], (N_EXPERTS, D_FF, D_MODEL), jnp.float32) * sf, 'down_b': jnp.zeros((N_EXPERTS, D_MODEL), jnp.float32)}
    _L3_ffn_all = _L3_ffn_setup()
    _L3_ffn_in = {k: v for k, v in _L3_ffn_all.items() if k in ('router_w', 'gate_w', 'gate_b', 'up_w', 'up_b', 'down_w', 'down_b')}
    del _L3_ffn_all
    return {'x': x, 'itok_B_0_8': itok_B_0_8, 'itok_B_0_2': itok_B_0_2, 'condB_tauraws': condB_tauraws, 'cond_256': cond_256, 'condB_bn2': condB_bn2, 'cond_1024': cond_1024, 'itok_B_0_7': itok_B_0_7, 'L0_cond_W1': _L0_cond_in['W1'], 'L0_cond_b1': _L0_cond_in['b1'], 'L0_cond_W2': _L0_cond_in['W2'], 'L0_cond_b2': _L0_cond_in['b2'], 'L0_cond_gamma': _L0_cond_in['gamma'], 'L0_cond_beta': _L0_cond_in['beta'], 'L0_ffn_w_router': _L0_ffn_in['w_router'], 'L0_ffn_w_fc': _L0_ffn_in['w_fc'], 'L0_ffn_w_gate': _L0_ffn_in['w_gate'], 'L0_ffn_w_proj': _L0_ffn_in['w_proj'], 'L1_cond_W1': _L1_cond_in['W1'], 'L1_cond_b1': _L1_cond_in['b1'], 'L1_cond_v': _L1_cond_in['v'], 'L1_ffn_Wg': _L1_ffn_in['Wg'], 'L1_ffn_W1': _L1_ffn_in['W1'], 'L1_ffn_b1': _L1_ffn_in['b1'], 'L1_ffn_W2': _L1_ffn_in['W2'], 'L1_ffn_b2': _L1_ffn_in['b2'], 'L2_cond_tau_ctx': _L2_cond_in['tau_ctx'], 'L2_cond_Wg': _L2_cond_in['Wg'], 'L2_cond_bg': _L2_cond_in['bg'], 'L2_cond_Wn1': _L2_cond_in['Wn1'], 'L2_cond_bn1': _L2_cond_in['bn1'], 'L2_cond_Wsoma': _L2_cond_in['Wsoma'], 'L2_cond_bsoma': _L2_cond_in['bsoma'], 'L2_cond_Wtemp': _L2_cond_in['Wtemp'], 'L2_cond_btemp': _L2_cond_in['btemp'], 'L2_cond_Wout': _L2_cond_in['Wout'], 'L2_cond_gamma': _L2_cond_in['gamma'], 'L2_cond_beta': _L2_cond_in['beta'], 'L2_ffn_U1': _L2_ffn_in['U1'], 'L2_ffn_V1': _L2_ffn_in['V1'], 'L2_ffn_b1': _L2_ffn_in['b1'], 'L2_ffn_U2': _L2_ffn_in['U2'], 'L2_ffn_V2': _L2_ffn_in['V2'], 'L2_ffn_b2': _L2_ffn_in['b2'], 'L3_cond_weight': _L3_cond_in['weight'], 'L3_cond_bias': _L3_cond_in['bias'], 'L3_ffn_router_w': _L3_ffn_in['router_w'], 'L3_ffn_gate_w': _L3_ffn_in['gate_w'], 'L3_ffn_gate_b': _L3_ffn_in['gate_b'], 'L3_ffn_up_w': _L3_ffn_in['up_w'], 'L3_ffn_up_b': _L3_ffn_in['up_b'], 'L3_ffn_down_w': _L3_ffn_in['down_w'], 'L3_ffn_down_b': _L3_ffn_in['down_b']}

def reference(x, itok_B_0_8, itok_B_0_2, condB_tauraws, cond_256, condB_bn2, cond_1024, itok_B_0_7, L0_cond_W1, L0_cond_b1, L0_cond_W2, L0_cond_b2, L0_cond_gamma, L0_cond_beta, L0_ffn_w_router, L0_ffn_w_fc, L0_ffn_w_gate, L0_ffn_w_proj, L1_cond_W1, L1_cond_b1, L1_cond_v, L1_ffn_Wg, L1_ffn_W1, L1_ffn_b1, L1_ffn_W2, L1_ffn_b2, L2_cond_tau_ctx, L2_cond_Wg, L2_cond_bg, L2_cond_Wn1, L2_cond_bn1, L2_cond_Wsoma, L2_cond_bsoma, L2_cond_Wtemp, L2_cond_btemp, L2_cond_Wout, L2_cond_gamma, L2_cond_beta, L2_ffn_U1, L2_ffn_V1, L2_ffn_b1, L2_ffn_U2, L2_ffn_V2, L2_ffn_b2, L3_cond_weight, L3_cond_bias, L3_ffn_router_w, L3_ffn_gate_w, L3_ffn_gate_b, L3_ffn_up_w, L3_ffn_up_b, L3_ffn_down_w, L3_ffn_down_b):
    import jax
    import jax.numpy as jnp

    def _L0_cond_ref(hidden_states, language_ids, W1, b1, W2, b2, gamma, beta):
        import jax, jax.numpy as jnp
        import numpy as np
        LN_EPS = 1e-05
        w1 = W1[language_ids]
        w2 = W2[language_ids]
        h = jnp.einsum('bsh,bha->bsa', hidden_states, w1) + b1[language_ids][:, None, :]
        h = jax.nn.relu(h)
        adapted = jnp.einsum('bsa,bah->bsh', h, w2) + b2[language_ids][:, None, :]
        x = hidden_states + adapted
        mean = jnp.mean(x, axis=-1, keepdims=True)
        var = jnp.mean(jnp.square(x - mean), axis=-1, keepdims=True)
        normed = (x - mean) * jax.lax.rsqrt(var + LN_EPS)
        return normed * gamma[language_ids][:, None, :] + beta[language_ids][:, None, :]

    def _L0_ffn_ref(x, w_router, w_fc, w_gate, w_proj):
        import jax, jax.numpy as jnp
        import numpy as np
        E = 16
        K = 2
        LOAD = 1.0

        def _dispatch(xb, pb, cap):
            T, C = xb.shape
            top_k_probs, ei = jax.lax.top_k(pb, K)
            flat = ei.swapaxes(0, 1).ravel()
            one_hot = jax.nn.one_hot(flat, E, dtype=jnp.int32)
            pos = jnp.cumsum(one_hot, axis=0) * one_hot
            pos = pos.reshape(K, T, E).swapaxes(0, 1)
            pos = jnp.max(pos, axis=-1) - 1
            ei2 = flat.reshape(K, T).swapaxes(0, 1)
            xr = jnp.repeat(xb, K, axis=0)
            buf = jnp.zeros((E, cap, C), xb.dtype)
            buf = buf.at[ei2.ravel(), pos.ravel()].set(xr, mode='drop')
            return (top_k_probs, pos, ei2, buf)

        def _collect(eo_b, ei_b, pos_b, tk_b):
            out = eo_b[ei_b, pos_b]
            return jnp.sum(tk_b[..., None] * out, axis=1)
        B, T, C = x.shape
        cap = int(LOAD * K * max(1, T / E))
        g = jnp.einsum('btc,ce->bte', x, w_router)
        gate_probs = jax.nn.softmax(g, axis=-1)
        top_k_probs, positions, indices, expert_inputs = jax.vmap(lambda xb, pb: _dispatch(xb, pb, cap))(x, gate_probs)
        expert_inputs = jnp.swapaxes(expert_inputs, 0, 1).reshape(E, B * cap, C)
        gg = jnp.einsum('enc,ech->enh', expert_inputs, w_gate)
        h = jnp.einsum('enc,ech->enh', expert_inputs, w_fc)
        h = jax.nn.silu(gg) * h
        o = jnp.einsum('enh,ehc->enc', h, w_proj)
        expert_outputs = jnp.swapaxes(o.reshape(E, B, cap, C), 0, 1)
        y = jax.vmap(_collect)(expert_outputs, indices, positions, top_k_probs)
        return y

    def _L1_cond_ref(hidden, W1, b1, v, prompt_type_ids):
        import jax, jax.numpy as jnp
        import numpy as np
        NEG_INF = -1e+30
        B, S, D = hidden.shape
        attn_in = jnp.tanh(jnp.einsum('bsd,da->bsa', hidden, W1) + b1)
        scores = jnp.einsum('bsa,a->bs', attn_in, v)
        idx = jnp.arange(S)
        j = idx[:, None]
        l = idx[None, :]
        prefix_m = l <= j
        postfix_m = l >= j
        cloze_m = l != j
        pt = prompt_type_ids[:, None, None]
        mask = jnp.where(pt == 0, prefix_m[None], jnp.where(pt == 1, postfix_m[None], cloze_m[None]))
        masked_scores = jnp.where(mask, scores[:, None, :], NEG_INF)
        p = jax.nn.softmax(masked_scores, axis=-1)
        cnt = jnp.sum(mask, axis=-1).astype(hidden.dtype)
        pooled = jnp.einsum('bjl,bld->bjd', p, hidden) / cnt[..., None]
        return pooled

    def _L1_ffn_ref(x, Wg, W1, b1, W2, b2):
        import jax, jax.numpy as jnp
        import numpy as np
        B, L, H, E, FF, C = (4, 256, 128, 8, 512, 2)
        b, l, h = x.shape
        e = Wg.shape[1]
        n = b * l
        k = min(max(int(n * C / e), 1), n)
        xt = x.reshape(n, h)
        S = jax.nn.sigmoid(xt @ Wg).T
        G, I = jax.lax.top_k(S, k)
        ex = xt[I]
        hid = jax.nn.gelu(jnp.einsum('ekh,ehf->ekf', ex, W1) + b1[:, None, :], approximate=False)
        out = (jnp.einsum('ekf,efh->ekh', hid, W2) + b2[:, None, :]) * G[..., None]
        new_x = jnp.zeros_like(xt).at[I.reshape(-1)].add(out.reshape(-1, h))
        return new_x.reshape(b, l, h)

    def _L2_cond_ref(x, tau_ctx, tau_raws, Wg, bg, Wn1, bn1, Wn2, bn2, blend, Wsoma, bsoma, Wtemp, btemp, Wout, gamma, beta):
        import jax, jax.numpy as jnp
        import numpy as np
        import math
        B, T, E, D = (4, 256, 128, 4)

        def _tau_init(t):
            a = 0.1 ** (1.0 / max(t - 1, 1))
            tt = -math.log(max(a, 1e-10))
            return math.log(math.exp(tt) - 1 + 1e-10)

        def causal_ema(b, tau_raw):
            alpha = jnp.exp(-jax.nn.softplus(tau_raw)).astype(b.dtype)

            def step(h, bt):
                h = alpha * h + bt
                return (h, h)
            h0 = jnp.zeros((b.shape[0], b.shape[2]), b.dtype)
            _, hs = jax.lax.scan(step, h0, jnp.swapaxes(b, 0, 1))
            return jnp.swapaxes(hs, 0, 1)
        ctx = causal_ema(x, tau_ctx)
        gate_in = jnp.concatenate([x, ctx], axis=-1)
        wg = jax.nn.sigmoid(jnp.einsum('btc,ec->bte', gate_in, Wg) + bg)
        gated = x * wg
        h1 = jax.nn.gelu(jnp.einsum('btc,hc->bth', x, Wn1) + bn1, approximate=False)
        mod = 0.5 + jax.nn.sigmoid(jnp.einsum('bth,dh->btd', h1, Wn2) + bn2)
        traces = jax.vmap(lambda tau, m: causal_ema(gated * m[..., None], tau))(tau_raws, jnp.moveaxis(mod, -1, 0))
        blend_w = jax.nn.softmax(blend, axis=0)
        temporal = jnp.einsum('dbtc,dc->btc', traces, blend_w)
        gate = jax.nn.sigmoid(jnp.einsum('btc,ec->bte', temporal, Wtemp) + btemp)
        soma = jax.nn.gelu(jnp.einsum('btc,ec->bte', x, Wsoma) + bsoma, approximate=False)
        out = jnp.einsum('btc,ec->bte', soma * gate, Wout)
        mu = out.mean(-1, keepdims=True)
        var = out.var(-1, keepdims=True)
        return (out - mu) / jnp.sqrt(var + 1e-05) * gamma + beta

    def _L2_ffn_ref(x, U1, V1, b1, U2, V2, b2):
        import jax, jax.numpy as jnp
        import numpy as np
        D_MODEL, D_FF, RANK = (128, 512, 32)
        B, S = (4, 512)
        P = jnp.einsum('bsd,dr->bsr', x, U1)
        H = jax.nn.gelu(jnp.einsum('bsr,rf->bsf', P, V1) + b1)
        Q = jnp.einsum('bsf,fr->bsr', H, U2)
        return jnp.einsum('bsr,rd->bsd', Q, V2) + b2

    def _L3_cond_ref(x, subject_id, weight, bias):
        import jax, jax.numpy as jnp
        import numpy as np
        S, O, H = (8, 128, 128)
        B, N = (32, 64)
        W = weight[subject_id]
        b = bias[subject_id]
        y = jnp.einsum('bnh,boh->bno', x, W) + b[:, None, :]
        return y

    def _L3_ffn_ref(x, router_w, gate_w, gate_b, up_w, up_b, down_w, down_b):
        import jax, jax.numpy as jnp
        import numpy as np
        D_MODEL, D_FF, N_EXPERTS, TOP_K = (128, 256, 8, 2)
        B, S = (2, 256)
        b, s, d = x.shape
        xf = x.reshape(b * s, d)
        n = xf.shape[0]
        router_logits = xf @ router_w.T
        probs = jax.nn.softmax(router_logits, axis=-1)
        topv, topi = jax.lax.top_k(probs, TOP_K)
        mask = jnp.zeros_like(probs).at[jnp.arange(n)[:, None], topi].set(1.0)
        probs = probs * mask
        probs = probs / (probs.sum(axis=-1, keepdims=True) + 1e-09)
        g = jnp.einsum('nd,edf->nef', xf, gate_w) + gate_b
        u = jnp.einsum('nd,edf->nef', xf, up_w) + up_b
        h = jax.nn.silu(g) * u
        expert_out = jnp.einsum('nef,efd->ned', h, down_w) + down_b
        y = jnp.einsum('ne,ned->nd', probs, expert_out)
        return y.reshape(b, s, d)
    x = x + _L0_ffn_ref(_L0_cond_ref(x, itok_B_0_8, L0_cond_W1, L0_cond_b1, L0_cond_W2, L0_cond_b2, L0_cond_gamma, L0_cond_beta), L0_ffn_w_router, L0_ffn_w_fc, L0_ffn_w_gate, L0_ffn_w_proj)
    x = x + _L1_ffn_ref(_L1_cond_ref(x, L1_cond_W1, L1_cond_b1, L1_cond_v, itok_B_0_2), L1_ffn_Wg, L1_ffn_W1, L1_ffn_b1, L1_ffn_W2, L1_ffn_b2)
    x = x + _L2_ffn_ref(_L2_cond_ref(x, L2_cond_tau_ctx, condB_tauraws, L2_cond_Wg, L2_cond_bg, L2_cond_Wn1, L2_cond_bn1, cond_256, condB_bn2, cond_1024, L2_cond_Wsoma, L2_cond_bsoma, L2_cond_Wtemp, L2_cond_btemp, L2_cond_Wout, L2_cond_gamma, L2_cond_beta), L2_ffn_U1, L2_ffn_V1, L2_ffn_b1, L2_ffn_U2, L2_ffn_V2, L2_ffn_b2)
    x = x + _L3_ffn_ref(_L3_cond_ref(x, itok_B_0_7, L3_cond_weight, L3_cond_bias), L3_ffn_router_w, L3_ffn_gate_w, L3_ffn_gate_b, L3_ffn_up_w, L3_ffn_up_b, L3_ffn_down_w, L3_ffn_down_b)
    return x

_drawn_inputs = setup_inputs


def setup_inputs(seed=0):
    import zlib

    import numpy as np

    out = dict(_drawn_inputs(seed))
    spreads = {'condB_bn2': (0.0, 2.0),
     'L0_cond_b1': (0.0, 0.8),
     'L0_cond_b2': (0.0, 0.8),
     'L0_cond_gamma': (1.0, 0.6),
     'L0_cond_beta': (0.0, 0.8),
     'L1_ffn_b1': (0.0, 0.298),
     'L1_ffn_b2': (0.0, 0.1),
     'L2_cond_bg': (-0.5, 0.6),
     'L2_cond_bn1': (0.0, 0.8),
     'L2_cond_bsoma': (0.0, 0.8),
     'L2_cond_btemp': (0.0, 0.8),
     'L2_cond_gamma': (1.0, 0.6),
     'L2_cond_beta': (0.0, 0.8),
     'L2_ffn_b1': (0.0, 0.8),
     'L2_ffn_b2': (0.0, 0.1),
     'L3_ffn_gate_b': (0.0, 0.338),
     'L3_ffn_up_b': (0.0, 0.35),
     'L3_ffn_down_b': (0.0, 0.8)}
    factors = {'condB_tauraws': 8.0,
     'cond_256': 8.0,
     'cond_1024': 8.0,
     'L0_cond_W1': 8.0,
     'L0_cond_W2': 8.0,
     'L0_ffn_w_router': 8.0,
     'L0_ffn_w_fc': 8.0,
     'L0_ffn_w_gate': 8.0,
     'L0_ffn_w_proj': 8.0,
     'L1_cond_b1': 8.0,
     'L1_ffn_W1': 5.195,
     'L2_cond_Wg': 8.0,
     'L2_cond_Wn1': 8.0,
     'L2_cond_Wsoma': 8.0,
     'L2_cond_Wtemp': 8.0,
     'L2_cond_Wout': 8.0,
     'L2_ffn_U1': 8.0,
     'L2_ffn_V1': 8.0,
     'L2_ffn_U2': 8.0,
     'L2_ffn_V2': 8.0}
    for name, (base, spread) in spreads.items():
        noise = np.random.default_rng([zlib.crc32(name.encode()), seed]).standard_normal(out[name].shape)
        drawn = base * np.exp(spread * noise) if base else spread * noise
        out[name] = jnp.asarray(drawn.astype(out[name].dtype))
    for name, factor in factors.items():
        out[name] = (out[name] * factor).astype(out[name].dtype)
    return out
```

```python
from contextlib import ExitStack

import concourse.bass as bass
from concourse import mybir

F32 = mybir.dt.float32
BF16 = mybir.dt.bfloat16
I32 = mybir.dt.int32
ALU = mybir.AluOpType
ACT = mybir.ActivationFunctionType
X_AXIS = mybir.AxisListType.X

P = 128
B, S, C = 32, 32, 128
N = B * S
TILES = N // P
BPT = P // S
HALF = 512
HALVES = N // HALF
LANGS, ADIM = 10, 32
LCH = (P, P, 64)
E0, H0, CAP = 16, 64, 4
SLOTS = E0 * CAP
E1, FF1 = 8, 512
FCH1 = FF1 // P
TOP1 = N * 2 // E1
RANK_PARTS = P // E1
BOUND = 128.0
ROUNDS = 8
D2 = 32
HN2 = 32
FF2, RK2 = 512, 32
FCH2 = FF2 // P
SUBJ = 8
E3, FF3 = 8, 256
FCH3 = FF3 // P
NEG = -1.0e30
FAR = -(2.0 ** 100)
EPS = 1e-5

PACKS = {
    "consts": [("ident", P), ("eye32", 32), ("tri_batch", P), ("ones_batch", P), ("tri_all", P),
               ("same_expert", P), ("far", LANGS * ADIM), ("pidx", 1), ("mask_pre", 32), ("mask_post", 32),
               ("mask_cloze", 32), ("counts", 3), ("iota16", E0), ("iota8", E3), ("eps", 1),
               ("steps", ROUNDS), ("eye8", 8)],
    "l0_small": [("w1", LANGS * ADIM), ("b1", 3), ("table", 3 * C), ("w2", 3 * C), ("router", E0)],
    "l0_gatefc": [("gatefc", E0 * 2 * H0)],
    "l0_proj": [("proj", E0 * C)],
    "l1_small": [("w1c", ADIM), ("b1c", 1), ("v", 1), ("router", P), ("b1", E1 * FCH1), ("b2", C)],
    "l1_w1": [("w1", E1 * FF1)],
    "l1_w2": [("w2", E1 * FCH1 * C)],
    "l2_decay": [("blend", D2), ("taus", 1), ("tau_ctx", 1)],
    "l2_all": [("wg_x", C), ("wg_ctx", C), ("bg", 1), ("wn1", HN2), ("bn1", 1), ("wn2", D2), ("bn2", 1),
               ("wtemp", C), ("btemp", 1), ("wsoma", C),
               ("bsoma", 1), ("wout", C), ("gamma", 1), ("beta", 1), ("u1", RK2), ("v1", FF2),
               ("b1", FCH2), ("u2", FCH2 * RK2), ("v2", C), ("b2", 1)],
    "l3_small": [("cbias", C), ("router", E3), ("gate_b", E3 * FCH3), ("up_b", E3 * FCH3), ("down_b", C)],
    "l3_gate": [("gate", E3 * FF3)],
    "l3_up": [("up", E3 * FF3)],
    "l3_down": [("down", E3 * FCH3 * C)],
}
WIDTH = {pack: sum(w for _, w in fields) for pack, fields in PACKS.items()}


def bc(ap, axis, n):
    shape = list(ap.shape)
    shape.insert(axis, n)
    return ap.unsqueeze(axis).to_broadcast(shape)


def program(nc, dram, out):
    ctx = ExitStack()
    with ctx:
        def sb(name, shape, dt=F32):
            return ctx.enter_context(nc.sbuf_tensor(name, shape, dt))

        def sem(name):
            return ctx.enter_context(nc.semaphore(name))

        psum = ctx.enter_context(nc.psum_tensor("psum", [P, 8, HALF], F32))

        shares = {"l3_gate": "l0_gatefc", "l3_up": "l0_proj"}
        packs = {name: sb("sb_" + name, [P, w]) for name, w in WIDTH.items() if name not in shares}
        packs.update({name: packs[old] for name, old in shares.items()})

        def field(pack, name):
            at = 0
            for f, w in PACKS[pack]:
                if f == name:
                    return packs[pack][:, at:at + w]
                at += w
            raise KeyError(name)

        ident, eye32, pidx = field("consts", "ident"), field("consts", "eye32"), field("consts", "pidx")
        x_tok = sb("x_tok", [P, TILES, C])
        x_ch = sb("x_ch", [P, N])
        ids_i = sb("ids_i", [P, 3 * B], I32)
        types_i = sb("types_i", [P, TILES], I32)
        subj_w = packs["l1_w1"][:, 0:B * C].rearrange("p (b c) -> p b c", c=C)

        loaded = {name: sem("loaded_" + name) for name in list(WIDTH) + ["ids", "x_ch", "x_tok"]}
        subj_loaded = sem("subj_loaded")

        far_h = sb("far_h", [LANGS, LANGS * ADIM], BF16)
        tri_batch_h = sb("tri_batch_h", [P, P], BF16)
        ones_batch_h = sb("ones_batch_h", [P, P], BF16)
        tri_all_h = sb("tri_all_h", [P, P], BF16)
        same_expert_h = sb("same_expert_h", [P, P], BF16)
        ones_h = sb("ones_h", [P, P], BF16)
        ones_f = sb("ones_f", [P, P])
        ids_f = sb("ids_f", [P, 3 * B])
        types_f = sb("types_f", [P, TILES])
        lang_b = sb("lang_b", [LANGS, B])
        lang_h = sb("lang_h", [LANGS, N], BF16)
        lang_f_rows = sb("lang_f_rows", [P, N])
        lang_f = lang_f_rows[0:LANGS, :]
        subj_b = sb("subj_b", [SUBJ, B])
        type_sel = sb("type_sel", [P, 3, TILES])
        mask_add = sb("mask_add", [P, TILES, S])
        mask_tmp = sb("mask_tmp", [P, TILES, S])
        seen = sb("seen", [P, TILES])
        seen_tmp = sb("seen_tmp", [P, TILES])
        pool_step = sem("pool_step")
        consts_ready = sem("consts_ready")

        big = sb("big", [P, 8 * N])
        quarter = [big[:, 2 * N * k:2 * N * (k + 1)] for k in range(4)]
        three = sb("three", [P, 3 * N])
        ad_hid = three[:, :].rearrange("p (k n) -> p k n", k=3)
        res0 = sb("res0", [P, TILES, C])
        bn_s = sb("bn_s", [P, TILES, 6])
        bn_m = sb("bn_m", [P, TILES, 2])
        std = sb("std", [P, TILES])
        rstd = sb("rstd", [P, TILES])
        c0 = sb("c0", [P, TILES, C])
        c0_ch = sb("c0_ch", [P, N])
        lg = sb("lg", [P, TILES, E0])
        eqm = sb("eqm", [P, TILES, E0])
        pick = sb("pick", [P, TILES])
        top1 = sb("top1", [P, TILES])
        top2 = sb("top2", [P, TILES])
        oh1 = sb("oh1", [P, TILES, E0])
        oh2 = sb("oh2", [P, TILES, E0])
        oh1_h = sb("oh1_h", [P, TILES * E0], BF16)
        oh2_h = sb("oh2_h", [P, TILES * E0], BF16)
        rest = sb("rest", [P, TILES, E0])
        ex = sb("ex", [P, TILES, E0])
        exsum = sb("exsum", [P, TILES])
        rsum = sb("rsum", [P, TILES])
        prob = sb("prob", [P, TILES, E0])
        posa = sb("posa", [P, TILES, E0])
        posb = sb("posb", [P, TILES, E0])
        disp = sb("disp", [P, TILES, E0, CAP])
        comb = sb("comb", [P, TILES, 2, E0, CAP])
        comb_t = sb("comb_t", [P, TILES, P])
        slot_in = quarter[0].rearrange("p (e t i c) -> p e t i c", e=E0, t=TILES, i=BPT)
        silu0 = quarter[1][0:H0, :]
        hid0 = quarter[2][0:H0, :]
        slot_ch = quarter[3].rearrange("p (t i e c) -> p t i e c", t=TILES, i=BPT, e=E0)
        slot_out = sb("slot_out", [P, B // 2, C])

        ad_ready = sem("ad_ready")
        adhid_ready = sem("adhid_ready")
        adapt_ready = sem("adapt_ready")
        affine_ready = sem("affine_ready")
        var_ready = sem("var_ready")
        std_ready = sem("std_ready")
        c0_ready = sem("c0_ready")
        c0t_ready = sem("c0t_ready")
        c0ch_ready = sem("c0ch_ready")
        lg_ready = sem("lg_ready")
        choice_ready = sem("choice_ready")
        rank_ready = sem("rank_ready")
        rest_ready = sem("rest_ready")
        exp_ready = sem("exp_ready")
        disp_ready = sem("disp_ready")
        comb_ready = sem("comb_ready")
        gather_ready = sem("gather_ready")
        slotin_act = sem("slotin_act")
        slotin_dve = sem("slotin_dve")
        combt_ready = sem("combt_ready")
        combt_used = sem("combt_used")
        gatefc_ready = sem("gatefc_ready")
        silu_ready = sem("silu_ready")
        hid0_ready = sem("hid0_ready")
        proj_ready = sem("proj_ready")
        slotch_act = sem("slotch_act")
        slotch_dve = sem("slotch_dve")
        slott_ready = sem("slott_ready")
        slotout_act = sem("slotout_act")
        slotout_dve = sem("slotout_dve")
        y0_ready = sem("y0_ready")
        x1_ready = sem("x1_ready")

        attn = c0_ch[0:ADIM, :]
        score_d = sb("score_d", [P, TILES, S])
        soft = sb("soft", [P, TILES, S])
        soft_e = sb("soft_e", [P, TILES, S])
        soft_t = sb("soft_t", [P, TILES, S])
        rmax = sb("rmax", [P, TILES])
        rden = sb("rden", [P, TILES])
        pool_ch = sb("pool_ch", [P, N])

        x1t_ready = sem("x1t_ready")
        x1tok_ready = sem("x1tok_ready")
        attn_ready = sem("attn_ready")
        attn_done = sem("attn_done")
        score_ready = sem("score_ready")
        scored_ready = sem("scored_ready")
        spread_ready = sem("spread_ready")
        soft_ready = sem("soft_ready")
        softexp_ready = sem("softexp_ready")
        softt_ready = sem("softt_ready")
        pooled_ready = sem("pooled_ready")
        poolch_act = sem("poolch_act")
        poolch_dve = sem("poolch_dve")

        lrow = slot_out[:, 0:TILES, :].rearrange("p q c -> p (q c)")
        above_row = slot_out[:, TILES:2 * TILES, :].rearrange("p q c -> p (q c)")
        thr = sb("thr", [P, 1])
        best_thr = sb("best_thr", [P, 1])
        best_end = sb("best_end", [P, 1])
        hits = sb("hits", [P, 1])
        enough_h = sb("enough_h", [P, 1], BF16)
        thr_d = sb("thr_d", [E1, 2, E1])
        ltok = sb("ltok", [P, TILES, E1])
        sure = sb("sure", [P, TILES, E1])
        sure_h = sb("sure_h", [P, TILES, E1], BF16)
        tied = sb("tied", [P, TILES, E1])
        tied_h = sb("tied_h", [P, TILES * E1], BF16)
        room = sb("room", [P, E1])
        gate1 = sb("gate1", [P, TILES, E1])
        sig1 = sb("sig1", [P, TILES, E1])
        gate1_t = sb("gate1_t", [E1, N])
        hid = big[:, :].rearrange("p (a k n) -> p a k n", a=2, k=FCH1)

        lrow_ready = sem("lrow_ready")
        lrow_done = sem("lrow_done")
        ltok_ready = sem("ltok_ready")
        ltok_done = sem("ltok_done")
        enough_ready = sem("enough_ready")
        count_ready = sem("count_ready")
        thrd_ready = sem("thrd_ready")
        thrtok_ready = sem("thrtok_ready")
        tied_ready = sem("tied_ready")
        order_ready = sem("order_ready")
        sig1_ready = sem("sig1_ready")
        gate1_ready = sem("gate1_ready")
        gate1t_ready = sem("gate1t_ready")
        gate1t_done = sem("gate1t_done")
        up1_ready = sem("up1_ready")
        hid1_ready = sem("hid1_ready")
        y1_ready = sem("y1_ready")
        y1_used = sem("y1_used")

        decay = sb("decay", [P, N])
        tau_e = sb("tau_e", [P, 2])
        alpha = sb("alpha", [P, 2])
        bl_max = sb("bl_max", [P, 1])
        bl = sb("bl", [P, D2])
        bl_e = sb("bl_e", [P, D2])
        bl_sum = sb("bl_sum", [P, 1])
        lag_w = sb("lag_w", [D2, S, C])
        ctx_ch = comb_t[:, :, :].rearrange("p t q -> p (t q)")
        soma = slot_out[:, 0:TILES, :].rearrange("p q c -> p (q c)")
        gated = slot_out[:, TILES:2 * TILES, :].rearrange("p q c -> p (q c)")
        net = lang_f_rows[0:HN2, :]
        mod = attn[0:D2, :]
        prod = three[:, :].rearrange("p (k n) -> p k n", k=3)
        temporal = pool_ch
        tgate = res0[:, :, :].rearrange("p t c -> p (t c)")
        ynorm = c0
        y_ch = c0_ch
        low = lrow[0:RK2, :]
        low2 = lang_f_rows[0:RK2, :]

        taue_ready = sem("taue_ready")
        blend_ready = sem("blend_ready")
        blexp_ready = sem("blexp_ready")
        blw_ready = sem("blw_ready")
        blt_ready = sem("blt_ready")
        lag0_ready = sem("lag0_ready")
        alpha_ready = sem("alpha_ready")
        lagw_ready = sem("lagw_ready")
        decay_ready = sem("decay_ready")
        x2t_ready = sem("x2t_ready")
        x2ch_ready = sem("x2ch_ready")
        ctx_ready = sem("ctx_ready")
        soma_pre = sem("soma_pre")
        soma_ready = sem("soma_ready")
        net_pre = sem("net_pre")
        net_ready = sem("net_ready")
        wg_pre = sem("wg_pre")
        wg_ready = sem("wg_ready")
        mod_pre = sem("mod_pre")
        mod_sig = sem("mod_sig")
        mod_ready = sem("mod_ready")
        lag_ready = sem("lag_ready")
        prod_ready = sem("prod_ready")
        summed = sem("summed")
        tg_pre = sem("tg_pre")
        tg_ready = sem("tg_ready")
        sg_ready = sem("sg_ready")
        out2_ready = sem("out2_ready")
        ynorm_ready = sem("ynorm_ready")
        yt_ready = sem("yt_ready")
        ych_ready = sem("ych_ready")
        low_pre = sem("low_pre")
        low_ready = sem("low_ready")
        ff2_pre = sem("ff2_pre")
        ff2_ready = sem("ff2_ready")
        low2_pre = sem("low2_pre")
        low2_ready = sem("low2_ready")
        y2_ready = sem("y2_ready")
        x3_ready = sem("x3_ready")

        subj_bias = sb("subj_bias", [P, B])
        z_ch = decay
        gate3 = sb("gate3", [P, TILES, E3])
        gate3_t = gate1_t
        silu3 = three[:, 0:2 * HALF].rearrange("p (k n) -> p k n", k=2)

        z_ready = sem("z_ready")
        zch_ready = sem("zch_ready")
        x3t_ready = sem("x3t_ready")
        x3tok_ready = sem("x3tok_ready")
        lg3_ready = sem("lg3_ready")
        rest3_ready = sem("rest3_ready")
        exp3_ready = sem("exp3_ready")
        gate3_ready = sem("gate3_ready")
        gate3t_ready = sem("gate3t_ready")
        gate3t_done = sem("gate3t_done")
        g3_ready = sem("g3_ready")
        silu3_ready = sem("silu3_ready")
        u3_ready = sem("u3_ready")
        hid3_ready = sem("hid3_ready")
        y3_ready = sem("y3_ready")
        y3_used = sem("y3_used")

        dve_step = sem("dve_step")
        act_step = sem("act_step")
        stored = sem("stored")

        block = ctx.enter_context(nc.Block())

        @block.sync
        def _(sp):
            sp.dma_start(packs["consts"][:, :], dram["consts"]).then_inc(loaded["consts"], 16)
            sp.dma_start(ids_i[:, :], dram["ids"]).then_inc(loaded["ids"], 16)
            sp.dma_start(types_i[:, :], dram["types"]).then_inc(loaded["ids"], 16)
            sp.dma_start(packs["l0_small"][:, :], dram["l0_small"]).then_inc(loaded["l0_small"], 16)
            sp.dma_start(x_ch[:, :], dram["x_ch"]).then_inc(loaded["x_ch"], 16)
            sp.dma_start(x_tok[:, :, :], dram["x"].rearrange("(t p) c -> p t c", p=P)).then_inc(loaded["x_tok"], 16)
            for name in ("l2_decay", "l0_gatefc", "l0_proj", "l1_small"):
                sp.dma_start(packs[name][:, :], dram[name]).then_inc(loaded[name], 16)
            for name in ("l1_w1", "l1_w2", "l2_all", "l3_small", "l3_down", "l3_gate", "l3_up"):
                if name == "l3_gate":
                    sp.wait_ge(proj_ready, 4)
                sp.dma_start(packs[name][:, :], dram[name]).then_inc(loaded[name], 16)
            sp.wait_ge(loaded["ids"], 32)
            sp.wait_ge(up1_ready, E1 * FCH1 * HALVES)
            for b in range(B):
                subject = sp.value_load(ids_i[0:1, 2 * B + b:2 * B + b + 1], min_val=0, max_val=SUBJ - 1)
                sp.dma_start(subj_w[:, b, :], dram["subj_w"][bass.ds(subject, 1), :, :].rearrange("a h o -> (a h) o")
                             ).then_inc(subj_loaded, 16)
            out_v = out.rearrange("b s c -> (b s) c").rearrange("(t p) c -> p t c", p=P)
            for h in range(HALVES):
                sp.wait_ge(y3_used, 2 * E3 + h + 1)
                sp.dma_start(out_v[:, 4 * h:4 * h + 4, :], x_tok[:, 4 * h:4 * h + 4, :]).then_inc(stored, 16)
            sp.wait_ge(stored, 32)

        @block.gpsimd
        def _(pool):
            steps = [0]

            def chain(ins):
                steps[0] += 1
                ins.then_inc(pool_step, 1)
                pool.wait_ge(pool_step, steps[0])

            pool.wait_ge(loaded["consts"], 16)
            pool.wait_ge(loaded["ids"], 32)
            nc.gpsimd.memset(ones_h[:, :], 1.0)
            nc.gpsimd.memset(ones_f[:, :], 1.0)
            chain(nc.gpsimd.tensor_copy(ids_f[:, :], ids_i[:, :]))
            nc.gpsimd.tensor_copy(far_h[:, :], field("consts", "far")[0:LANGS, :])
            chain(nc.gpsimd.tensor_scalar(lang_b[:, :], ids_f[0:LANGS, 0:B], pidx[0:LANGS, :], None, ALU.is_equal))
            lang_rows = bc(lang_b[:, :], 2, S)
            chain(nc.gpsimd.tensor_copy(lang_h[:, :].rearrange("l (b s) -> l b s", s=S), lang_rows))
            nc.gpsimd.tensor_copy(lang_f[:, :].rearrange("l (b s) -> l b s", s=S), lang_rows).then_inc(consts_ready, 1)
            for dst, name in ((tri_batch_h, "tri_batch"), (ones_batch_h, "ones_batch"), (tri_all_h, "tri_all"),
                              (same_expert_h, "same_expert")):
                nc.gpsimd.tensor_copy(dst[:, :], field("consts", name))
            nc.gpsimd.tensor_scalar(subj_b[:, :], ids_f[0:SUBJ, 2 * B:3 * B], pidx[0:SUBJ, :], None, ALU.is_equal)
            chain(nc.gpsimd.tensor_copy(types_f[:, :], types_i[:, :]))
            chain(nc.gpsimd.tensor_scalar(type_sel[:, 0, :], types_f[:, :], 0.0, None, ALU.is_equal))
            chain(nc.gpsimd.tensor_scalar(type_sel[:, 1, :], types_f[:, :], 1.0, None, ALU.is_equal))
            chain(nc.gpsimd.tensor_tensor(type_sel[:, 2, :], type_sel[:, 0, :], type_sel[:, 1, :], ALU.add))
            chain(nc.gpsimd.tensor_scalar(type_sel[:, 2, :], type_sel[:, 2, :], -1.0, 1.0, ALU.mult, ALU.add))
            for k, name in enumerate(("mask_pre", "mask_post", "mask_cloze")):
                sel = bc(type_sel[:, k, :], 2, S)
                mask = bc(field("consts", name), 1, TILES)
                count = field("consts", "counts")[:, k:k + 1]
                if k == 0:
                    nc.gpsimd.tensor_tensor(mask_add[:, :, :], mask, sel, ALU.mult)
                    chain(nc.gpsimd.tensor_scalar(seen[:, :], type_sel[:, k, :], count, None, ALU.mult))
                    continue
                nc.gpsimd.tensor_tensor(mask_tmp[:, :, :], mask, sel, ALU.mult)
                chain(nc.gpsimd.tensor_scalar(seen_tmp[:, :], type_sel[:, k, :], count, None, ALU.mult))
                nc.gpsimd.tensor_tensor(mask_add[:, :, :], mask_add[:, :, :], mask_tmp[:, :, :], ALU.add)
                chain(nc.gpsimd.tensor_tensor(seen[:, :], seen[:, :], seen_tmp[:, :], ALU.add))
            nc.gpsimd.memset(mask_tmp[:, :, :], 0.0).then_inc(consts_ready, 1)
            chain(nc.gpsimd.memset(decay[:, :], 1.0))
            chain(nc.gpsimd.memset(decay[:, :].rearrange("p (b s) -> p b s", s=S)[:, :, 0:1], 0.0))
            pool.wait_ge(alpha_ready, 1)
            nc.gpsimd.tensor_scalar(decay[:, :], decay[:, :], alpha[:, 1:2], None, ALU.mult).then_inc(decay_ready, 1)
            pool.wait_ge(lag0_ready, 1)
            for lag in range(1, S):
                nc.gpsimd.tensor_scalar(lag_w[:, lag, :], lag_w[:, lag - 1, :], alpha[0:D2, 0:1], None, ALU.mult
                                        ).then_inc(lagw_ready, 1)
                pool.wait_ge(lagw_ready, lag)
            traces = temporal[:, :].rearrange("p (b s) -> p b s", s=S)
            for lag in range(1, S):
                n = S - lag
                part = prod[:, lag % 3, 0:B * n].rearrange("p (b s) -> p b s", s=n)
                pool.wait_ge(prod_ready, lag + 1)
                if lag > 1:
                    pool.wait_ge(summed, lag - 1)
                nc.gpsimd.tensor_tensor(traces[:, :, lag:S], traces[:, :, lag:S], part, ALU.add).then_inc(summed, 1)

        @block.tensor
        def _(pe):
            mm, tr = nc.tensor.matmul, nc.tensor.transpose

            pe.wait_ge(loaded["l0_small"], 16)
            pe.wait_ge(loaded["x_ch"], 16)
            pe.wait_ge(consts_ready, 1)
            w1, w2 = field("l0_small", "w1"), field("l0_small", "w2")
            table = field("l0_small", "table")
            for h in range(HALVES):
                cols = slice(h * HALF, (h + 1) * HALF)
                for k, rows in enumerate(LCH):
                    dst = psum[0:rows, 3 * h + k, :]
                    mm(dst, w1[:, k * P:k * P + rows], x_ch[:, cols], start=True, stop=False)
                    mm(dst, far_h[:, k * P:k * P + rows], lang_h[:, cols], start=False, stop=True).then_inc(ad_ready, 1)
            for h in range(HALVES):
                pe.wait_ge(adhid_ready, 3 * (h + 1))
                for t in range(4 * h, 4 * h + 4):
                    dst = psum[:, 6 + h, (t % 4) * C:(t % 4 + 1) * C]
                    tok = slice(t * P, (t + 1) * P)
                    for k, rows in enumerate(LCH):
                        mm(dst, ad_hid[0:rows, k, tok], w2[0:rows, k * C:(k + 1) * C], start=(k == 0), stop=False)
                    last = mm(dst, lang_f[:, tok], table[0:LANGS, 0:C], start=False, stop=True)
                last.then_inc(adapt_ready, 1)
            for t in range(TILES):
                last = mm(psum[:, t // 2, (t % 2) * 2 * C:(t % 2 + 1) * 2 * C], lang_f[:, t * P:(t + 1) * P],
                          table[0:LANGS, C:3 * C], start=True, stop=True)
            last.then_inc(affine_ready, 1)
            for h in range(HALVES):
                pe.wait_ge(c0_ready, h + 1)
                for t in range(4 * h, 4 * h + 4):
                    last = tr(psum[:, 4 + h, (t % 4) * P:(t % 4 + 1) * P], c0[:, t, :], ident)
                last.then_inc(c0t_ready, 1)
            for t in range(TILES):
                if t % 4 == 0:
                    pe.wait_ge(c0ch_ready, t // 4 + 1)
                last = mm(psum[:, 6, t * E0:(t + 1) * E0], c0_ch[:, t * P:(t + 1) * P], field("l0_small", "router"),
                          start=True, stop=True)
            last.then_inc(lg_ready, 1)
            pe.wait_ge(consts_ready, 2)
            pe.wait_ge(choice_ready, 2)
            mm(psum[:, 7, 0:P], tri_batch_h[:, :], oh1_h[:, :], start=True, stop=True)
            mm(psum[:, 7, P:2 * P], ones_batch_h[:, :], oh1_h[:, :], start=True, stop=False)
            mm(psum[:, 7, P:2 * P], tri_batch_h[:, :], oh2_h[:, :], start=False, stop=True).then_inc(rank_ready, 1)
            pe.wait_ge(disp_ready, 1)
            for t in range(TILES):
                for i in range(BPT):
                    rows = slice(i * S, (i + 1) * S)
                    last = mm(psum[:, i, t * SLOTS:(t + 1) * SLOTS], c0[rows, t, :],
                              disp[rows, t, :, :].rearrange("p e c -> p (e c)"), start=True, stop=True,
                              tile_position=(i * S, 0))
            last.then_inc(gather_ready, 1)
            pe.wait_ge(comb_ready, 1)
            for t in range(TILES):
                last = tr(psum[:, 4 + t // 4, (t % 4) * P:(t % 4 + 1) * P],
                          comb[:, t, :, :, :].rearrange("p a e c -> p (a e c)"), ident)
                if t % 4 == 3:
                    last.then_inc(combt_ready, 1)
            pe.wait_ge(loaded["l0_gatefc"], 16)
            pe.wait_ge(slotin_act, 2)
            pe.wait_ge(slotin_dve, 2)
            for e in range(E0):
                bank = (6, 7, 4, 5)[e // 4]
                if e == 8:
                    pe.wait_ge(combt_used, 2)
                last = mm(psum[:, bank, (e % 4) * P:(e % 4 + 1) * P],
                          field("l0_gatefc", "gatefc")[:, e * P:(e + 1) * P],
                          slot_in[:, e, :, :, :].rearrange("p t i c -> p (t i c)"), start=True, stop=True)
                if e % 4 == 3:
                    last.then_inc(gatefc_ready, 1)
            pe.wait_ge(loaded["l0_proj"], 16)
            for e in range(E0):
                if e % 4 == 0:
                    pe.wait_ge(hid0_ready, e // 4 + 1)
                last = mm(psum[:, e // 4, (e % 4) * P:(e % 4 + 1) * P],
                          field("l0_proj", "proj")[0:H0, e * C:(e + 1) * C], hid0[:, e * P:(e + 1) * P],
                          start=True, stop=True)
                if e % 4 == 3:
                    last.then_inc(proj_ready, 1)
            pe.wait_ge(slotch_act, 2)
            pe.wait_ge(slotch_dve, 2)
            pairs = slot_ch[:, :, :, :, :].rearrange("p t (j a) e c -> p (t j) (a e c)", a=2)
            for q in range(B // 2):
                last = tr(psum[:, 4 + q // 4, (q % 4) * P:(q % 4 + 1) * P], pairs[:, q, :], ident)
                if q % 4 == 3:
                    last.then_inc(slott_ready, 1)
            pe.wait_ge(slotout_act, 2)
            pe.wait_ge(slotout_dve, 2)
            for b in range(B):
                rows = slice((b % 2) * SLOTS, (b % 2 + 1) * SLOTS)
                last = mm(psum[:, b % 2, (b // 2) * S:(b // 2 + 1) * S], slot_out[rows, b // 2, :],
                          comb_t[rows, b // BPT, (b % BPT) * S:(b % BPT + 1) * S], start=True, stop=True,
                          tile_position=((b % 2) * SLOTS, 0))
            last.then_inc(y0_ready, 1)

            pe.wait_ge(blw_ready, 1)
            tr(psum[0:D2, 7, 0:C], bl[:, :], ident).then_inc(blt_ready, 1)

            pe.wait_ge(x1_ready, 1)
            for t in range(TILES):
                last = tr(psum[:, 2 + t // 4, (t % 4) * C:(t % 4 + 1) * C], x_ch[:, t * P:(t + 1) * P], ident)
                if t % 4 == 3:
                    last.then_inc(x1t_ready, 1)
            pe.wait_ge(loaded["l1_small"], 16)
            for h in range(HALVES):
                mm(psum[0:ADIM, 4 + h, :], field("l1_small", "w1c"), x_ch[:, h * HALF:(h + 1) * HALF],
                   start=True, stop=True).then_inc(attn_ready, 1)
            for t in range(TILES):
                if t % 4 == 0:
                    pe.wait_ge(attn_done, t // 4 + 1)
                last = mm(psum[:, 6, t:t + 1], attn[:, t * P:(t + 1) * P], field("l1_small", "v")[0:ADIM, :],
                          start=True, stop=True)
            last.then_inc(score_ready, 1)
            pe.wait_ge(scored_ready, 1)
            pe.wait_ge(lag0_ready, 1)
            mm(psum[:, 7, 0:TILES * S], field("consts", "ones_batch"), score_d[:, :, :].rearrange("p t s -> p (t s)"),
               start=True, stop=True).then_inc(spread_ready, 1)
            pe.wait_ge(softt_ready, 1)
            pe.wait_ge(x1tok_ready, 2)
            for t in range(TILES):
                for i in range(BPT):
                    rows = slice(i * S, (i + 1) * S)
                    last = mm(psum[:, i, t * S:(t + 1) * S], x_tok[rows, t, :], soft_t[rows, t, :],
                              start=True, stop=True, tile_position=(i * S, 0))
            last.then_inc(pooled_ready, 1)

            pe.wait_ge(poolch_act, 2)
            pe.wait_ge(poolch_dve, 2)
            for h in range(HALVES):
                mm(psum[:, 4 + h, :], field("l1_small", "router"), pool_ch[:, h * HALF:(h + 1) * HALF],
                   start=True, stop=True).then_inc(lrow_ready, 1)

            units = [(e, k, h) for e in range(E1) for k in range(FCH1) for h in range(HALVES)]
            UNITS = FCH1 * HALVES

            def up1(u):
                e, k, h = units[u]
                if u >= 3:
                    pe.wait_ge(hid1_ready, u - 2)
                at = (e * FCH1 + k) * P
                mm(psum[:, u % 3, :], field("l1_w1", "w1")[:, at:at + P], pool_ch[:, h * HALF:(h + 1) * HALF],
                   start=True, stop=True).then_inc(up1_ready, 1)

            def down1(e, h):
                pe.wait_ge(hid1_ready, (e + 1) * UNITS - 1 + h)
                if e >= 1:
                    pe.wait_ge(y1_used, 2 * (e - 1) + h + 1)
                for t in range(4 * h, 4 * h + 4):
                    for k in range(FCH1):
                        at = (e * FCH1 + k) * C
                        last = mm(psum[:, 3 + h, (t % 4) * C:(t % 4 + 1) * C], hid[:, e % 2, k, t * P:(t + 1) * P],
                                  field("l1_w2", "w2")[:, at:at + C], start=(k == 0), stop=(k == FCH1 - 1))
                last.then_inc(y1_ready, 1)

            pe.wait_ge(loaded["l1_w1"], 16)
            up1(0)
            pe.wait_ge(lrow_done, 2)
            for t in range(TILES):
                last = tr(psum[:, 6, t * E1:(t + 1) * E1], lrow[0:E1, t * P:(t + 1) * P], ident[0:E1, 0:E1])
            last.then_inc(ltok_ready, 1)
            up1(1)
            pe.wait_ge(ltok_done, 1)
            for r in range(ROUNDS):
                pe.wait_ge(enough_ready, r + 1)
                mm(psum[:, 6, 0:1], same_expert_h[:, :], enough_h[:, :], start=True, stop=True).then_inc(count_ready, 1)
                up1(2 * r + 2 if r < 7 else 15)
                if r < 6:
                    up1(2 * r + 3)
            pe.wait_ge(loaded["l1_w2"], 16)
            pe.wait_ge(thrd_ready, 1)
            mm(psum[:, 6, 0:2 * E1], ones_f[0:E1, :], thr_d[:, :, :].rearrange("p a e -> p (a e)"), start=True,
               stop=True).then_inc(thrtok_ready, 1)
            down1(0, 0)
            pe.wait_ge(tied_ready, 1)
            mm(psum[:, 7, 0:TILES * E1], tri_all_h[:, :], tied_h[:, :], start=True, stop=False)
            for t in range(TILES - 1):
                left = TILES - 1 - t
                mm(psum[:, 7, (t + 1) * E1:TILES * E1].rearrange("p (a e) -> p a e", e=E1), ones_h[:, :],
                   bc(tied_h[:, t * E1:(t + 1) * E1], 1, left), start=False, stop=(t == TILES - 2))
            for t in range(TILES):
                last = mm(psum[:, 7, HALF - E1:HALF], ones_h[:, :], sure_h[:, t, :], start=(t == 0),
                          stop=(t == TILES - 1))
            last.then_inc(order_ready, 1)
            down1(0, 1)
            for e in range(1, E1):
                if e >= 2:
                    for u in range(e * UNITS, (e + 1) * UNITS):
                        up1(u)
                if e == 2:
                    pe.wait_ge(gate1_ready, 1)
                    for t in range(TILES):
                        last = tr(psum[0:E1, (5, 7)[t // 4], (t % 4) * P:(t % 4 + 1) * P], gate1[:, t, :], ident)
                        if t % 4 == 3:
                            last.then_inc(gate1t_ready, 1)
                if e >= 2:
                    down1(e - 1, 0)
                    down1(e - 1, 1)
            down1(E1 - 1, 0)
            down1(E1 - 1, 1)
            pe.wait_ge(gate1t_done, 2)
            for h in range(HALVES):
                pe.wait_ge(y1_used, 2 * (E1 - 1) + h + 1)
                for t in range(4 * h, 4 * h + 4):
                    last = mm(psum[:, 3 + h, (t % 4) * C:(t % 4 + 1) * C], gate1_t[:, t * P:(t + 1) * P],
                              field("l1_small", "b2")[0:E1, :], start=True, stop=True)
                last.then_inc(y1_ready, 1)

            for h in range(HALVES):
                pe.wait_ge(y1_used, 2 * E1 + h + 1)
                for t in range(4 * h, 4 * h + 4):
                    last = tr(psum[:, h, (t % 4) * P:(t % 4 + 1) * P], x_tok[:, t, :], ident)
                last.then_inc(x2t_ready, 1)
            pe.wait_ge(loaded["l2_all"], 16)
            l2 = lambda name: field("l2_all", name)
            halves = [slice(h * HALF, (h + 1) * HALF) for h in range(HALVES)]
            for h, cols in enumerate(halves):
                pe.wait_ge(x2ch_ready, h + 1)
                mm(psum[:, 2 + h, :], l2("wsoma"), x_ch[:, cols], start=True, stop=True).then_inc(soma_pre, 1)
                mm(psum[0:HN2, 4 + h, :], l2("wn1"), x_ch[:, cols], start=True, stop=True).then_inc(net_pre, 1)
            pe.wait_ge(ctx_ready, 1)
            for h, cols in enumerate(halves):
                mm(psum[:, h, :], l2("wg_x"), x_ch[:, cols], start=True, stop=False)
                mm(psum[:, h, :], l2("wg_ctx"), ctx_ch[:, cols], start=False, stop=True).then_inc(wg_pre, 1)
            for h, cols in enumerate(halves):
                pe.wait_ge(net_ready, h + 1)
                mm(psum[0:D2, 6 + h, :], l2("wn2")[0:HN2, :], net[:, cols], start=True, stop=True).then_inc(mod_pre, 1)
            pe.wait_ge(mod_ready, 1)
            pe.wait_ge(wg_ready, 2)
            pe.wait_ge(soma_ready, 2)
            mods = mod[:, :].rearrange("d (b s) -> d b s", s=S)
            for lag in range(S):
                n = S - lag
                if lag >= 1:
                    pe.wait_ge(lagw_ready, lag)
                if lag >= 4:
                    pe.wait_ge(prod_ready, lag - 3)
                for a in range(2):
                    last = mm(psum[:, 2 * (lag % 4) + a, 0:16 * n].rearrange("p (b s) -> p b s", s=n),
                              lag_w[:, lag, :], mods[:, 16 * a:16 * (a + 1), 0:n], start=True, stop=True)
                last.then_inc(lag_ready, 1)
            pe.wait_ge(summed, S - 1)
            pe.wait_ge(prod_ready, S)
            for h, cols in enumerate(halves):
                mm(psum[:, h, :], l2("wtemp"), temporal[:, cols], start=True, stop=True).then_inc(tg_pre, 1)
            for h in range(HALVES):
                pe.wait_ge(sg_ready, h + 1)
                for t in range(4 * h, 4 * h + 4):
                    last = mm(psum[:, 2 + h, (t % 4) * C:(t % 4 + 1) * C], soma[:, t * P:(t + 1) * P], l2("wout"),
                              start=True, stop=True)
                last.then_inc(out2_ready, 1)
            for h in range(HALVES):
                pe.wait_ge(ynorm_ready, h + 1)
                for t in range(4 * h, 4 * h + 4):
                    last = tr(psum[:, 4 + h, (t % 4) * P:(t % 4 + 1) * P], ynorm[:, t, :], ident)
                last.then_inc(yt_ready, 1)
            for h, cols in enumerate(halves):
                pe.wait_ge(ych_ready, h + 1)
                mm(psum[0:RK2, 6 + h, :], l2("u1"), y_ch[:, cols], start=True, stop=True).then_inc(low_pre, 1)
            for u in range(HALVES * FCH2):
                h, k = u // FCH2, u % FCH2
                if u % FCH2 == 0:
                    pe.wait_ge(low_ready, h + 1)
                if u >= 4:
                    pe.wait_ge(ff2_ready, u - 3)
                mm(psum[:, u % 4, :], l2("v1")[0:RK2, k * P:(k + 1) * P], low[:, halves[h]], start=True, stop=True
                   ).then_inc(ff2_pre, 1)
            for h, cols in enumerate(halves):
                for k in range(FCH2):
                    pe.wait_ge(ff2_ready, h * FCH2 + k + 1)
                    last = mm(psum[0:RK2, 4 + h, :], l2("u2")[:, k * RK2:(k + 1) * RK2], hid[:, 0, k, cols],
                              start=(k == 0), stop=(k == FCH2 - 1))
                last.then_inc(low2_pre, 1)
            for h, cols in enumerate(halves):
                pe.wait_ge(low2_ready, h + 1)
                mm(psum[:, 6 + h, :], l2("v2")[0:RK2, :], low2[:, cols], start=True, stop=True).then_inc(y2_ready, 1)

            pe.wait_ge(subj_loaded, 16 * B)
            pe.wait_ge(loaded["l3_small"], 16)
            mm(psum[:, 2, 0:B], field("l3_small", "cbias")[0:SUBJ, :], subj_b[:, :], start=True, stop=True)
            for b in range(B):
                if b % 16 == 0:
                    pe.wait_ge(x3_ready, b // 16 + 1)
                last = mm(psum[:, b // 16, (b % 16) * S:(b % 16 + 1) * S], subj_w[:, b, :], x_ch[:, b * S:(b + 1) * S],
                          start=True, stop=True)
                if b % 16 == 15:
                    last.then_inc(z_ready, 1)
            for h in range(HALVES):
                for t in range(4 * h, 4 * h + 4):
                    last = tr(psum[:, 6 + h, (t % 4) * P:(t % 4 + 1) * P], x_ch[:, t * P:(t + 1) * P], ident)
                last.then_inc(x3t_ready, 1)
            for t in range(TILES):
                if t % 4 == 0:
                    pe.wait_ge(zch_ready, t // 4 + 1)
                last = mm(psum[:, 3, t * E3:(t + 1) * E3], z_ch[:, t * P:(t + 1) * P], field("l3_small", "router"),
                          start=True, stop=True)
            last.then_inc(lg3_ready, 1)
            for name in ("l3_gate", "l3_up", "l3_down"):
                pe.wait_ge(loaded[name], 16)

            units3 = [(e, k, h) for e in range(E3) for k in range(FCH3) for h in range(HALVES)]
            UNITS3 = FCH3 * HALVES

            def up3(u):
                e, k, h = units3[u]
                at = (e * FCH3 + k) * P
                if u == 1:
                    pe.wait_ge(gate3_ready, 1)
                if u >= 2:
                    pe.wait_ge(silu3_ready, u - 1)
                mm(psum[:, u % 2, :], field("l3_gate", "gate")[:, at:at + P], z_ch[:, halves[h]], start=True,
                   stop=True).then_inc(g3_ready, 1)
                if u >= 2:
                    pe.wait_ge(hid3_ready, u - 1)
                mm(psum[:, 2 + u % 2, :], field("l3_up", "up")[:, at:at + P], z_ch[:, halves[h]], start=True,
                   stop=True).then_inc(u3_ready, 1)

            def down3(e, h):
                pe.wait_ge(hid3_ready, (e + 1) * UNITS3 - 1 + h)
                if e >= 1:
                    pe.wait_ge(y3_used, 2 * (e - 1) + h + 1)
                for t in range(4 * h, 4 * h + 4):
                    for k in range(FCH3):
                        at = (e * FCH3 + k) * C
                        last = mm(psum[:, 4 + h, (t % 4) * C:(t % 4 + 1) * C], hid[:, 0, (e % 2) * 2 + k, t * P:(t + 1) * P],
                                  field("l3_down", "down")[:, at:at + C], start=(k == 0), stop=(k == FCH3 - 1))
                last.then_inc(y3_ready, 1)

            for e in range(E3):
                for u in range(e * UNITS3, (e + 1) * UNITS3):
                    up3(u)
                if e == 1:
                    for t in range(TILES):
                        last = tr(psum[0:E3, 6 + t // 4, (t % 4) * P:(t % 4 + 1) * P], gate3[:, t, :], ident)
                        if t % 4 == 3:
                            last.then_inc(gate3t_ready, 1)
                if e >= 1:
                    down3(e - 1, 0)
                    down3(e - 1, 1)
            down3(E3 - 1, 0)
            down3(E3 - 1, 1)
            pe.wait_ge(gate3t_done, 2)
            for h in range(HALVES):
                pe.wait_ge(y3_used, 2 * (E3 - 1) + h + 1)
                for t in range(4 * h, 4 * h + 4):
                    last = mm(psum[:, 4 + h, (t % 4) * C:(t % 4 + 1) * C], gate3_t[:, t * P:(t + 1) * P],
                              field("l3_small", "down_b")[0:E3, :], start=True, stop=True)
                last.then_inc(y3_ready, 1)

        @block.scalar
        def _(act):
            act.wait_ge(loaded["l2_decay"], 16)
            nc.scalar.activation(tau_e[0:D2, 0:1], field("l2_decay", "taus")[0:D2, :], ACT.Exp)
            nc.scalar.activation(tau_e[:, 1:2], field("l2_decay", "tau_ctx"), ACT.Exp).then_inc(taue_ready, 1)
            act.wait_ge(blend_ready, 1)
            nc.scalar.activation(bl_e[:, :], bl[:, :], ACT.Exp).then_inc(blexp_ready, 1)
            for h in range(HALVES):
                for k, rows in enumerate(LCH):
                    act.wait_ge(ad_ready, 3 * h + k + 1)
                    nc.scalar.activation(ad_hid[0:rows, k, h * HALF:(h + 1) * HALF], psum[0:rows, 3 * h + k, :],
                                         ACT.Relu, bias=field("l0_small", "b1")[0:rows, k:k + 1]
                                         ).then_inc(adhid_ready, 1)
            act.wait_ge(var_ready, 1)
            nc.scalar.activation(std[:, :], bn_m[:, :, 1], ACT.Sqrt, bias=field("consts", "eps")).then_inc(std_ready, 1)
            for h in range(HALVES):
                act.wait_ge(c0t_ready, h + 1)
                nc.scalar.activation(c0_ch[:, h * HALF:(h + 1) * HALF], psum[:, 4 + h, :], ACT.Copy
                                     ).then_inc(c0ch_ready, 1)
            act.wait_ge(rest_ready, 1)
            nc.scalar.activation(ex[:, :, :], rest[:, :, :], ACT.Exp).then_inc(exp_ready, 1)
            act.wait_ge(gather_ready, 1)
            for i in (0, 1):
                nc.scalar.activation(slot_in[:, :, :, i, :],
                                     psum[:, i, :].rearrange("p (t e c) -> p e t c", e=E0, c=CAP), ACT.Copy
                                     ).then_inc(slotin_act, 1)
            for h in range(HALVES):
                act.wait_ge(combt_ready, h + 1)
                nc.scalar.activation(comb_t[:, 4 * h:4 * h + 4, :],
                                     psum[:, 4 + h, :].rearrange("p (t q) -> p t q", q=P), ACT.Copy
                                     ).then_inc(combt_used, 1)
            for g in range(4):
                act.wait_ge(gatefc_ready, g + 1)
                nc.scalar.activation(silu0[:, g * HALF:(g + 1) * HALF], psum[0:H0, (6, 7, 4, 5)[g], :], ACT.Silu
                                     ).then_inc(silu_ready, 1)
            for g in (0, 1):
                act.wait_ge(proj_ready, g + 1)
                nc.scalar.activation(slot_ch[:, :, :, 4 * g:4 * g + 4, :].rearrange("p t i e c -> p (t i) e c"),
                                     psum[:, g, :].rearrange("p (e b c) -> p b e c", e=4, c=CAP), ACT.Copy
                                     ).then_inc(slotch_act, 1)
            for g in (0, 1):
                act.wait_ge(slott_ready, g + 1)
                nc.scalar.activation(slot_out[:, 4 * g:4 * g + 4, :],
                                     psum[:, 4 + g, :].rearrange("p (q c) -> p q c", c=C), ACT.Copy
                                     ).then_inc(slotout_act, 1)
            act.wait_ge(blt_ready, 1)
            nc.scalar.activation(lag_w[:, 0, :], psum[0:D2, 7, 0:C], ACT.Copy).then_inc(lag0_ready, 1)

            halves = [slice(h * HALF, (h + 1) * HALF) for h in range(HALVES)]
            for h in range(HALVES):
                act.wait_ge(x1t_ready, h + 1)
                nc.scalar.activation(x_tok[:, 4 * h:4 * h + 4, :], psum[:, 2 + h, :].rearrange("p (t c) -> p t c", c=C),
                                     ACT.Copy).then_inc(x1tok_ready, 1)
            for h, cols in enumerate(halves):
                act.wait_ge(attn_ready, h + 1)
                nc.scalar.activation(attn[:, cols], psum[0:ADIM, 4 + h, :], ACT.Tanh,
                                     bias=field("l1_small", "b1c")[0:ADIM, :]).then_inc(attn_done, 1)
            act.wait_ge(soft_ready, 1)
            nc.scalar.activation(soft_e[:, :, :], soft[:, :, :], ACT.Exp).then_inc(softexp_ready, 1)
            act.wait_ge(pooled_ready, 1)
            pooled = pool_ch[:, :].rearrange("p (t i s) -> p t i s", i=BPT, s=S)
            for i in (0, 1):
                nc.scalar.activation(pooled[:, :, i, :], psum[:, i, 0:TILES * S].rearrange("p (t s) -> p t s", s=S),
                                     ACT.Copy).then_inc(poolch_act, 1)

            units = [(e, k, h) for e in range(E1) for k in range(FCH1) for h in range(HALVES)]
            UNITS = FCH1 * HALVES
            act.wait_ge(ltok_done, 1)
            nc.scalar.activation(sig1[:, :, :], ltok[:, :, :], ACT.Sigmoid).then_inc(sig1_ready, 1)
            for u, (e, k, h) in enumerate(units):
                act.wait_ge(up1_ready, u + 1)
                if e >= 2 and u % UNITS == 0:
                    act.wait_ge(y1_ready, 2 * (e - 2) + 2)
                nc.scalar.activation(hid[:, e % 2, k, halves[h]], psum[:, u % 3, :], ACT.Gelu,
                                     bias=field("l1_small", "b1")[:, e * FCH1 + k:e * FCH1 + k + 1]
                                     ).then_inc(hid1_ready, 1)
                if u == 3 * UNITS - 1:
                    for a in range(2):
                        act.wait_ge(gate1t_ready, a + 1)
                        nc.scalar.activation(gate1_t[:, halves[a]], psum[0:E1, (5, 7)[a], :], ACT.Copy
                                             ).then_inc(gate1t_done, 1)

            l2 = lambda name: field("l2_all", name)
            for h, cols in enumerate(halves):
                act.wait_ge(x2t_ready, h + 1)
                nc.scalar.activation(x_ch[:, cols], psum[:, h, :], ACT.Copy).then_inc(x2ch_ready, 1)
            for h, cols in enumerate(halves):
                act.wait_ge(net_pre, h + 1)
                nc.scalar.activation(net[:, cols], psum[0:HN2, 4 + h, :], ACT.Gelu, bias=l2("bn1")[0:HN2, :]
                                     ).then_inc(net_ready, 1)
            for h, cols in enumerate(halves):
                act.wait_ge(soma_pre, h + 1)
                nc.scalar.activation(soma[:, cols], psum[:, 2 + h, :], ACT.Gelu, bias=l2("bsoma")
                                     ).then_inc(soma_ready, 1)
            for h, cols in enumerate(halves):
                act.wait_ge(wg_pre, h + 1)
                nc.scalar.activation(gated[:, cols], psum[:, h, :], ACT.Sigmoid, bias=l2("bg")).then_inc(wg_ready, 1)
            for h, cols in enumerate(halves):
                act.wait_ge(mod_pre, h + 1)
                nc.scalar.activation(mod[:, cols], psum[0:D2, 6 + h, :], ACT.Sigmoid, bias=l2("bn2")[0:D2, :]
                                     ).then_inc(mod_sig, 1)
            for h, cols in enumerate(halves):
                act.wait_ge(tg_pre, h + 1)
                nc.scalar.activation(tgate[:, cols], psum[:, h, :], ACT.Sigmoid, bias=l2("btemp")).then_inc(tg_ready, 1)
            act.wait_ge(var_ready, 2)
            nc.scalar.activation(std[:, :], bn_m[:, :, 1], ACT.Sqrt, bias=field("consts", "eps")).then_inc(std_ready, 1)
            for h, cols in enumerate(halves):
                act.wait_ge(yt_ready, h + 1)
                nc.scalar.activation(y_ch[:, cols], psum[:, 4 + h, :], ACT.Identity, bias=l2("beta"), scale=l2("gamma")
                                     ).then_inc(ych_ready, 1)
            for h, cols in enumerate(halves):
                act.wait_ge(low_pre, h + 1)
                nc.scalar.activation(low[:, cols], psum[0:RK2, 6 + h, :], ACT.Copy).then_inc(low_ready, 1)
            for u in range(HALVES * FCH2):
                h, k = u // FCH2, u % FCH2
                act.wait_ge(ff2_pre, u + 1)
                nc.scalar.activation(hid[:, 0, k, halves[h]], psum[:, u % 4, :], ACT.Gelu_apprx_tanh,
                                     bias=l2("b1")[:, k:k + 1]).then_inc(ff2_ready, 1)
            for h, cols in enumerate(halves):
                act.wait_ge(low2_pre, h + 1)
                nc.scalar.activation(low2[:, cols], psum[0:RK2, 4 + h, :], ACT.Copy).then_inc(low2_ready, 1)

            for h in range(HALVES):
                act.wait_ge(x3t_ready, h + 1)
                nc.scalar.activation(x_tok[:, 4 * h:4 * h + 4, :], psum[:, 6 + h, :].rearrange("p (t c) -> p t c", c=C),
                                     ACT.Copy).then_inc(x3tok_ready, 1)
            act.wait_ge(rest3_ready, 1)
            nc.scalar.activation(ex[:, :, 0:E3], rest[:, :, 0:E3], ACT.Exp).then_inc(exp3_ready, 1)
            units3 = [(e, k, h) for e in range(E3) for k in range(FCH3) for h in range(HALVES)]
            for u, (e, k, h) in enumerate(units3):
                act.wait_ge(g3_ready, u + 1)
                if u >= 2:
                    act.wait_ge(hid3_ready, u - 1)
                nc.scalar.activation(silu3[:, u % 2, :], psum[:, u % 2, :], ACT.Silu,
                                     bias=field("l3_small", "gate_b")[:, e * FCH3 + k:e * FCH3 + k + 1]
                                     ).then_inc(silu3_ready, 1)
                if u == 2 * FCH3 * HALVES - 1:
                    for a in range(2):
                        act.wait_ge(gate3t_ready, a + 1)
                        nc.scalar.activation(gate3_t[:, halves[a]], psum[0:E3, 6 + a, :], ACT.Copy
                                             ).then_inc(gate3t_done, 1)

        @block.vector
        def _(dve):
            steps = [0]
            ts, tt = nc.vector.tensor_scalar, nc.vector.tensor_tensor
            stt, red = nc.vector.scalar_tensor_tensor, nc.vector.tensor_reduce

            def chain(ins):
                steps[0] += 1
                ins.then_inc(dve_step, 1)
                dve.wait_ge(dve_step, steps[0])

            def layer_stats(src):
                for t in range(TILES):
                    last = nc.vector.bn_stats(bn_s[:, t, :], src(t))
                chain(last)
                for t in range(TILES):
                    last = nc.vector.bn_aggr(bn_m[:, t, :], bn_s[:, t, :])
                last.then_inc(var_ready, 1)

            dve.wait_ge(loaded["l2_decay"], 16)
            blend = field("l2_decay", "blend")
            chain(red(bl_max[:, :], blend, X_AXIS, ALU.max))
            ts(bl[:, :], blend, bl_max[:, :], None, ALU.subtract).then_inc(blend_ready, 1)
            dve.wait_ge(taue_ready, 1)
            ts(tau_e[0:D2, 0:1], tau_e[0:D2, 0:1], 1.0, None, ALU.add)
            chain(ts(tau_e[:, 1:2], tau_e[:, 1:2], 1.0, None, ALU.add))
            nc.vector.reciprocal(alpha[0:D2, 0:1], tau_e[0:D2, 0:1])
            nc.vector.reciprocal(alpha[:, 1:2], tau_e[:, 1:2]).then_inc(alpha_ready, 1)
            dve.wait_ge(blexp_ready, 1)
            chain(red(bl_sum[:, :], bl_e[:, :], X_AXIS, ALU.add))
            chain(nc.vector.reciprocal(bl_sum[:, :], bl_sum[:, :]))
            ts(bl[:, :], bl_e[:, :], bl_sum[:, :], None, ALU.mult).then_inc(blw_ready, 1)

            dve.wait_ge(loaded["x_tok"], 16)
            for h in range(HALVES):
                dve.wait_ge(adapt_ready, h + 1)
                last = tt(res0[:, 4 * h:4 * h + 4, :], psum[:, 6 + h, :].rearrange("p (t c) -> p t c", c=C),
                          x_tok[:, 4 * h:4 * h + 4, :], ALU.add)
            chain(last)
            layer_stats(lambda t: res0[:, t, :])
            dve.wait_ge(std_ready, 1)
            chain(nc.vector.reciprocal(rstd[:, :], std[:, :]))
            for t in range(TILES):
                last = ts(res0[:, t, :], res0[:, t, :], bn_m[:, t, 0:1], rstd[:, t:t + 1], ALU.subtract, ALU.mult)
            chain(last)
            dve.wait_ge(affine_ready, 1)
            for h in range(HALVES):
                tiles = slice(4 * h, 4 * h + 4)
                affine = psum[:, 2 * h:2 * h + 2, :].rearrange("p b (t a c) -> p (b t) a c", a=2, c=C)
                chain(tt(res0[:, tiles, :], affine[:, :, 0, :], res0[:, tiles, :], ALU.mult))
                tt(c0[:, tiles, :], affine[:, :, 1, :], res0[:, tiles, :], ALU.add).then_inc(c0_ready, 1)

            def first_best(src, best, onehot, iota, n):
                chain(red(best[:, :], src[:, :, 0:n], X_AXIS, ALU.max))
                chain(tt(eqm[:, :, 0:n], src[:, :, 0:n], bc(best[:, :], 2, n), ALU.is_equal))
                chain(tt(eqm[:, :, 0:n], eqm[:, :, 0:n], bc(iota, 1, TILES), ALU.mult))
                chain(red(pick[:, :], eqm[:, :, 0:n], X_AXIS, ALU.min))
                return tt(onehot[:, :, 0:n], bc(iota, 1, TILES), bc(pick[:, :], 2, n), ALU.is_equal)

            flat = "p t e -> p (t e)"
            iota16 = field("consts", "iota16")
            dve.wait_ge(lg_ready, 1)
            chain(nc.vector.tensor_copy(lg[:, :, :].rearrange(flat), psum[:, 6, 0:TILES * E0]))
            chain(first_best(lg, top1, oh1, iota16, E0))
            nc.vector.tensor_copy(oh1_h[:, :], oh1[:, :, :].rearrange(flat)).then_inc(choice_ready, 1)
            chain(stt(rest[:, :, :].rearrange(flat), oh1[:, :, :].rearrange(flat), NEG, lg[:, :, :].rearrange(flat),
                      ALU.mult, ALU.add))
            chain(first_best(rest, top2, oh2, iota16, E0))
            nc.vector.tensor_copy(oh2_h[:, :], oh2[:, :, :].rearrange(flat)).then_inc(choice_ready, 1)
            tt(rest[:, :, :], lg[:, :, :], bc(top1[:, :], 2, E0), ALU.subtract).then_inc(rest_ready, 1)
            dve.wait_ge(exp_ready, 1)
            chain(red(exsum[:, :], ex[:, :, :], X_AXIS, ALU.add))
            nc.vector.reciprocal(rsum[:, :], exsum[:, :])
            chain(tt(eqm[:, :, :], oh1[:, :, :], oh2[:, :, :], ALU.add))
            chain(tt(prob[:, :, :], ex[:, :, :], eqm[:, :, :], ALU.mult))
            chain(tt(prob[:, :, :], prob[:, :, :], bc(rsum[:, :], 2, E0), ALU.mult))
            dve.wait_ge(rank_ready, 1)
            rank = psum[:, 7, 0:2 * P].rearrange("p (a q) -> p a q", a=2)
            tt(posa[:, :, :].rearrange(flat), rank[:, 0, :], oh1[:, :, :].rearrange(flat), ALU.mult)
            chain(tt(posb[:, :, :].rearrange(flat), rank[:, 1, :], oh2[:, :, :].rearrange(flat), ALU.mult))
            chain(tt(posa[:, :, :], posa[:, :, :], posb[:, :, :], ALU.add))
            for c in range(CAP):
                last = ts(disp[:, :, :, c], posa[:, :, :], float(c + 1), None, ALU.is_equal)
            last.then_inc(disp_ready, 1)
            chain(ts(posb[:, :, :], posa[:, :, :], float(CAP), None, ALU.min))
            for twice in range(2):
                for c in range(CAP):
                    last = stt(comb[:, :, twice, :, c], posb[:, :, :], float(c + 1), prob[:, :, :],
                               ALU.is_equal, ALU.mult)
            last.then_inc(comb_ready, 1)
            dve.wait_ge(gather_ready, 1)
            for i in (2, 3):
                nc.vector.tensor_copy(slot_in[:, :, :, i, :],
                                      psum[:, i, :].rearrange("p (t e c) -> p e t c", e=E0, c=CAP)
                                      ).then_inc(slotin_dve, 1)
            for g in range(4):
                dve.wait_ge(silu_ready, g + 1)
                cols = slice(g * HALF, (g + 1) * HALF)
                tt(hid0[:, cols], psum[H0:2 * H0, (6, 7, 4, 5)[g], :], silu0[:, cols], ALU.mult).then_inc(hid0_ready, 1)
            for g in (2, 3):
                dve.wait_ge(proj_ready, g + 1)
                nc.vector.tensor_copy(slot_ch[:, :, :, 4 * g:4 * g + 4, :].rearrange("p t i e c -> p (t i) e c"),
                                      psum[:, g, :].rearrange("p (e b c) -> p b e c", e=4, c=CAP)
                                      ).then_inc(slotch_dve, 1)
            for g in (2, 3):
                dve.wait_ge(slott_ready, g + 1)
                nc.vector.tensor_copy(slot_out[:, 4 * g:4 * g + 4, :],
                                      psum[:, 4 + g, :].rearrange("p (q c) -> p q c", c=C)).then_inc(slotout_dve, 1)
            dve.wait_ge(y0_ready, 1)
            by_parity = x_ch[:, :].rearrange("p (q a s) -> p a q s", a=2, s=S)
            for a in range(2):
                last = tt(by_parity[:, a, :, :], psum[:, a, :].rearrange("p (q s) -> p q s", s=S),
                          by_parity[:, a, :, :], ALU.add)
            last.then_inc(x1_ready, 1)

            dve.wait_ge(score_ready, 1)
            tt(score_d[:, :, :], bc(eye32, 1, TILES), bc(psum[:, 6, 0:TILES], 2, S), ALU.mult).then_inc(scored_ready, 1)
            dve.wait_ge(spread_ready, 1)
            chain(tt(soft[:, :, :], psum[:, 7, 0:TILES * S].rearrange("p (t s) -> p t s", s=S), mask_add[:, :, :],
                     ALU.add))
            chain(red(rmax[:, :], soft[:, :, :], X_AXIS, ALU.max))
            tt(soft[:, :, :], soft[:, :, :], bc(rmax[:, :], 2, S), ALU.subtract).then_inc(soft_ready, 1)
            dve.wait_ge(softexp_ready, 1)
            chain(red(rden[:, :], soft_e[:, :, :], X_AXIS, ALU.add))
            chain(tt(rden[:, :], rden[:, :], seen[:, :], ALU.mult))
            chain(nc.vector.reciprocal(rden[:, :], rden[:, :]))
            chain(tt(soft_e[:, :, :], soft_e[:, :, :], bc(rden[:, :], 2, S), ALU.mult))
            nc.vector.transpose(soft_t[:, :, :].rearrange("p t s -> p (t s)"),
                                soft_e[:, :, :].rearrange("p t s -> p (t s)")).then_inc(softt_ready, 1)
            dve.wait_ge(pooled_ready, 1)
            pooled = pool_ch[:, :].rearrange("p (t i s) -> p t i s", i=BPT, s=S)
            for i in (2, 3):
                nc.vector.tensor_copy(pooled[:, :, i, :], psum[:, i, 0:TILES * S].rearrange("p (t s) -> p t s", s=S)
                                      ).then_inc(poolch_dve, 1)

            nc.vector.memset(best_thr[:, :], -BOUND)
            for h in range(HALVES):
                dve.wait_ge(lrow_ready, h + 1)
                ts(lrow[:, h * HALF:(h + 1) * HALF], psum[:, 4 + h, :], -BOUND, None, ALU.max).then_inc(lrow_done, 1)
            dve.wait_ge(ltok_ready, 1)
            nc.vector.tensor_copy(ltok[:, :, :].rearrange(flat), psum[:, 6, 0:TILES * E1]).then_inc(ltok_done, 1)
            for r in range(ROUNDS):
                width = 2 * BOUND / 16.0 ** (r + 1)
                chain(tt(thr[:, :], best_thr[:, :], field("consts", "steps")[:, r:r + 1], ALU.add))
                chain(ts(above_row[:, :], lrow[:, :], thr[:, :], None, ALU.is_ge, ALU.add, accum_out=hits[:, :]))
                ts(enough_h[:, :], hits[:, :], float(TOP1), None, ALU.is_ge).then_inc(enough_ready, 1)
                dve.wait_ge(count_ready, r + 1)
                chain(stt(best_thr[:, :], psum[:, 6, 0:1], width, best_thr[:, :], ALU.mult, ALU.add))
            chain(ts(best_end[:, :], best_thr[:, :], width, None, ALU.add))
            eye8 = field("consts", "eye8")[0:E1, :]
            ts(thr_d[:, 0, :], eye8, best_thr[0:E1, :], None, ALU.mult)
            ts(thr_d[:, 1, :], eye8, best_end[0:E1, :], None, ALU.mult).then_inc(thrd_ready, 1)
            dve.wait_ge(thrtok_ready, 1)
            low_end = bc(psum[:, 6, 0:E1], 1, TILES)
            tt(sure[:, :, :], ltok[:, :, :], bc(psum[:, 6, E1:2 * E1], 1, TILES), ALU.is_ge)
            chain(tt(tied[:, :, :], ltok[:, :, :], low_end, ALU.is_gt))
            chain(tt(sure[:, :, :], sure[:, :, :], tied[:, :, :], ALU.mult))
            chain(tt(tied[:, :, :], ltok[:, :, :], low_end, ALU.is_ge))
            nc.vector.tensor_copy(sure_h[:, :, :], sure[:, :, :])
            chain(tt(tied[:, :, :], tied[:, :, :], sure[:, :, :], ALU.subtract))
            nc.vector.tensor_copy(tied_h[:, :], tied[:, :, :].rearrange(flat)).then_inc(tied_ready, 1)
            dve.wait_ge(order_ready, 1)
            chain(ts(room[:, :], psum[:, 7, HALF - E1:HALF], -1.0, float(TOP1), ALU.mult, ALU.add))
            chain(tt(gate1[:, :, :], psum[:, 7, 0:TILES * E1].rearrange("p (t e) -> p t e", e=E1),
                     bc(room[:, :], 1, TILES), ALU.is_le))
            chain(tt(gate1[:, :, :], gate1[:, :, :], tied[:, :, :], ALU.mult))
            chain(tt(gate1[:, :, :], gate1[:, :, :], sure[:, :, :], ALU.add))
            dve.wait_ge(sig1_ready, 1)
            tt(gate1[:, :, :], gate1[:, :, :], sig1[:, :, :], ALU.mult).then_inc(gate1_ready, 1)
            dve.wait_ge(gate1_ready, 1)
            for g in range(2 * E1):
                e, h = g // 2, g % 2
                dve.wait_ge(y1_ready, g + 1)
                if g >= 2:
                    dve.wait_ge(y1_used, g - 1)
                for t in range(4 * h, 4 * h + 4):
                    last = stt(x_tok[:, t, :], psum[:, 3 + h, (t % 4) * C:(t % 4 + 1) * C], gate1[:, t, e:e + 1],
                               x_tok[:, t, :], ALU.mult, ALU.add)
                last.then_inc(y1_used, 1)
            for h in range(HALVES):
                dve.wait_ge(y1_ready, 2 * E1 + h + 1)
                dve.wait_ge(y1_used, 2 * E1 + h - 1)
                tt(x_tok[:, 4 * h:4 * h + 4, :], psum[:, 3 + h, :].rearrange("p (t c) -> p t c", c=C),
                   x_tok[:, 4 * h:4 * h + 4, :], ALU.add).then_inc(y1_used, 1)

            halves = [slice(h * HALF, (h + 1) * HALF) for h in range(HALVES)]
            dve.wait_ge(decay_ready, 1)
            dve.wait_ge(x2ch_ready, 2)
            nc.vector.tensor_tensor_scan(ctx_ch[:, :], decay[:, :], x_ch[:, :], 0.0, ALU.mult, ALU.add
                                         ).then_inc(ctx_ready, 1)
            dve.wait_ge(mod_sig, 2)
            ts(mod[:, :], mod[:, :], 0.5, None, ALU.add).then_inc(mod_ready, 1)
            dve.wait_ge(wg_ready, 2)
            chain(tt(gated[:, :], gated[:, :], x_ch[:, :], ALU.mult))
            gateds = gated[:, :].rearrange("p (a b s) -> p a b s", a=2, s=S)
            for lag in range(S):
                n = S - lag
                bank = 2 * (lag % 4)
                dve.wait_ge(lag_ready, lag + 1)
                if lag >= 4:
                    dve.wait_ge(summed, lag - 3)
                dst = temporal[:, :] if lag == 0 else prod[:, lag % 3, 0:B * n]
                tt(dst.rearrange("p (a b s) -> p a b s", a=2, s=n),
                   psum[:, bank:bank + 2, 0:16 * n].rearrange("p a (b s) -> p a b s", s=n), gateds[:, :, :, 0:n],
                   ALU.mult).then_inc(prod_ready, 1)
            for h, cols in enumerate(halves):
                dve.wait_ge(tg_ready, h + 1)
                tt(soma[:, cols], soma[:, cols], tgate[:, cols], ALU.mult).then_inc(sg_ready, 1)
            dve.wait_ge(out2_ready, 2)
            out2 = lambda t: psum[:, 2 + t // 4, (t % 4) * C:(t % 4 + 1) * C]
            layer_stats(out2)
            dve.wait_ge(std_ready, 2)
            chain(nc.vector.reciprocal(rstd[:, :], std[:, :]))
            for t in range(TILES):
                last = ts(ynorm[:, t, :], out2(t), bn_m[:, t, 0:1], rstd[:, t:t + 1], ALU.subtract, ALU.mult)
                if t % 4 == 3:
                    last.then_inc(ynorm_ready, 1)
            for h, cols in enumerate(halves):
                dve.wait_ge(y2_ready, h + 1)
                stt(x_ch[:, cols], psum[:, 6 + h, :], field("l2_all", "b2"), x_ch[:, cols], ALU.add, ALU.add
                    ).then_inc(x3_ready, 1)

            dve.wait_ge(z_ready, 1)
            chain(nc.vector.tensor_copy(subj_bias[:, :], psum[:, 2, 0:B]))
            for h, cols in enumerate(halves):
                dve.wait_ge(z_ready, h + 1)
                tt(z_ch[:, cols].rearrange("p (b s) -> p b s", s=S), psum[:, h, :].rearrange("p (b s) -> p b s", s=S),
                   bc(subj_bias[:, 16 * h:16 * (h + 1)], 2, S), ALU.add).then_inc(zch_ready, 1)
            iota8 = field("consts", "iota8")
            n = E3
            dve.wait_ge(lg3_ready, 1)
            chain(nc.vector.tensor_copy(lg[:, :, 0:n], psum[:, 3, 0:TILES * n].rearrange("p (t e) -> p t e", e=n)))
            chain(first_best(lg, top1, oh1, iota8, n))
            chain(stt(rest[:, :, 0:n], oh1[:, :, 0:n], NEG, lg[:, :, 0:n], ALU.mult, ALU.add))
            chain(first_best(rest, top2, oh2, iota8, n))
            tt(rest[:, :, 0:n], lg[:, :, 0:n], bc(top1[:, :], 2, n), ALU.subtract).then_inc(rest3_ready, 1)
            dve.wait_ge(exp3_ready, 1)
            chain(red(exsum[:, :], ex[:, :, 0:n], X_AXIS, ALU.add))
            chain(nc.vector.reciprocal(rsum[:, :], exsum[:, :]))
            chain(tt(eqm[:, :, 0:n], oh1[:, :, 0:n], oh2[:, :, 0:n], ALU.add))
            chain(tt(prob[:, :, 0:n], ex[:, :, 0:n], eqm[:, :, 0:n], ALU.mult))
            chain(tt(prob[:, :, 0:n], prob[:, :, 0:n], bc(rsum[:, :], 2, n), ALU.mult))
            chain(red(exsum[:, :], prob[:, :, 0:n], X_AXIS, ALU.add))
            chain(ts(exsum[:, :], exsum[:, :], 1e-9, None, ALU.add))
            chain(nc.vector.reciprocal(rsum[:, :], exsum[:, :]))
            tt(gate3[:, :, :], prob[:, :, 0:n], bc(rsum[:, :], 2, n), ALU.mult).then_inc(gate3_ready, 1)
            dve.wait_ge(gate3_ready, 1)
            dve.wait_ge(x3tok_ready, 2)
            units3 = [(e, k, h) for e in range(E3) for k in range(FCH3) for h in range(HALVES)]
            UNITS3 = FCH3 * HALVES

            def hidden3(u):
                e, k, h = units3[u]
                dve.wait_ge(silu3_ready, u + 1)
                dve.wait_ge(u3_ready, u + 1)
                if e >= 2 and u % UNITS3 == 0:
                    dve.wait_ge(y3_ready, 2 * (e - 2) + 2)
                stt(hid[:, 0, (e % 2) * 2 + k, halves[h]], psum[:, 2 + u % 2, :],
                    field("l3_small", "up_b")[:, e * FCH3 + k:e * FCH3 + k + 1], silu3[:, u % 2, :],
                    ALU.add, ALU.mult).then_inc(hid3_ready, 1)

            def output3(g):
                e, h = g // 2, g % 2
                dve.wait_ge(y3_ready, g + 1)
                if g >= 2:
                    dve.wait_ge(y3_used, g - 1)
                for t in range(4 * h, 4 * h + 4):
                    last = stt(x_tok[:, t, :], psum[:, 4 + h, (t % 4) * C:(t % 4 + 1) * C], gate3[:, t, e:e + 1],
                               x_tok[:, t, :], ALU.mult, ALU.add)
                last.then_inc(y3_used, 1)

            for e in range(E3):
                for u in range(e * UNITS3, (e + 1) * UNITS3):
                    hidden3(u)
                if e >= 1:
                    output3(2 * (e - 1))
                    output3(2 * (e - 1) + 1)
            output3(2 * (E3 - 1))
            output3(2 * (E3 - 1) + 1)
            for h in range(HALVES):
                dve.wait_ge(y3_ready, 2 * E3 + h + 1)
                dve.wait_ge(y3_used, 2 * E3 + h - 1)
                tt(x_tok[:, 4 * h:4 * h + 4, :], psum[:, 4 + h, :].rearrange("p (t c) -> p t c", c=C),
                   x_tok[:, 4 * h:4 * h + 4, :], ALU.add).then_inc(y3_used, 1)


def layouts(inputs):
    import numpy as np

    f = {k: np.asarray(v) for k, v in inputs.items()}

    def rows(a, n=P):
        a = np.asarray(a)
        return np.concatenate([a, np.zeros((n - a.shape[0],) + a.shape[1:], a.dtype)]) if a.shape[0] < n else a

    def col(a):
        return rows(np.asarray(a).reshape(-1, 1))

    def cols(a):
        return np.asarray(a).reshape(-1, P).T

    def kmajor(a):
        return a.transpose(1, 0, 2).reshape(a.shape[1], -1)

    def chunked(a):
        return a.reshape(-1, P, a.shape[-1]).transpose(1, 0, 2).reshape(P, -1)

    p = np.arange(P)
    j, l = p[:, None] % S, np.arange(S)[None, :]
    own = np.repeat(np.eye(LANGS, dtype=bool), ADIM, axis=1)
    lang_ff = f["L0_cond_W1"].shape[0] * ADIM
    w2 = rows(f["L0_cond_W2"].reshape(lang_ff, C), 3 * P)
    fields = {
        "consts": {
            "ident": np.eye(P), "eye32": j == l, "tri_batch": (p[:, None] // S == p // S) & (p[:, None] <= p),
            "ones_batch": p[:, None] // S == p // S, "tri_all": p[:, None] <= p,
            "same_expert": (p[:, None] % E1 == p % E1) & (p[:, None] >= E1), "far": rows(np.where(own, 0.0, FAR)), "pidx": p[:, None],
            "mask_pre": np.where(l <= j, 0.0, NEG), "mask_post": np.where(l >= j, 0.0, NEG),
            "mask_cloze": np.where(l != j, 0.0, NEG),
            "counts": np.concatenate([j + 1, S - j, 0 * j + S - 1], 1),
            "iota16": np.tile(np.arange(E0) - E0, (P, 1)), "iota8": np.tile(np.arange(E3) - E3, (P, 1)),
            "eps": np.full((P, 1), EPS),
            "steps": (p[:, None] // E1) * (2 * BOUND / 16.0 ** (1 + np.arange(ROUNDS)))[None, :],
            "eye8": rows(np.eye(8)),
        },
        "l0_small": {
            "w1": kmajor(f["L0_cond_W1"]), "b1": cols(rows(f["L0_cond_b1"].reshape(-1), 3 * P)),
            "table": rows(np.concatenate([f["L0_cond_b2"], f["L0_cond_gamma"], f["L0_cond_beta"]], 1)),
            "w2": chunked(w2), "router": f["L0_ffn_w_router"],
        },
        "l0_gatefc": {"gatefc": kmajor(np.concatenate([f["L0_ffn_w_gate"], f["L0_ffn_w_fc"]], 2))},
        "l0_proj": {"proj": rows(kmajor(f["L0_ffn_w_proj"]))},
        "l1_small": {
            "w1c": f["L1_cond_W1"], "b1c": col(f["L1_cond_b1"]), "v": col(f["L1_cond_v"]),
            "router": np.tile(f["L1_ffn_Wg"], (1, RANK_PARTS)), "b1": cols(f["L1_ffn_b1"]),
            "b2": rows(f["L1_ffn_b2"]),
        },
        "l1_w1": {"w1": kmajor(f["L1_ffn_W1"])},
        "l1_w2": {"w2": chunked(f["L1_ffn_W2"])},
        "l2_decay": {
            "blend": f["cond_1024"].T, "taus": col(f["condB_tauraws"]),
            "tau_ctx": np.tile(f["L2_cond_tau_ctx"].reshape(1, 1), (P, 1)),
        },
        "l2_all": {
            "wg_x": f["L2_cond_Wg"][:, 0:C].T, "wg_ctx": f["L2_cond_Wg"][:, C:2 * C].T, "bg": col(f["L2_cond_bg"]),
            "wn1": f["L2_cond_Wn1"].T, "bn1": col(f["L2_cond_bn1"]), "wn2": rows(f["cond_256"].T),
            "bn2": col(f["condB_bn2"]), "wtemp": f["L2_cond_Wtemp"].T,
            "btemp": col(f["L2_cond_btemp"]), "wsoma": f["L2_cond_Wsoma"].T, "bsoma": col(f["L2_cond_bsoma"]),
            "wout": f["L2_cond_Wout"].T, "gamma": col(f["L2_cond_gamma"]), "beta": col(f["L2_cond_beta"]),
            "u1": f["L2_ffn_U1"], "v1": rows(f["L2_ffn_V1"]), "b1": cols(f["L2_ffn_b1"]),
            "u2": chunked(f["L2_ffn_U2"]), "v2": rows(f["L2_ffn_V2"]), "b2": col(f["L2_ffn_b2"]),
        },
        "l3_small": {
            "cbias": rows(f["L3_cond_bias"]), "router": f["L3_ffn_router_w"].T, "gate_b": cols(f["L3_ffn_gate_b"]),
            "up_b": cols(f["L3_ffn_up_b"]), "down_b": rows(f["L3_ffn_down_b"]),
        },
        "l3_gate": {"gate": kmajor(f["L3_ffn_gate_w"])},
        "l3_up": {"up": kmajor(f["L3_ffn_up_w"])},
        "l3_down": {"down": chunked(f["L3_ffn_down_w"])},
    }
    arrays = {}
    for pack, names in PACKS.items():
        parts = [np.asarray(fields[pack][name]) for name, _ in names]
        for (name, width), part in zip(names, parts):
            assert part.shape == (P, width), (pack, name, part.shape)
        if pack == "consts":
            parts = [np.asarray(part, np.float32) for part in parts]
        arrays[pack] = np.ascontiguousarray(np.concatenate(parts, 1))
    ids = np.concatenate([f["itok_B_0_8"], f["itok_B_0_2"], f["itok_B_0_7"]])
    arrays["ids"] = np.ascontiguousarray(np.tile(ids[None, :], (P, 1)))
    arrays["types"] = np.ascontiguousarray(np.repeat(f["itok_B_0_2"].reshape(TILES, BPT), S, axis=1).T)
    arrays["x"] = np.ascontiguousarray(f["x"].reshape(N, C))
    arrays["x_ch"] = np.ascontiguousarray(f["x"].reshape(N, C).T)
    arrays["subj_w"] = np.ascontiguousarray(f["L3_cond_weight"].transpose(0, 2, 1))
    return arrays


def kernel(**inputs):
    import concourse.bacc as bacc
    from concourse.bass_utils import run_bass_kernel_spmd

    arrays = layouts(inputs)
    nc = bacc.Bacc("TRN2", target_bir_lowering=False, num_devices=1)
    dram = {name: nc.dram_tensor("in_" + name, a.shape, mybir.dt.from_np(a.dtype), kind="ExternalInput").ap()
            for name, a in arrays.items()}
    out = nc.dram_tensor("out", (B, S, C), F32, kind="ExternalOutput").ap()
    program(nc, dram, out)
    r = run_bass_kernel_spmd(nc, [{"in_" + name: a for name, a in arrays.items()}], core_ids=[0])
    return r.results[0]["out"]
```

```python
from contextlib import ExitStack

import concourse.bass as bass
from concourse import mybir

F32 = mybir.dt.float32
F32R = mybir.dt.float32r
BF16 = mybir.dt.bfloat16
I32 = mybir.dt.int32
ALU = mybir.AluOpType
ACT = mybir.ActivationFunctionType
X_AXIS = mybir.AxisListType.X

P = 128
B, S, C = 32, 32, 128
N = B * S
TILES = N // P
BPT = P // S
HALF = 512
HALVES = N // HALF
LANGS, ADIM = 10, 32
LCH = (P, P, 64)
E0, H0, CAP = 16, 64, 4
SLOTS = E0 * CAP
E1, FF1 = 8, 512
FCH1 = FF1 // P
TOP1 = N * 2 // E1
RANK_PARTS = P // E1
BOUND = 128.0
ROUNDS = 8
D2 = 32
HN2 = 32
FF2, RK2 = 512, 32
FCH2 = FF2 // P
SUBJ = 8
E3, FF3 = 8, 256
FCH3 = FF3 // P
VECTOR_LAGS = [lag for lag in range(3, S) if lag % 5 in (0, 3)]
POOL_LAGS = [lag for lag in range(1, S) if lag not in VECTOR_LAGS]
NEG = -1.0e30
FAR = -(2.0 ** 100)
EPS = 1e-5

PACKS = {
    "early": [("far", LANGS * ADIM), ("pidx", 1), ("eps", 1)],
    "l0_w1": [("w1", LANGS * ADIM), ("b1", 3)],
    "consts": [("ident", P), ("eye32", 32), ("tri_batch", P), ("ones_batch", P), ("tri_all", P),
               ("same_expert", P), ("mask_pre", 32), ("mask_post", 32),
               ("mask_cloze", 32), ("counts", 3), ("iota16", E0), ("iota8", E3),
               ("steps", ROUNDS), ("eye8", 8), ("batch_in_tile", BPT), ("parity", 2), ("lo_w", 1), ("lo_x", 1)],
    "l0_small": [("table", 3 * C), ("w2", 3 * C), ("router", E0)],
    "l0_gatefc": [("gatefc", E0 * 2 * H0)],
    "l0_proj": [("proj", E0 * C)],
    "l1_small": [("w1c", ADIM), ("b1c", 1), ("v", 1), ("router", P), ("b1", E1 * FCH1), ("b2", C)],
    "l1_w1": [("w1", E1 * FF1)],
    "l1_w2": [("w2", E1 * FCH1 * C)],
    "l2_decay": [("blend", P), ("taus", 1), ("tau_ctx", 1)],
    "l2_all": [("wg_x", C), ("wg_ctx", C), ("bg", 1), ("wn1", HN2), ("bn1", 1), ("wn2", P), ("bn2", 1),
               ("wtemp", C), ("btemp", 1), ("wsoma", C),
               ("bsoma", 1), ("wout", C), ("gamma", 1), ("beta", 1), ("u1", P), ("v1", FF2),
               ("b1", FCH2), ("u2", FCH2 * RK2), ("v2", C), ("b2", 1)],
    "l3_small": [("cbias", C), ("router", E3), ("gate_b", E3 * FCH3), ("up_b", E3 * FCH3), ("down_b", C)],
    "l3_gate": [("gate", E3 * FF3)],
    "l3_up": [("up", E3 * FF3)],
    "l3_down": [("down", E3 * FCH3 * C)],
}
WIDTH = {pack: sum(w for _, w in fields) for pack, fields in PACKS.items()}


def bc(ap, axis, n):
    shape = list(ap.shape)
    shape.insert(axis, n)
    return ap.unsqueeze(axis).to_broadcast(shape)


def program(nc, dram, out):
    ctx = ExitStack()
    with ctx:
        def sb(name, shape, dt=F32):
            return ctx.enter_context(nc.sbuf_tensor(name, shape, dt))

        def sem(name):
            return ctx.enter_context(nc.semaphore(name))

        psum = ctx.enter_context(nc.psum_tensor("psum", [P, 8, HALF], F32))

        shares = {"l3_gate": "l0_gatefc", "l3_up": "l0_proj"}
        packs = {name: sb("sb_" + name, [P, w]) for name, w in WIDTH.items() if name not in shares}
        packs.update({name: packs[old] for name, old in shares.items()})

        def field(pack, name):
            at = 0
            for f, w in PACKS[pack]:
                if f == name:
                    return packs[pack][:, at:at + w]
                at += w
            raise KeyError(name)

        ident, eye32, pidx = field("consts", "ident"), field("consts", "eye32"), field("early", "pidx")
        x_tok = sb("x_tok", [P, TILES, C])
        x_ch = sb("x_ch", [P, N])
        ids_i = sb("ids_i", [P, 3 * B], I32)
        types_i = sb("types_i", [P, TILES], I32)
        subj_w = packs["l1_w1"][:, 0:B * C].rearrange("p (b c) -> p b c", c=C)

        loaded = {name: sem("loaded_" + name) for name in list(WIDTH) + ["ids", "types", "x_ch", "x_ch2", "x_tok"]}
        subj_loaded = sem("subj_loaded")

        far_h = sb("far_h", [LANGS, LANGS * ADIM], BF16)
        tri_batch_h = sb("tri_batch_h", [P, P], BF16)
        ones_batch_h = sb("ones_batch_h", [P, P], BF16)
        tri_all_h = sb("tri_all_h", [P, P], BF16)
        same_expert_h = sb("same_expert_h", [P, P], BF16)
        ones_h = sb("ones_h", [P, P], BF16)
        ones_f = sb("ones_f", [P, P])
        ids_f = sb("ids_f", [P, 3 * B])
        types_f = sb("types_f", [P, TILES])
        lang_b = sb("lang_b", [LANGS, B])
        lang_h = sb("lang_h", [LANGS, N], BF16)
        lang_f_rows = sb("lang_f_rows", [P, N])
        lang_f = lang_f_rows[0:LANGS, :]
        subj_b = sb("subj_b", [SUBJ, B])
        type_sel = sb("type_sel", [P, 3, TILES])
        mask_add = sb("mask_add", [P, TILES, S])
        mask_tmp = sb("mask_tmp", [P, TILES, S])
        seen = sb("seen", [P, TILES])
        seen_tmp = sb("seen_tmp", [P, TILES])
        pool_step = sem("pool_step")
        far_ready = sem("far_ready")
        lang_ready = sem("lang_ready")
        langf_ready = sem("langf_ready")
        consts_ready = sem("consts_ready")

        with nc.sbuf_tensor("big", [P, 8 * N], F32) as big:
            pass
        mod_hi = sb("mod_hi", [P, N], F32R)
        mod_w = sb("mod_w", [P, N], F32R)
        traces_v = sb("traces_v", [P, N])
        prod_v = sb("prod_v", [P, N])
        gated_s = sb("gated_s", [P, N])
        v1_w = sb("v1_w", [P, FF2], F32R)
        under_big = sb("under_big", [P, 5 * HALF])
        quarter = [big[:, 2 * N * k:2 * N * (k + 1)] for k in range(4)]
        with nc.sbuf_tensor("three", [P, 3 * N], F32) as three:
            pass
        w_hi = sb("w_hi", [P, 2, HALF], F32R)
        w_lo = sb("w_lo", [P, 2, HALF], F32R)
        x_lo = sb("x_lo", [P, N], F32R)
        ad_hid = three[:, :].rearrange("p (k n) -> p k n", k=3)
        with nc.sbuf_tensor("res0", [P, TILES, C], F32) as res0:
            pass
        x_hi = sb("x_hi", [P, N], F32R)
        bn_s = sb("bn_s", [P, TILES, 6])
        bn_m = sb("bn_m", [P, TILES, 2])
        std = sb("std", [P, TILES])
        rstd = sb("rstd", [P, TILES])
        c0 = sb("c0", [P, TILES, C])
        c0_ch = sb("c0_ch", [P, N])
        lg = sb("lg", [P, TILES, E0])
        eqm = sb("eqm", [P, TILES, E0])
        pick = sb("pick", [P, TILES])
        top1 = sb("top1", [P, TILES])
        top2 = sb("top2", [P, TILES])
        oh1 = sb("oh1", [P, TILES, E0])
        oh2 = sb("oh2", [P, TILES, E0])
        oh1_h = sb("oh1_h", [P, TILES * E0], BF16)
        oh2_h = sb("oh2_h", [P, TILES * E0], BF16)
        rest = sb("rest", [P, TILES, E0])
        ex = sb("ex", [P, TILES, E0])
        exsum = sb("exsum", [P, TILES])
        rsum = sb("rsum", [P, TILES])
        prob = sb("prob", [P, TILES, E0])
        posa = sb("posa", [P, TILES, E0])
        posb = sb("posb", [P, TILES, E0])
        comb = sb("comb", [P, TILES, 2, E0, CAP])
        comb_t = sb("comb_t", [P, TILES, P])
        slot_in = quarter[0].rearrange("p (e t i c) -> p e t i c", e=E0, t=TILES, i=BPT)
        silu0 = quarter[1][0:H0, :]
        hid0 = quarter[2][0:H0, :]
        disp = quarter[2].rearrange("p (t i e c) -> p t i e c", t=TILES, i=BPT, e=E0)
        place = quarter[1][:, 0:TILES * BPT * E0].rearrange("p (t i e) -> p t i e", t=TILES, i=BPT)
        prob_par = quarter[1][:, HALF:HALF + TILES * 2 * E0].rearrange("p (t a e) -> p t a e", t=TILES, a=2)
        slot_ch = quarter[3].rearrange("p (t i e c) -> p t i e c", t=TILES, i=BPT, e=E0)
        slot_out = sb("slot_out", [P, B // 2, C])

        ad_ready = sem("ad_ready")
        adhid_ready = sem("adhid_ready")
        adapt_ready = sem("adapt_ready")
        affine_ready = sem("affine_ready")
        var_ready = sem("var_ready")
        std_ready = sem("std_ready")
        c0_ready = sem("c0_ready")
        c0t_ready = sem("c0t_ready")
        c0ch_ready = sem("c0ch_ready")
        lg_ready = sem("lg_ready")
        choice_ready = sem("choice_ready")
        rank_ready = sem("rank_ready")
        rest_ready = sem("rest_ready")
        exp_ready = sem("exp_ready")
        disp_ready = sem("disp_ready")
        comb_ready = sem("comb_ready")
        gather_ready = sem("gather_ready")
        slotin_act = sem("slotin_act")
        slotin_dve = sem("slotin_dve")
        combt_ready = sem("combt_ready")
        combt_used = sem("combt_used")
        gatefc_ready = sem("gatefc_ready")
        silu_ready = sem("silu_ready")
        hid0_ready = sem("hid0_ready")
        proj_ready = sem("proj_ready")
        slotch_act = sem("slotch_act")
        slotch_dve = sem("slotch_dve")
        slott_ready = sem("slott_ready")
        slotout_act = sem("slotout_act")
        slotout_dve = sem("slotout_dve")
        y0_ready = sem("y0_ready")
        x1_ready = sem("x1_ready")

        attn = c0_ch[0:ADIM, :]
        score_d = sb("score_d", [P, TILES, S])
        soft = mask_tmp
        soft_e = sb("soft_e", [P, TILES, S])
        soft_wide = quarter[0][:, 0:N].rearrange("p (t i s) -> p t i s", t=TILES, i=BPT)
        soft_t = quarter[0][:, N:2 * N].rearrange("p (t q) -> p t q", t=TILES)
        rmax = sb("rmax", [P, TILES])
        rden = sb("rden", [P, TILES])
        rden_wide = sb("rden_wide", [P, TILES, BPT])
        pool_ch = sb("pool_ch", [P, N])

        x1t_ready = sem("x1t_ready")
        x1tok_ready = sem("x1tok_ready")
        attn_ready = sem("attn_ready")
        attn_done = sem("attn_done")
        score_ready = sem("score_ready")
        scored_ready = sem("scored_ready")
        spread_ready = sem("spread_ready")
        soft_ready = sem("soft_ready")
        softexp_ready = sem("softexp_ready")
        softt_ready = sem("softt_ready")
        pooled_ready = sem("pooled_ready")
        poolch_act = sem("poolch_act")
        poolch_dve = sem("poolch_dve")

        lrow = slot_out[:, 0:TILES, :].rearrange("p q c -> p (q c)")
        above_row = slot_out[:, TILES:2 * TILES, :].rearrange("p q c -> p (q c)")
        thr = sb("thr", [P, 1])
        best_thr = sb("best_thr", [P, 1])
        best_end = sb("best_end", [P, 1])
        hits = sb("hits", [P, 1])
        enough_h = sb("enough_h", [P, 1], BF16)
        thr_d = sb("thr_d", [E1, 2, E1])
        ltok = sb("ltok", [P, TILES, E1])
        sure = sb("sure", [P, TILES, E1])
        sure_h = sb("sure_h", [P, TILES, E1], BF16)
        tied = sb("tied", [P, TILES, E1])
        tied_h = sb("tied_h", [P, TILES * E1], BF16)
        room = sb("room", [P, E1])
        gate1 = sb("gate1", [P, TILES, E1])
        sig1 = sb("sig1", [P, TILES, E1])
        gate1_t = sb("gate1_t", [E1, N])
        hid = big[:, :].rearrange("p (a k n) -> p a k n", a=2, k=FCH1)

        lrow_ready = sem("lrow_ready")
        lrow_done = sem("lrow_done")
        ltok_ready = sem("ltok_ready")
        ltok_done = sem("ltok_done")
        enough_ready = sem("enough_ready")
        count_ready = sem("count_ready")
        thrd_ready = sem("thrd_ready")
        thrtok_ready = sem("thrtok_ready")
        tied_ready = sem("tied_ready")
        order_ready = sem("order_ready")
        sig1_ready = sem("sig1_ready")
        gate1_ready = sem("gate1_ready")
        gate1t_ready = sem("gate1t_ready")
        gate1t_done = sem("gate1t_done")
        w1_split = sem("w1_split")
        xhi_ready = sem("xhi_ready")
        xlo_ready = sem("xlo_ready")
        up1_ready = sem("up1_ready")
        hid1_ready = sem("hid1_ready")
        y1_ready = sem("y1_ready")
        y1_used = sem("y1_used")

        decay = sb("decay", [P, N])
        tau_e = sb("tau_e", [P, 2])
        alpha = sb("alpha", [P, 2])
        bl_max = sb("bl_max", [P, 1])
        bl = sb("bl", [P, 4 * D2])
        bl_e = sb("bl_e", [P, 4 * D2])
        bl_sum = sb("bl_sum", [P, 1])
        lag_f = sb("lag_f", [P, 2, C])
        lag_hi = sb("lag_hi", [P, C], F32R)
        lag_lo = sb("lag_lo", [P, C])
        lag_w = sb("lag_w", [P, S, C], F32R)
        ctx_ch = comb_t[:, :, :].rearrange("p t q -> p (t q)")
        soma = slot_out[:, 0:TILES, :].rearrange("p q c -> p (q c)")
        gated = slot_out[:, TILES:2 * TILES, :].rearrange("p q c -> p (q c)")
        net = lang_f_rows[0:HN2, :]
        mod = c0_ch
        prod = three[:, :].rearrange("p (k n) -> p k n", k=3)
        traces = pool_ch
        temporal = traces
        tgate = res0[:, :, :].rearrange("p t c -> p (t c)")
        ynorm = c0
        y_ch = c0_ch
        low_hi = x_hi
        low_w = x_lo
        low2 = lang_f_rows

        taue_ready = sem("taue_ready")
        blend_ready = sem("blend_ready")
        blexp_ready = sem("blexp_ready")
        blw_ready = sem("blw_ready")
        blt_ready = sem("blt_ready")
        lag0_ready = sem("lag0_ready")
        alpha_ready = sem("alpha_ready")
        lagw_ready = sem("lagw_ready")
        decay_ready = sem("decay_ready")
        x2t_ready = sem("x2t_ready")
        x2ch_ready = sem("x2ch_ready")
        ctx_ready = sem("ctx_ready")
        soma_pre = sem("soma_pre")
        soma_ready = sem("soma_ready")
        net_pre = sem("net_pre")
        net_ready = sem("net_ready")
        wg_pre = sem("wg_pre")
        wg_ready = sem("wg_ready")
        mod_pre = sem("mod_pre")
        mod_sig = sem("mod_sig")
        mod_ready = sem("mod_ready")
        lag_ready = sem("lag_ready")
        prod_ready = sem("prod_ready")
        summed = sem("summed")
        temporal_ready = sem("temporal_ready")
        tg_pre = sem("tg_pre")
        tg_ready = sem("tg_ready")
        sg_ready = sem("sg_ready")
        out2_ready = sem("out2_ready")
        ynorm_ready = sem("ynorm_ready")
        yt_ready = sem("yt_ready")
        ych_ready = sem("ych_ready")
        low_pre = sem("low_pre")
        low_ready = sem("low_ready")
        ff2_pre = sem("ff2_pre")
        ff2_ready = sem("ff2_ready")
        low2_pre = sem("low2_pre")
        low2_ready = sem("low2_ready")
        y2_ready = sem("y2_ready")
        x3_ready = sem("x3_ready")

        subj_bias = sb("subj_bias", [P, B])
        z_ch = decay
        gate3 = sb("gate3", [P, TILES, E3])
        gate3_t = gate1_t
        silu3 = hid[:, 1, 0, :].rearrange("p (k n) -> p k n", k=2)

        z_ready = sem("z_ready")
        zch_ready = sem("zch_ready")
        x3t_ready = sem("x3t_ready")
        x3tok_ready = sem("x3tok_ready")
        lg3_ready = sem("lg3_ready")
        lg3_used = sem("lg3_used")
        rest3_ready = sem("rest3_ready")
        exp3_ready = sem("exp3_ready")
        gate3_ready = sem("gate3_ready")
        gate3t_ready = sem("gate3t_ready")
        gate3t_done = sem("gate3t_done")
        w3_split = sem("w3_split")
        zhi_ready = sem("zhi_ready")
        zlo_ready = sem("zlo_ready")
        g3_ready = sem("g3_ready")
        silu3_ready = sem("silu3_ready")
        u3_ready = sem("u3_ready")
        hid3_ready = sem("hid3_ready")
        y3_ready = sem("y3_ready")
        y3_used = sem("y3_used")

        dve_step = sem("dve_step")
        act_step = sem("act_step")
        stored = sem("stored")

        block = ctx.enter_context(nc.Block())

        @block.sync
        def _(sp):
            sp.dma_start(ids_i[:, :], dram["ids"]).then_inc(loaded["ids"], 16)
            for name in ("early", "l0_w1"):
                sp.dma_start(packs[name][:, :], dram[name]).then_inc(loaded[name], 16)
            sp.dma_start(x_ch[:, 0:HALF], dram["x_ch"][:, 0:HALF]).then_inc(loaded["x_ch"], 16)
            sp.dma_start(x_ch[:, HALF:N], dram["x_ch"][:, HALF:N]).then_inc(loaded["x_ch2"], 16)
            sp.dma_start(packs["l0_small"][:, :], dram["l0_small"]).then_inc(loaded["l0_small"], 16)
            sp.dma_start(x_tok[:, :, :], dram["x"].rearrange("(t p) c -> p t c", p=P)).then_inc(loaded["x_tok"], 16)
            sp.dma_start(packs["consts"][:, :], dram["consts"]).then_inc(loaded["consts"], 16)
            sp.dma_start(types_i[:, :], dram["types"]).then_inc(loaded["types"], 16)
            for name in ("l2_decay", "l0_gatefc", "l0_proj", "l1_small"):
                sp.dma_start(packs[name][:, :], dram[name]).then_inc(loaded[name], 16)
            for name in ("l1_w1", "l1_w2", "l2_all", "l3_small", "l3_down", "l3_gate", "l3_up"):
                if name == "l3_gate":
                    sp.wait_ge(proj_ready, 4)
                sp.dma_start(packs[name][:, :], dram[name]).then_inc(loaded[name], 16)
            sp.wait_ge(loaded["ids"], 16)
            sp.wait_ge(up1_ready, E1 * FCH1 * HALVES)
            for b in range(B):
                subject = sp.value_load(ids_i[0:1, 2 * B + b:2 * B + b + 1], min_val=0, max_val=SUBJ - 1)
                sp.dma_start(subj_w[:, b, :], dram["subj_w"][bass.ds(subject, 1), :, :].rearrange("a h o -> (a h) o")
                             ).then_inc(subj_loaded, 16)
            out_v = out.rearrange("b s c -> (b s) c").rearrange("(t p) c -> p t c", p=P)
            for h in range(HALVES):
                sp.wait_ge(y3_used, 2 * E3 + h + 1)
                sp.dma_start(out_v[:, 4 * h:4 * h + 4, :], x_tok[:, 4 * h:4 * h + 4, :]).then_inc(stored, 16)
            sp.wait_ge(stored, 32)

        @block.gpsimd
        def _(pool):
            steps = [0]

            def chain(ins):
                steps[0] += 1
                ins.then_inc(pool_step, 1)
                pool.wait_ge(pool_step, steps[0])

            pool.wait_ge(loaded["early"], 16)
            nc.gpsimd.tensor_copy(far_h[:, :], field("early", "far")[0:LANGS, :]).then_inc(far_ready, 1)
            nc.gpsimd.memset(ones_h[:, :], 1.0)
            nc.gpsimd.memset(ones_f[:, :], 1.0)
            pool.wait_ge(lang_ready, 1)
            nc.gpsimd.tensor_copy(lang_f[:, :].rearrange("l (b s) -> l b s", s=S), bc(lang_b[:, :], 2, S)
                                  ).then_inc(langf_ready, 1)
            pool.wait_ge(loaded["consts"], 16)
            pool.wait_ge(loaded["types"], 16)
            for dst, name in ((tri_batch_h, "tri_batch"), (ones_batch_h, "ones_batch"), (tri_all_h, "tri_all"),
                              (same_expert_h, "same_expert")):
                nc.gpsimd.tensor_copy(dst[:, :], field("consts", name))
            nc.gpsimd.tensor_scalar(subj_b[:, :], ids_f[0:SUBJ, 2 * B:3 * B], pidx[0:SUBJ, :], None, ALU.is_equal)
            chain(nc.gpsimd.tensor_copy(types_f[:, :], types_i[:, :]))
            chain(nc.gpsimd.tensor_scalar(type_sel[:, 0, :], types_f[:, :], 0.0, None, ALU.is_equal))
            chain(nc.gpsimd.tensor_scalar(type_sel[:, 1, :], types_f[:, :], 1.0, None, ALU.is_equal))
            chain(nc.gpsimd.tensor_tensor(type_sel[:, 2, :], type_sel[:, 0, :], type_sel[:, 1, :], ALU.add))
            chain(nc.gpsimd.tensor_scalar(type_sel[:, 2, :], type_sel[:, 2, :], -1.0, 1.0, ALU.mult, ALU.add))
            for k, name in enumerate(("mask_pre", "mask_post", "mask_cloze")):
                sel = bc(type_sel[:, k, :], 2, S)
                mask = bc(field("consts", name), 1, TILES)
                count = field("consts", "counts")[:, k:k + 1]
                if k == 0:
                    nc.gpsimd.tensor_tensor(mask_add[:, :, :], mask, sel, ALU.mult)
                    chain(nc.gpsimd.tensor_scalar(seen[:, :], type_sel[:, k, :], count, None, ALU.mult))
                    continue
                nc.gpsimd.tensor_tensor(mask_tmp[:, :, :], mask, sel, ALU.mult)
                chain(nc.gpsimd.tensor_scalar(seen_tmp[:, :], type_sel[:, k, :], count, None, ALU.mult))
                nc.gpsimd.tensor_tensor(mask_add[:, :, :], mask_add[:, :, :], mask_tmp[:, :, :], ALU.add)
                chain(nc.gpsimd.tensor_tensor(seen[:, :], seen[:, :], seen_tmp[:, :], ALU.add))
            nc.gpsimd.memset(mask_tmp[:, :, :], 0.0).then_inc(consts_ready, 1)
            chain(nc.gpsimd.memset(decay[:, :], 1.0))
            chain(nc.gpsimd.memset(decay[:, :].rearrange("p (b s) -> p b s", s=S)[:, :, 0:1], 0.0))
            pool.wait_ge(alpha_ready, 1)
            nc.gpsimd.tensor_scalar(decay[:, :], decay[:, :], alpha[:, 1:2], None, ALU.mult).then_inc(decay_ready, 1)

            def split(buf, at, weights):
                n = weights.shape[-1]
                chain(nc.gpsimd.tensor_copy(w_hi[:, buf, at:at + n], weights))
                return nc.gpsimd.tensor_tensor(w_lo[:, buf, at:at + n], weights,
                                               w_hi[:, buf, at:at + n].bitcast(F32), ALU.subtract)

            def split1(e):
                if e == 0:
                    pool.wait_ge(loaded["l1_w1"], 16)
                    pool.wait_ge(adapt_ready, 2)
                if e >= 2:
                    pool.wait_ge(up1_ready, (e - 1) * FCH1 * HALVES)
                split(e % 2, 0, field("l1_w1", "w1")[:, e * FF1:(e + 1) * FF1]).then_inc(w1_split, 1)

            split1(0)
            split1(1)
            pool.wait_ge(lag0_ready, 1)
            for lag in range(S):
                if lag % 5 == 4 and lag // 5 + 2 < E1:
                    split1(lag // 5 + 2)
                now = lag_f[:, lag % 2, :]
                if lag + 1 < S:
                    nc.gpsimd.tensor_scalar(lag_f[:, (lag + 1) % 2, :], now, alpha[:, 0:1], None, ALU.mult)
                chain(nc.gpsimd.tensor_copy(lag_hi[:, :], now))
                chain(nc.gpsimd.tensor_scalar(lag_lo[:, :], lag_hi[:, :].bitcast(F32), field("consts", "lo_w"), None,
                                              ALU.mult))
                last = nc.gpsimd.tensor_tensor(lag_w[:, lag, :], lag_lo[:, :], now, ALU.subtract)
                if lag + 1 < S:
                    chain(last)
            last.then_inc(lagw_ready, 1)
            pool.wait_ge(loaded["l2_all"], 16)
            pool.wait_ge(y1_ready, 2 * E1)
            for k in range(FCH2):
                part = field("l2_all", "v1")[:, k * P:(k + 1) * P]
                pool.wait_ge(lagw_ready, k + 1)
                chain(nc.gpsimd.tensor_copy(lag_hi[:, :], part))
                chain(nc.gpsimd.tensor_scalar(lag_lo[:, :], lag_hi[:, :].bitcast(F32), field("consts", "lo_w"), None,
                                              ALU.mult))
                nc.gpsimd.tensor_tensor(v1_w[:, k * P:(k + 1) * P], lag_lo[:, :], part, ALU.subtract
                                        ).then_inc(lagw_ready, 1)
            for lag in range(2, S):
                if lag in VECTOR_LAGS:
                    continue
                n = (S - lag) * B
                turn = POOL_LAGS.index(lag)
                pool.wait_ge(prod_ready, lag + 1)
                if turn > 1:
                    pool.wait_ge(summed, turn - 1)
                nc.gpsimd.tensor_tensor(traces[:, lag * B:N], traces[:, lag * B:N], prod[:, turn % 3, 0:n], ALU.add
                                        ).then_inc(summed, 1)
            pool.wait_ge(summed, len(POOL_LAGS) - 1)
            pool.wait_ge(loaded["l3_gate"], 16)
            pool.wait_ge(loaded["l3_up"], 16)
            for e in range(E3):
                if e >= 2:
                    pool.wait_ge(u3_ready, (e - 1) * FCH3 * HALVES)
                split(e % 2, 0, field("l3_gate", "gate")[:, e * FF3:(e + 1) * FF3])
                split(e % 2, FF3, field("l3_up", "up")[:, e * FF3:(e + 1) * FF3]).then_inc(w3_split, 1)

        @block.tensor
        def _(pe):
            mm, tr = nc.tensor.matmul, nc.tensor.transpose

            def mm_split(dst, buf, at, cols):
                w = slice(at, at + P)
                mm(dst, w_hi[:, buf, w], x_hi[:, cols], start=True, stop=False)
                mm(dst, w_hi[:, buf, w], x_lo[:, cols], start=False, stop=False)
                return mm(dst, w_lo[:, buf, w], x_hi[:, cols], start=False, stop=True)

            pe.wait_ge(loaded["l0_w1"], 16)
            pe.wait_ge(far_ready, 1)
            w1, w2 = field("l0_w1", "w1"), field("l0_small", "w2")
            table = field("l0_small", "table")
            for h in range(HALVES):
                cols = slice(h * HALF, (h + 1) * HALF)
                pe.wait_ge(loaded[("x_ch", "x_ch2")[h]], 16)
                for k, rows in enumerate(LCH):
                    dst = psum[0:rows, 3 * h + k, :]
                    mm(dst, w1[:, k * P:k * P + rows], x_ch[:, cols], start=True, stop=False)
                    if h == 0 and k == 0:
                        pe.wait_ge(lang_ready, 2)
                    mm(dst, far_h[:, k * P:k * P + rows], lang_h[:, cols], start=False, stop=True).then_inc(ad_ready, 1)
            pe.wait_ge(loaded["l0_small"], 16)
            pe.wait_ge(langf_ready, 1)
            for h in range(HALVES):
                pe.wait_ge(adhid_ready, 3 * (h + 1))
                for t in range(4 * h, 4 * h + 4):
                    dst = psum[:, 6 + h, (t % 4) * C:(t % 4 + 1) * C]
                    tok = slice(t * P, (t + 1) * P)
                    for k, rows in enumerate(LCH):
                        mm(dst, ad_hid[0:rows, k, tok], w2[0:rows, k * C:(k + 1) * C], start=(k == 0), stop=False)
                    last = mm(dst, lang_f[:, tok], table[0:LANGS, 0:C], start=False, stop=True)
                last.then_inc(adapt_ready, 1)
            for t in range(TILES):
                last = mm(psum[:, t // 2, (t % 2) * 2 * C:(t % 2 + 1) * 2 * C], lang_f[:, t * P:(t + 1) * P],
                          table[0:LANGS, C:3 * C], start=True, stop=True)
            last.then_inc(affine_ready, 1)
            pe.wait_ge(loaded["consts"], 16)
            for h in range(HALVES):
                pe.wait_ge(c0_ready, h + 1)
                for t in range(4 * h, 4 * h + 4):
                    last = tr(psum[:, 4 + h, (t % 4) * P:(t % 4 + 1) * P], c0[:, t, :], ident)
                last.then_inc(c0t_ready, 1)
            for t in range(TILES):
                if t % 4 == 0:
                    pe.wait_ge(c0ch_ready, t // 4 + 1)
                last = mm(psum[:, 6, t * E0:(t + 1) * E0], c0_ch[:, t * P:(t + 1) * P], field("l0_small", "router"),
                          start=True, stop=True)
            last.then_inc(lg_ready, 1)
            pe.wait_ge(consts_ready, 1)
            pe.wait_ge(choice_ready, 2)
            mm(psum[:, 7, 0:P], tri_batch_h[:, :], oh1_h[:, :], start=True, stop=True)
            mm(psum[:, 7, P:2 * P], ones_batch_h[:, :], oh1_h[:, :], start=True, stop=False)
            mm(psum[:, 7, P:2 * P], tri_batch_h[:, :], oh2_h[:, :], start=False, stop=True).then_inc(rank_ready, 1)
            pe.wait_ge(disp_ready, 1)
            for t in range(TILES):
                last = mm(psum[:, t // 2, (t % 2) * BPT * SLOTS:(t % 2 + 1) * BPT * SLOTS], c0[:, t, :],
                          disp[:, t, :, :, :].rearrange("p i e c -> p (i e c)"), start=True, stop=True)
                if t % 2 == 1:
                    last.then_inc(gather_ready, 1)
            pe.wait_ge(comb_ready, 1)
            for t in range(TILES):
                last = tr(psum[:, 4 + t // 4, (t % 4) * P:(t % 4 + 1) * P],
                          comb[:, t, :, :, :].rearrange("p a e c -> p (a e c)"), ident)
                if t % 4 == 3:
                    last.then_inc(combt_ready, 1)
            pe.wait_ge(loaded["l0_gatefc"], 16)
            pe.wait_ge(slotin_act, 2)
            pe.wait_ge(slotin_dve, 2)
            for e in range(E0):
                bank = (6, 7, 4, 5)[e // 4]
                if e == 8:
                    pe.wait_ge(combt_used, 2)
                last = mm(psum[:, bank, (e % 4) * P:(e % 4 + 1) * P],
                          field("l0_gatefc", "gatefc")[:, e * P:(e + 1) * P],
                          slot_in[:, e, :, :, :].rearrange("p t i c -> p (t i c)"), start=True, stop=True)
                if e % 4 == 3:
                    last.then_inc(gatefc_ready, 1)
            pe.wait_ge(loaded["l0_proj"], 16)
            for e in range(E0):
                if e % 4 == 0:
                    pe.wait_ge(hid0_ready, e // 4 + 1)
                last = mm(psum[:, e // 4, (e % 4) * P:(e % 4 + 1) * P],
                          field("l0_proj", "proj")[0:H0, e * C:(e + 1) * C], hid0[:, e * P:(e + 1) * P],
                          start=True, stop=True)
                if e % 4 == 3:
                    last.then_inc(proj_ready, 1)
            pe.wait_ge(slotch_act, 2)
            pe.wait_ge(slotch_dve, 2)
            pairs = slot_ch[:, :, :, :, :].rearrange("p t (j a) e c -> p (t j) (a e c)", a=2)
            for q in range(B // 2):
                last = tr(psum[:, 4 + q // 4, (q % 4) * P:(q % 4 + 1) * P], pairs[:, q, :], ident)
                if q % 4 == 3:
                    last.then_inc(slott_ready, 1)
            pe.wait_ge(slotout_act, 2)
            pe.wait_ge(slotout_dve, 2)
            for q in range(B // 2):
                last = mm(psum[:, q // 8, (q % 8) * 2 * S:(q % 8 + 1) * 2 * S], slot_out[:, q, :],
                          comb_t[:, q // 2, (q % 2) * 2 * S:(q % 2 + 1) * 2 * S], start=True, stop=True)
                if q % 8 == 7:
                    last.then_inc(y0_ready, 1)

            pe.wait_ge(blw_ready, 1)
            tr(psum[:, 7, 0:C], bl[:, :], ident).then_inc(blt_ready, 1)

            for t in range(TILES):
                if t % 4 == 0:
                    pe.wait_ge(x1_ready, t // 4 + 1)
                last = tr(psum[:, 2 + t // 4, (t % 4) * C:(t % 4 + 1) * C], x_ch[:, t * P:(t + 1) * P], ident)
                if t % 4 == 3:
                    last.then_inc(x1t_ready, 1)
            pe.wait_ge(loaded["l1_small"], 16)
            for h in range(HALVES):
                mm(psum[0:ADIM, 4 + h, :], field("l1_small", "w1c"), x_ch[:, h * HALF:(h + 1) * HALF],
                   start=True, stop=True).then_inc(attn_ready, 1)
            for t in range(TILES):
                if t % 4 == 0:
                    pe.wait_ge(attn_done, t // 4 + 1)
                last = mm(psum[:, 6, t:t + 1], attn[:, t * P:(t + 1) * P], field("l1_small", "v")[0:ADIM, :],
                          start=True, stop=True)
            last.then_inc(score_ready, 1)
            pe.wait_ge(scored_ready, 1)
            pe.wait_ge(lag0_ready, 1)
            mm(psum[:, 7, 0:TILES * S], field("consts", "ones_batch"), score_d[:, :, :].rearrange("p t s -> p (t s)"),
               start=True, stop=True).then_inc(spread_ready, 1)
            pe.wait_ge(softt_ready, 1)
            pe.wait_ge(x1tok_ready, 2)
            for t in range(TILES):
                last = mm(psum[:, t // 4, (t % 4) * P:(t % 4 + 1) * P], x_tok[:, t, :], soft_t[:, t, :],
                          start=True, stop=True)
                if t % 4 == 3:
                    last.then_inc(pooled_ready, 1)

            for h in range(HALVES):
                pe.wait_ge((poolch_act, poolch_dve)[h], 1)
                mm(psum[:, 4 + h, :], field("l1_small", "router"), pool_ch[:, h * HALF:(h + 1) * HALF],
                   start=True, stop=True).then_inc(lrow_ready, 1)

            units = [(e, k, h) for e in range(E1) for k in range(FCH1) for h in range(HALVES)]
            UNITS = FCH1 * HALVES

            def up1(u):
                e, k, h = units[u]
                if u >= 3:
                    pe.wait_ge(hid1_ready, u - 2)
                if k == 0 and h == 0:
                    pe.wait_ge(w1_split, e + 1)
                mm_split(psum[:, u % 3, :], e % 2, k * P, slice(h * HALF, (h + 1) * HALF)).then_inc(up1_ready, 1)

            def down1(e, h, pair):
                if pair == 0:
                    pe.wait_ge(hid1_ready, (e + 1) * UNITS - 1 + h)
                    if e >= 1:
                        pe.wait_ge(y1_used, 2 * (e - 1) + h + 1)
                for t in range(4 * h + 2 * pair, 4 * h + 2 * pair + 2):
                    for k in range(FCH1):
                        at = (e * FCH1 + k) * C
                        last = mm(psum[:, 3 + h, (t % 4) * C:(t % 4 + 1) * C], hid[:, e % 2, k, t * P:(t + 1) * P],
                                  field("l1_w2", "w2")[:, at:at + C], start=(k == 0), stop=(k == FCH1 - 1))
                if pair == 1:
                    last.then_inc(y1_ready, 1)

            pe.wait_ge(xhi_ready, 2)
            pe.wait_ge(xlo_ready, 2)
            up1(0)
            pe.wait_ge(lrow_done, 2)
            for t in range(TILES):
                last = tr(psum[:, 6, t * E1:(t + 1) * E1], lrow[0:E1, t * P:(t + 1) * P], ident[0:E1, 0:E1])
            last.then_inc(ltok_ready, 1)
            up1(1)
            pe.wait_ge(ltok_done, 1)
            for r in range(ROUNDS):
                pe.wait_ge(enough_ready, r + 1)
                mm(psum[:, 6, 0:1], same_expert_h[:, :], enough_h[:, :], start=True, stop=True).then_inc(count_ready, 1)
                if r < 4:
                    for u in range(3 * r + 2, 3 * r + 5):
                        up1(u)
                elif r == 4:
                    up1(14)
                    up1(15)
                    pe.wait_ge(loaded["l1_w2"], 16)
                else:
                    down1(0, (r - 5) // 2, (r - 5) % 2)
            pe.wait_ge(thrd_ready, 1)
            mm(psum[:, 6, 0:2 * E1], ones_f[0:E1, :], thr_d[:, :, :].rearrange("p a e -> p (a e)"), start=True,
               stop=True).then_inc(thrtok_ready, 1)
            down1(0, 1, 1)
            pe.wait_ge(tied_ready, 1)
            mm(psum[:, 7, 0:TILES * E1], tri_all_h[:, :], tied_h[:, :], start=True, stop=False)
            for t in range(TILES - 1):
                left = TILES - 1 - t
                mm(psum[:, 7, (t + 1) * E1:TILES * E1].rearrange("p (a e) -> p a e", e=E1), ones_h[:, :],
                   bc(tied_h[:, t * E1:(t + 1) * E1], 1, left), start=False, stop=(t == TILES - 2))
            for t in range(TILES):
                last = mm(psum[:, 7, HALF - E1:HALF], ones_h[:, :], sure_h[:, t, :], start=(t == 0),
                          stop=(t == TILES - 1))
            last.then_inc(order_ready, 1)
            for e in range(1, E1):
                if e >= 2:
                    for u in range(e * UNITS, (e + 1) * UNITS):
                        up1(u)
                if e == 2:
                    pe.wait_ge(gate1_ready, 1)
                    for t in range(TILES):
                        last = tr(psum[0:E1, (5, 7)[t // 4], (t % 4) * P:(t % 4 + 1) * P], gate1[:, t, :], ident)
                        if t % 4 == 3:
                            last.then_inc(gate1t_ready, 1)
                if e >= 2:
                    for h in range(HALVES):
                        down1(e - 1, h, 0)
                        down1(e - 1, h, 1)
            for h in range(HALVES):
                down1(E1 - 1, h, 0)
                down1(E1 - 1, h, 1)
            pe.wait_ge(gate1t_done, 2)
            for h in range(HALVES):
                pe.wait_ge(y1_used, 2 * (E1 - 1) + h + 1)
                for t in range(4 * h, 4 * h + 4):
                    last = mm(psum[:, 3 + h, (t % 4) * C:(t % 4 + 1) * C], gate1_t[:, t * P:(t + 1) * P],
                              field("l1_small", "b2")[0:E1, :], start=True, stop=True)
                last.then_inc(y1_ready, 1)

            for h in range(HALVES):
                pe.wait_ge(y1_used, 2 * E1 + h + 1)
                for t in range(4 * h, 4 * h + 4):
                    last = tr(psum[:, h, (t % 4) * P:(t % 4 + 1) * P], x_tok[:, t, :], ident)
                last.then_inc(x2t_ready, 1)
            pe.wait_ge(loaded["l2_all"], 16)
            l2 = lambda name: field("l2_all", name)
            halves = [slice(h * HALF, (h + 1) * HALF) for h in range(HALVES)]
            for h, cols in enumerate(halves):
                pe.wait_ge(x2ch_ready, h + 1)
                mm(psum[:, 2 + h, :], l2("wsoma"), x_ch[:, cols], start=True, stop=True).then_inc(soma_pre, 1)
                mm(psum[0:HN2, 4 + h, :], l2("wn1"), x_ch[:, cols], start=True, stop=True).then_inc(net_pre, 1)
            pe.wait_ge(ctx_ready, 1)
            for h, cols in enumerate(halves):
                mm(psum[:, h, :], l2("wg_x"), x_ch[:, cols], start=True, stop=False)
                mm(psum[:, h, :], l2("wg_ctx"), ctx_ch[:, cols], start=False, stop=True).then_inc(wg_pre, 1)
            for h, cols in enumerate(halves):
                pe.wait_ge(net_ready, h + 1)
                mm(psum[:, 6 + h, :], l2("wn2")[0:HN2, :], net[:, cols], start=True, stop=True).then_inc(mod_pre, 1)
            pe.wait_ge(mod_ready, 2)
            pe.wait_ge(wg_ready, 2)
            pe.wait_ge(soma_ready, 2)
            pe.wait_ge(lagw_ready, 1)
            for lag in range(S):
                n = (S - lag) * B
                if lag >= 4:
                    pe.wait_ge(prod_ready, lag - 3)
                for at in range(0, n, HALF):
                    end = min(n, at + HALF)
                    last = mm(psum[:, 2 * (lag % 4) + at // HALF, 0:end - at], lag_w[:, lag, :], mod_w[:, at:end],
                              start=True, stop=True)
                last.then_inc(lag_ready, 1)
            for h, cols in enumerate(halves):
                pe.wait_ge(temporal_ready, h + 1)
                mm(psum[:, h, :], l2("wtemp"), temporal[:, cols], start=True, stop=True).then_inc(tg_pre, 1)
            for h in range(HALVES):
                pe.wait_ge(sg_ready, h + 1)
                for t in range(4 * h, 4 * h + 4):
                    last = mm(psum[:, 2 + h, (t % 4) * C:(t % 4 + 1) * C], soma[:, t * P:(t + 1) * P], l2("wout"),
                              start=True, stop=True)
                last.then_inc(out2_ready, 1)
            for h in range(HALVES):
                pe.wait_ge(ynorm_ready, h + 1)
                for t in range(4 * h, 4 * h + 4):
                    last = tr(psum[:, 4 + h, (t % 4) * P:(t % 4 + 1) * P], ynorm[:, t, :], ident)
                last.then_inc(yt_ready, 1)
            for h, cols in enumerate(halves):
                pe.wait_ge(ych_ready, h + 1)
                mm(psum[:, 6 + h, :], l2("u1"), y_ch[:, cols], start=True, stop=True).then_inc(low_pre, 1)
            pe.wait_ge(lagw_ready, 1 + FCH2)
            for u in range(HALVES * FCH2):
                h, k = u // FCH2, u % FCH2
                if u % FCH2 == 0:
                    pe.wait_ge(low_ready, h + 1)
                if u >= 4:
                    pe.wait_ge(ff2_ready, u - 3)
                mm(psum[:, u % 4, :], v1_w[:, k * P:(k + 1) * P], low_w[:, halves[h]], start=True, stop=True
                   ).then_inc(ff2_pre, 1)
            for h, cols in enumerate(halves):
                for k in range(FCH2):
                    pe.wait_ge(ff2_ready, h * FCH2 + k + 1)
                    last = mm(psum[k * RK2:(k + 1) * RK2, 4 + h, :], l2("u2")[:, k * RK2:(k + 1) * RK2],
                              hid[:, 0, k, cols], start=True, stop=True, tile_position=(0, k * RK2))
                last.then_inc(low2_pre, 1)
            for h, cols in enumerate(halves):
                pe.wait_ge(low2_ready, h + 1)
                mm(psum[:, 6 + h, :], l2("v2"), low2[:, cols], start=True, stop=True).then_inc(y2_ready, 1)

            pe.wait_ge(subj_loaded, 16 * B)
            pe.wait_ge(loaded["l3_small"], 16)
            mm(psum[:, 2, 0:B], field("l3_small", "cbias")[0:SUBJ, :], subj_b[:, :], start=True, stop=True)
            for b in range(B):
                if b % 16 == 0:
                    pe.wait_ge(x3_ready, b // 16 + 1)
                last = mm(psum[:, b // 16, (b % 16) * S:(b % 16 + 1) * S], subj_w[:, b, :], x_ch[:, b * S:(b + 1) * S],
                          start=True, stop=True)
                if b % 16 == 15:
                    last.then_inc(z_ready, 1)
            for h in range(HALVES):
                for t in range(4 * h, 4 * h + 4):
                    last = tr(psum[:, 6 + h, (t % 4) * P:(t % 4 + 1) * P], x_ch[:, t * P:(t + 1) * P], ident)
                last.then_inc(x3t_ready, 1)
            for t in range(TILES):
                if t % 4 == 0:
                    pe.wait_ge(zch_ready, t // 4 + 1)
                last = mm(psum[:, 3, t * E3:(t + 1) * E3], z_ch[:, t * P:(t + 1) * P], field("l3_small", "router"),
                          start=True, stop=True)
            last.then_inc(lg3_ready, 1)
            pe.wait_ge(loaded["l3_down"], 16)
            pe.wait_ge(zhi_ready, 2)
            pe.wait_ge(zlo_ready, 2)

            units3 = [(e, k, h) for e in range(E3) for k in range(FCH3) for h in range(HALVES)]
            UNITS3 = FCH3 * HALVES

            def up3(u):
                e, k, h = units3[u]
                if k == 0 and h == 0:
                    pe.wait_ge(w3_split, e + 1)
                if u == 1:
                    pe.wait_ge(lg3_used, 1)
                if u >= 2:
                    pe.wait_ge(silu3_ready, u - 1)
                mm_split(psum[:, u % 2, :], e % 2, k * P, halves[h]).then_inc(g3_ready, 1)
                if u >= 2:
                    pe.wait_ge(hid3_ready, u - 1)
                mm_split(psum[:, 2 + u % 2, :], e % 2, FF3 + k * P, halves[h]).then_inc(u3_ready, 1)

            def down3(e, h):
                pe.wait_ge(hid3_ready, (e + 1) * UNITS3 - 1 + h)
                if e >= 1:
                    pe.wait_ge(y3_used, 2 * (e - 1) + h + 1)
                for t in range(4 * h, 4 * h + 4):
                    for k in range(FCH3):
                        at = (e * FCH3 + k) * C
                        last = mm(psum[:, 4 + h, (t % 4) * C:(t % 4 + 1) * C], hid[:, 0, (e % 2) * 2 + k, t * P:(t + 1) * P],
                                  field("l3_down", "down")[:, at:at + C], start=(k == 0), stop=(k == FCH3 - 1))
                last.then_inc(y3_ready, 1)

            for e in range(E3):
                for u in range(e * UNITS3, (e + 1) * UNITS3):
                    up3(u)
                if e == 1:
                    pe.wait_ge(gate3_ready, 1)
                    for t in range(TILES):
                        last = tr(psum[0:E3, 6 + t // 4, (t % 4) * P:(t % 4 + 1) * P], gate3[:, t, :], ident)
                        if t % 4 == 3:
                            last.then_inc(gate3t_ready, 1)
                if e >= 1:
                    down3(e - 1, 0)
                    down3(e - 1, 1)
            down3(E3 - 1, 0)
            down3(E3 - 1, 1)
            pe.wait_ge(gate3t_done, 2)
            for h in range(HALVES):
                pe.wait_ge(y3_used, 2 * (E3 - 1) + h + 1)
                for t in range(4 * h, 4 * h + 4):
                    last = mm(psum[:, 4 + h, (t % 4) * C:(t % 4 + 1) * C], gate3_t[:, t * P:(t + 1) * P],
                              field("l3_small", "down_b")[0:E3, :], start=True, stop=True)
                last.then_inc(y3_ready, 1)

        @block.scalar
        def _(act):
            act.wait_ge(loaded["l2_decay"], 16)
            nc.scalar.activation(tau_e[:, 0:1], field("l2_decay", "taus"), ACT.Exp)
            nc.scalar.activation(tau_e[:, 1:2], field("l2_decay", "tau_ctx"), ACT.Exp).then_inc(taue_ready, 1)
            act.wait_ge(blend_ready, 1)
            nc.scalar.activation(bl_e[:, :], bl[:, :], ACT.Exp).then_inc(blexp_ready, 1)
            for h in range(HALVES):
                for k, rows in enumerate(LCH):
                    act.wait_ge(ad_ready, 3 * h + k + 1)
                    nc.scalar.activation(ad_hid[0:rows, k, h * HALF:(h + 1) * HALF], psum[0:rows, 3 * h + k, :],
                                         ACT.Relu, bias=field("l0_w1", "b1")[0:rows, k:k + 1]
                                         ).then_inc(adhid_ready, 1)
            act.wait_ge(var_ready, 1)
            nc.scalar.activation(std[:, :], bn_m[:, :, 1], ACT.Sqrt, bias=field("early", "eps")).then_inc(std_ready, 1)
            for h in range(HALVES):
                act.wait_ge(c0t_ready, h + 1)
                nc.scalar.activation(c0_ch[:, h * HALF:(h + 1) * HALF], psum[:, 4 + h, :], ACT.Copy
                                     ).then_inc(c0ch_ready, 1)
            act.wait_ge(rest_ready, 1)
            nc.scalar.activation(ex[:, :, :], rest[:, :, :], ACT.Exp).then_inc(exp_ready, 1)
            for g in (0, 1):
                act.wait_ge(gather_ready, g + 1)
                nc.scalar.activation(slot_in[:, :, 2 * g:2 * g + 2, :, :].rearrange("p e t i c -> p e (t i) c"),
                                     psum[:, g, :].rearrange("p (b e c) -> p e b c", e=E0, c=CAP), ACT.Copy
                                     ).then_inc(slotin_act, 1)
            for h in range(HALVES):
                act.wait_ge(combt_ready, h + 1)
                nc.scalar.activation(comb_t[:, 4 * h:4 * h + 4, :],
                                     psum[:, 4 + h, :].rearrange("p (t q) -> p t q", q=P), ACT.Copy
                                     ).then_inc(combt_used, 1)
            for g in range(4):
                act.wait_ge(gatefc_ready, g + 1)
                nc.scalar.activation(silu0[:, g * HALF:(g + 1) * HALF], psum[0:H0, (6, 7, 4, 5)[g], :], ACT.Silu
                                     ).then_inc(silu_ready, 1)
            for g in (0, 1):
                act.wait_ge(proj_ready, g + 1)
                nc.scalar.activation(slot_ch[:, :, :, 4 * g:4 * g + 4, :].rearrange("p t i e c -> p (t i) e c"),
                                     psum[:, g, :].rearrange("p (e b c) -> p b e c", e=4, c=CAP), ACT.Copy
                                     ).then_inc(slotch_act, 1)
            for g in (0, 1):
                act.wait_ge(slott_ready, g + 1)
                nc.scalar.activation(slot_out[:, 4 * g:4 * g + 4, :],
                                     psum[:, 4 + g, :].rearrange("p (q c) -> p q c", c=C), ACT.Copy
                                     ).then_inc(slotout_act, 1)
            act.wait_ge(blt_ready, 1)
            nc.scalar.activation(lag_f[:, 0, :], psum[:, 7, 0:C], ACT.Copy).then_inc(lag0_ready, 1)

            halves = [slice(h * HALF, (h + 1) * HALF) for h in range(HALVES)]
            for h in range(HALVES):
                act.wait_ge(x1t_ready, h + 1)
                nc.scalar.activation(x_tok[:, 4 * h:4 * h + 4, :], psum[:, 2 + h, :].rearrange("p (t c) -> p t c", c=C),
                                     ACT.Copy).then_inc(x1tok_ready, 1)
            for h, cols in enumerate(halves):
                act.wait_ge(attn_ready, h + 1)
                nc.scalar.activation(attn[:, cols], psum[0:ADIM, 4 + h, :], ACT.Tanh,
                                     bias=field("l1_small", "b1c")[0:ADIM, :]).then_inc(attn_done, 1)
            act.wait_ge(soft_ready, 1)
            nc.scalar.activation(soft_e[:, :, :], soft[:, :, :], ACT.Exp).then_inc(softexp_ready, 1)
            act.wait_ge(pooled_ready, 1)
            nc.scalar.activation(pool_ch[:, halves[0]], psum[:, 0, :], ACT.Copy).then_inc(poolch_act, 1)
            for h, cols in enumerate(halves):
                act.wait_ge((poolch_act, poolch_dve)[h], 1)
                nc.scalar.activation(x_hi[:, cols], pool_ch[:, cols], ACT.Copy).then_inc(xhi_ready, 1)

            units = [(e, k, h) for e in range(E1) for k in range(FCH1) for h in range(HALVES)]
            UNITS = FCH1 * HALVES
            act.wait_ge(ltok_done, 1)
            nc.scalar.activation(sig1[:, :, :], ltok[:, :, :], ACT.Sigmoid).then_inc(sig1_ready, 1)
            for u, (e, k, h) in enumerate(units):
                act.wait_ge(up1_ready, u + 1)
                if e >= 2 and u % UNITS == 0:
                    act.wait_ge(y1_ready, 2 * (e - 2) + 2)
                nc.scalar.activation(hid[:, e % 2, k, halves[h]], psum[:, u % 3, :], ACT.Gelu,
                                     bias=field("l1_small", "b1")[:, e * FCH1 + k:e * FCH1 + k + 1]
                                     ).then_inc(hid1_ready, 1)
                if u == 3 * UNITS - 1:
                    for a in range(2):
                        act.wait_ge(gate1t_ready, a + 1)
                        nc.scalar.activation(gate1_t[:, halves[a]], psum[0:E1, (5, 7)[a], :], ACT.Copy
                                             ).then_inc(gate1t_done, 1)

            l2 = lambda name: field("l2_all", name)
            for h, cols in enumerate(halves):
                act.wait_ge(x2t_ready, h + 1)
                nc.scalar.activation(x_ch[:, cols], psum[:, h, :], ACT.Copy).then_inc(x2ch_ready, 1)
            for h, cols in enumerate(halves):
                act.wait_ge(net_pre, h + 1)
                nc.scalar.activation(net[:, cols], psum[0:HN2, 4 + h, :], ACT.Gelu, bias=l2("bn1")[0:HN2, :]
                                     ).then_inc(net_ready, 1)
            for h, cols in enumerate(halves):
                act.wait_ge(soma_pre, h + 1)
                nc.scalar.activation(soma[:, cols], psum[:, 2 + h, :], ACT.Gelu, bias=l2("bsoma")
                                     ).then_inc(soma_ready, 1)
            for h, cols in enumerate(halves):
                act.wait_ge(wg_pre, h + 1)
                nc.scalar.activation(gated[:, cols], psum[:, h, :], ACT.Sigmoid, bias=l2("bg")).then_inc(wg_ready, 1)
            for h, cols in enumerate(halves):
                act.wait_ge(mod_pre, h + 1)
                nc.scalar.activation(mod[:, cols], psum[:, 6 + h, :], ACT.Sigmoid, bias=l2("bn2")).then_inc(mod_sig, 1)
            for h, cols in enumerate(halves):
                act.wait_ge(tg_pre, h + 1)
                nc.scalar.activation(tgate[:, :].rearrange("p (b s) -> p s b", s=S)[:, 16 * h:16 * (h + 1), :],
                                     psum[:, h, :].rearrange("p (s b) -> p s b", b=B), ACT.Sigmoid, bias=l2("btemp")).then_inc(tg_ready, 1)
            act.wait_ge(var_ready, 2)
            nc.scalar.activation(std[:, :], bn_m[:, :, 1], ACT.Sqrt, bias=field("early", "eps")).then_inc(std_ready, 1)
            for h, cols in enumerate(halves):
                act.wait_ge(yt_ready, h + 1)
                nc.scalar.activation(y_ch[:, cols], psum[:, 4 + h, :], ACT.Identity, bias=l2("beta"), scale=l2("gamma")
                                     ).then_inc(ych_ready, 1)
            for u in range(HALVES * FCH2):
                h, k = u // FCH2, u % FCH2
                act.wait_ge(ff2_pre, u + 1)
                nc.scalar.activation(hid[:, 0, k, halves[h]], psum[:, u % 4, :], ACT.Gelu_apprx_tanh,
                                     bias=l2("b1")[:, k:k + 1]).then_inc(ff2_ready, 1)
            for h, cols in enumerate(halves):
                act.wait_ge(low2_pre, h + 1)
                nc.scalar.activation(low2[:, cols], psum[:, 4 + h, :], ACT.Copy).then_inc(low2_ready, 1)

            for h in range(HALVES):
                act.wait_ge(x3t_ready, h + 1)
                nc.scalar.activation(x_tok[:, 4 * h:4 * h + 4, :], psum[:, 6 + h, :].rearrange("p (t c) -> p t c", c=C),
                                     ACT.Copy).then_inc(x3tok_ready, 1)
            for h, cols in enumerate(halves):
                act.wait_ge(zch_ready, h + 1)
                nc.scalar.activation(x_hi[:, cols], z_ch[:, cols], ACT.Copy).then_inc(zhi_ready, 1)
            units3 = [(e, k, h) for e in range(E3) for k in range(FCH3) for h in range(HALVES)]
            for u, (e, k, h) in enumerate(units3):
                act.wait_ge(g3_ready, u + 1)
                if u >= 2:
                    act.wait_ge(hid3_ready, u - 1)
                nc.scalar.activation(silu3[:, u % 2, :], psum[:, u % 2, :], ACT.Silu,
                                     bias=field("l3_small", "gate_b")[:, e * FCH3 + k:e * FCH3 + k + 1]
                                     ).then_inc(silu3_ready, 1)
                if u == 1:
                    act.wait_ge(rest3_ready, 1)
                    nc.scalar.activation(ex[:, :, 0:E3], rest[:, :, 0:E3], ACT.Exp).then_inc(exp3_ready, 1)
                if u == 2 * FCH3 * HALVES - 1:
                    for a in range(2):
                        act.wait_ge(gate3t_ready, a + 1)
                        nc.scalar.activation(gate3_t[:, halves[a]], psum[0:E3, 6 + a, :], ACT.Copy
                                             ).then_inc(gate3t_done, 1)

        @block.vector
        def _(dve):
            steps = [0]
            ts, tt = nc.vector.tensor_scalar, nc.vector.tensor_tensor
            stt, red = nc.vector.scalar_tensor_tensor, nc.vector.tensor_reduce

            def chain(ins):
                steps[0] += 1
                ins.then_inc(dve_step, 1)
                dve.wait_ge(dve_step, steps[0])

            def layer_stats(src):
                for t in range(TILES):
                    last = nc.vector.bn_stats(bn_s[:, t, :], src(t))
                chain(last)
                for t in range(TILES):
                    last = nc.vector.bn_aggr(bn_m[:, t, :], bn_s[:, t, :])
                last.then_inc(var_ready, 1)

            dve.wait_ge(loaded["ids"], 16)
            dve.wait_ge(loaded["early"], 16)
            chain(nc.vector.tensor_copy(ids_f[:, :], ids_i[:, :]))
            ts(lang_b[:, :], ids_f[0:LANGS, 0:B], pidx[0:LANGS, :], None, ALU.is_equal).then_inc(lang_ready, 1)
            dve.wait_ge(lang_ready, 1)
            nc.vector.tensor_copy(lang_h[:, :].rearrange("l (b s) -> l b s", s=S), bc(lang_b[:, :], 2, S)
                                  ).then_inc(lang_ready, 1)

            dve.wait_ge(loaded["l2_decay"], 16)
            blend = field("l2_decay", "blend")
            chain(red(bl_max[:, :], blend, X_AXIS, ALU.max))
            ts(bl[:, :], blend, bl_max[:, :], None, ALU.subtract).then_inc(blend_ready, 1)
            dve.wait_ge(taue_ready, 1)
            chain(ts(tau_e[:, :], tau_e[:, :], 1.0, None, ALU.add))
            nc.vector.reciprocal(alpha[:, :], tau_e[:, :]).then_inc(alpha_ready, 1)
            dve.wait_ge(blexp_ready, 1)
            chain(red(bl_sum[:, :], bl_e[:, 0:D2], X_AXIS, ALU.add))
            chain(nc.vector.reciprocal(bl_sum[:, :], bl_sum[:, :]))
            ts(bl[:, :], bl_e[:, :], bl_sum[:, :], None, ALU.mult).then_inc(blw_ready, 1)

            dve.wait_ge(loaded["x_tok"], 16)
            for h in range(HALVES):
                dve.wait_ge(adapt_ready, h + 1)
                last = tt(res0[:, 4 * h:4 * h + 4, :], psum[:, 6 + h, :].rearrange("p (t c) -> p t c", c=C),
                          x_tok[:, 4 * h:4 * h + 4, :], ALU.add)
            chain(last)
            layer_stats(lambda t: res0[:, t, :])
            dve.wait_ge(std_ready, 1)
            chain(nc.vector.reciprocal(rstd[:, :], std[:, :]))
            for t in range(TILES):
                last = ts(res0[:, t, :], res0[:, t, :], bn_m[:, t, 0:1], rstd[:, t:t + 1], ALU.subtract, ALU.mult)
            chain(last)
            dve.wait_ge(affine_ready, 1)
            for h in range(HALVES):
                tiles = slice(4 * h, 4 * h + 4)
                affine = psum[:, 2 * h:2 * h + 2, :].rearrange("p b (t a c) -> p (b t) a c", a=2, c=C)
                chain(tt(res0[:, tiles, :], affine[:, :, 0, :], res0[:, tiles, :], ALU.mult))
                tt(c0[:, tiles, :], affine[:, :, 1, :], res0[:, tiles, :], ALU.add).then_inc(c0_ready, 1)

            def first_best(src, best, onehot, iota, n):
                chain(red(best[:, :], src[:, :, 0:n], X_AXIS, ALU.max))
                chain(tt(eqm[:, :, 0:n], src[:, :, 0:n], bc(best[:, :], 2, n), ALU.is_equal))
                chain(tt(eqm[:, :, 0:n], eqm[:, :, 0:n], bc(iota, 1, TILES), ALU.mult))
                chain(red(pick[:, :], eqm[:, :, 0:n], X_AXIS, ALU.min))
                return tt(onehot[:, :, 0:n], bc(iota, 1, TILES), bc(pick[:, :], 2, n), ALU.is_equal)

            flat = "p t e -> p (t e)"
            iota16 = field("consts", "iota16")
            dve.wait_ge(lg_ready, 1)
            chain(nc.vector.tensor_copy(lg[:, :, :].rearrange(flat), psum[:, 6, 0:TILES * E0]))
            chain(first_best(lg, top1, oh1, iota16, E0))
            nc.vector.tensor_copy(oh1_h[:, :], oh1[:, :, :].rearrange(flat)).then_inc(choice_ready, 1)
            chain(stt(rest[:, :, :].rearrange(flat), oh1[:, :, :].rearrange(flat), NEG, lg[:, :, :].rearrange(flat),
                      ALU.mult, ALU.add))
            chain(first_best(rest, top2, oh2, iota16, E0))
            nc.vector.tensor_copy(oh2_h[:, :], oh2[:, :, :].rearrange(flat)).then_inc(choice_ready, 1)
            tt(rest[:, :, :], lg[:, :, :], bc(top1[:, :], 2, E0), ALU.subtract).then_inc(rest_ready, 1)
            dve.wait_ge(exp_ready, 1)
            chain(red(exsum[:, :], ex[:, :, :], X_AXIS, ALU.add))
            nc.vector.reciprocal(rsum[:, :], exsum[:, :])
            chain(tt(eqm[:, :, :], oh1[:, :, :], oh2[:, :, :], ALU.add))
            chain(tt(prob[:, :, :], ex[:, :, :], eqm[:, :, :], ALU.mult))
            chain(tt(prob[:, :, :], prob[:, :, :], bc(rsum[:, :], 2, E0), ALU.mult))
            dve.wait_ge(rank_ready, 1)
            rank = psum[:, 7, 0:2 * P].rearrange("p (a q) -> p a q", a=2)
            tt(posa[:, :, :].rearrange(flat), rank[:, 0, :], oh1[:, :, :].rearrange(flat), ALU.mult)
            chain(tt(posb[:, :, :].rearrange(flat), rank[:, 1, :], oh2[:, :, :].rearrange(flat), ALU.mult))
            chain(tt(posa[:, :, :], posa[:, :, :], posb[:, :, :], ALU.add))
            for i in range(BPT):
                last = ts(place[:, :, i, :], posa[:, :, :], field("consts", "batch_in_tile")[:, i:i + 1], None, ALU.mult)
            chain(last)
            for c in range(CAP):
                last = ts(disp[:, :, :, :, c].rearrange("p t i e -> p (t i e)"),
                          place[:, :, :, :].rearrange("p t i e -> p (t i e)"), float(c + 1), None, ALU.is_equal)
            last.then_inc(disp_ready, 1)
            for a in range(2):
                ts(prob_par[:, :, a, :], prob[:, :, :], field("consts", "parity")[:, a:a + 1], None, ALU.mult)
            chain(ts(posb[:, :, :], posa[:, :, :], float(CAP), None, ALU.min))
            for a in range(2):
                for c in range(CAP):
                    last = stt(comb[:, :, a, :, c], posb[:, :, :], float(c + 1), prob_par[:, :, a, :],
                               ALU.is_equal, ALU.mult)
            last.then_inc(comb_ready, 1)
            for g in (2, 3):
                dve.wait_ge(gather_ready, g + 1)
                nc.vector.tensor_copy(slot_in[:, :, 2 * g:2 * g + 2, :, :].rearrange("p e t i c -> p e (t i) c"),
                                      psum[:, g, :].rearrange("p (b e c) -> p e b c", e=E0, c=CAP)
                                      ).then_inc(slotin_dve, 1)
            for g in range(4):
                dve.wait_ge(silu_ready, g + 1)
                cols = slice(g * HALF, (g + 1) * HALF)
                tt(hid0[:, cols], psum[H0:2 * H0, (6, 7, 4, 5)[g], :], silu0[:, cols], ALU.mult).then_inc(hid0_ready, 1)
            for g in (2, 3):
                dve.wait_ge(proj_ready, g + 1)
                nc.vector.tensor_copy(slot_ch[:, :, :, 4 * g:4 * g + 4, :].rearrange("p t i e c -> p (t i) e c"),
                                      psum[:, g, :].rearrange("p (e b c) -> p b e c", e=4, c=CAP)
                                      ).then_inc(slotch_dve, 1)
            for g in (2, 3):
                dve.wait_ge(slott_ready, g + 1)
                nc.vector.tensor_copy(slot_out[:, 4 * g:4 * g + 4, :],
                                      psum[:, 4 + g, :].rearrange("p (q c) -> p q c", c=C)).then_inc(slotout_dve, 1)
            for h in range(HALVES):
                cols = slice(h * HALF, (h + 1) * HALF)
                dve.wait_ge(y0_ready, h + 1)
                tt(x_ch[:, cols], psum[:, h, :], x_ch[:, cols], ALU.add).then_inc(x1_ready, 1)

            dve.wait_ge(score_ready, 1)
            tt(score_d[:, :, :], bc(eye32, 1, TILES), bc(psum[:, 6, 0:TILES], 2, S), ALU.mult).then_inc(scored_ready, 1)
            dve.wait_ge(spread_ready, 1)
            chain(tt(soft[:, :, :], psum[:, 7, 0:TILES * S].rearrange("p (t s) -> p t s", s=S), mask_add[:, :, :],
                     ALU.add))
            chain(red(rmax[:, :], soft[:, :, :], X_AXIS, ALU.max))
            tt(soft[:, :, :], soft[:, :, :], bc(rmax[:, :], 2, S), ALU.subtract).then_inc(soft_ready, 1)
            dve.wait_ge(softexp_ready, 1)
            chain(red(rden[:, :], soft_e[:, :, :], X_AXIS, ALU.add))
            chain(tt(rden[:, :], rden[:, :], seen[:, :], ALU.mult))
            chain(nc.vector.reciprocal(rden[:, :], rden[:, :]))
            chain(tt(rden_wide[:, :, :], bc(rden[:, :], 2, BPT), bc(field("consts", "batch_in_tile"), 1, TILES), ALU.mult))
            chain(tt(soft_wide[:, :, :, :], bc(soft_e[:, :, :], 2, BPT), bc(rden_wide[:, :, :], 3, S), ALU.mult))
            nc.vector.transpose(soft_t[:, :, :].rearrange("p t q -> p (t q)"),
                                soft_wide[:, :, :, :].rearrange("p t i s -> p (t i s)")).then_inc(softt_ready, 1)
            dve.wait_ge(pooled_ready, 2)
            nc.vector.tensor_copy(pool_ch[:, HALF:2 * HALF], psum[:, 1, :]).then_inc(poolch_dve, 1)

            for h in range(HALVES):
                cols = slice(h * HALF, (h + 1) * HALF)
                dve.wait_ge(xhi_ready, h + 1)
                tt(x_lo[:, cols], pool_ch[:, cols], x_hi[:, cols].bitcast(F32), ALU.subtract).then_inc(xlo_ready, 1)
            nc.vector.memset(best_thr[:, :], -BOUND)
            for h in range(HALVES):
                dve.wait_ge(lrow_ready, h + 1)
                ts(lrow[:, h * HALF:(h + 1) * HALF], psum[:, 4 + h, :], -BOUND, None, ALU.max).then_inc(lrow_done, 1)
            dve.wait_ge(ltok_ready, 1)
            nc.vector.tensor_copy(ltok[:, :, :].rearrange(flat), psum[:, 6, 0:TILES * E1]).then_inc(ltok_done, 1)
            for r in range(ROUNDS):
                width = 2 * BOUND / 16.0 ** (r + 1)
                chain(tt(thr[:, :], best_thr[:, :], field("consts", "steps")[:, r:r + 1], ALU.add))
                chain(ts(above_row[:, :], lrow[:, :], thr[:, :], None, ALU.is_ge, ALU.add, accum_out=hits[:, :]))
                ts(enough_h[:, :], hits[:, :], float(TOP1), None, ALU.is_ge).then_inc(enough_ready, 1)
                dve.wait_ge(count_ready, r + 1)
                chain(stt(best_thr[:, :], psum[:, 6, 0:1], width, best_thr[:, :], ALU.mult, ALU.add))
            chain(ts(best_end[:, :], best_thr[:, :], width, None, ALU.add))
            eye8 = field("consts", "eye8")[0:E1, :]
            ts(thr_d[:, 0, :], eye8, best_thr[0:E1, :], None, ALU.mult)
            ts(thr_d[:, 1, :], eye8, best_end[0:E1, :], None, ALU.mult).then_inc(thrd_ready, 1)
            dve.wait_ge(thrtok_ready, 1)
            low_end = bc(psum[:, 6, 0:E1], 1, TILES)
            tt(sure[:, :, :], ltok[:, :, :], bc(psum[:, 6, E1:2 * E1], 1, TILES), ALU.is_ge)
            chain(tt(tied[:, :, :], ltok[:, :, :], low_end, ALU.is_gt))
            chain(tt(sure[:, :, :], sure[:, :, :], tied[:, :, :], ALU.mult))
            chain(tt(tied[:, :, :], ltok[:, :, :], low_end, ALU.is_ge))
            nc.vector.tensor_copy(sure_h[:, :, :], sure[:, :, :])
            chain(tt(tied[:, :, :], tied[:, :, :], sure[:, :, :], ALU.subtract))
            nc.vector.tensor_copy(tied_h[:, :], tied[:, :, :].rearrange(flat)).then_inc(tied_ready, 1)
            dve.wait_ge(order_ready, 1)
            chain(ts(room[:, :], psum[:, 7, HALF - E1:HALF], -1.0, float(TOP1), ALU.mult, ALU.add))
            chain(tt(gate1[:, :, :], psum[:, 7, 0:TILES * E1].rearrange("p (t e) -> p t e", e=E1),
                     bc(room[:, :], 1, TILES), ALU.is_le))
            chain(tt(gate1[:, :, :], gate1[:, :, :], tied[:, :, :], ALU.mult))
            chain(tt(gate1[:, :, :], gate1[:, :, :], sure[:, :, :], ALU.add))
            dve.wait_ge(sig1_ready, 1)
            tt(gate1[:, :, :], gate1[:, :, :], sig1[:, :, :], ALU.mult).then_inc(gate1_ready, 1)
            dve.wait_ge(gate1_ready, 1)
            for g in range(2 * E1):
                e, h = g // 2, g % 2
                dve.wait_ge(y1_ready, g + 1)
                if g >= 2:
                    dve.wait_ge(y1_used, g - 1)
                for t in range(4 * h, 4 * h + 4):
                    last = stt(x_tok[:, t, :], psum[:, 3 + h, (t % 4) * C:(t % 4 + 1) * C], gate1[:, t, e:e + 1],
                               x_tok[:, t, :], ALU.mult, ALU.add)
                last.then_inc(y1_used, 1)
            for h in range(HALVES):
                dve.wait_ge(y1_ready, 2 * E1 + h + 1)
                dve.wait_ge(y1_used, 2 * E1 + h - 1)
                tt(x_tok[:, 4 * h:4 * h + 4, :], psum[:, 3 + h, :].rearrange("p (t c) -> p t c", c=C),
                   x_tok[:, 4 * h:4 * h + 4, :], ALU.add).then_inc(y1_used, 1)

            halves = [slice(h * HALF, (h + 1) * HALF) for h in range(HALVES)]
            dve.wait_ge(decay_ready, 1)
            dve.wait_ge(x2ch_ready, 2)
            nc.vector.tensor_tensor_scan(ctx_ch[:, :], decay[:, :], x_ch[:, :], 0.0, ALU.mult, ALU.add
                                         ).then_inc(ctx_ready, 1)
            by_step = lambda a: a[:, :].rearrange("p (s b) -> p b s", b=B)
            for h, cols in enumerate(halves):
                dve.wait_ge(mod_sig, h + 1)
                chain(ts(mod[:, cols], mod[:, cols], 0.5, None, ALU.add))
                chain(nc.vector.tensor_copy(mod_hi[:, cols], mod[:, cols]))
                stt(by_step(mod_w)[:, 16 * h:16 * (h + 1), :],
                    mod_hi[:, cols].bitcast(F32).rearrange("p (b s) -> p b s", s=S), field("consts", "lo_x"),
                    mod[:, cols].rearrange("p (b s) -> p b s", s=S), ALU.mult, ALU.subtract).then_inc(mod_ready, 1)
            dve.wait_ge(wg_ready, 2)
            chain(tt(by_step(gated_s), gated[:, :].rearrange("p (b s) -> p b s", s=S),
                     x_ch[:, :].rearrange("p (b s) -> p b s", s=S), ALU.mult))
            nc.vector.memset(traces[:, 0:B], 0.0)
            for lag in range(S):
                n = (S - lag) * B
                bank = 2 * (lag % 4)
                dve.wait_ge(lag_ready, lag + 1)
                if lag <= 1:
                    dst = (traces_v[:, :], traces[:, B:N])[lag]
                elif lag in VECTOR_LAGS:
                    dst = prod_v[:, 0:n]
                else:
                    turn = POOL_LAGS.index(lag)
                    dst = prod[:, turn % 3, 0:n]
                    if turn >= 4:
                        dve.wait_ge(summed, turn - 3)
                tt(dst, psum[:, bank:bank + 2, :].rearrange("p a n -> p (a n)")[:, 0:n], gated_s[:, 0:n],
                   ALU.mult).then_inc(prod_ready, 1)
                if lag in VECTOR_LAGS:
                    dve.wait_ge(prod_ready, lag + 1)
                    chain(tt(traces_v[:, lag * B:N], traces_v[:, lag * B:N], prod_v[:, 0:n], ALU.add))
            dve.wait_ge(summed, len(POOL_LAGS) - 1)
            for h, cols in enumerate(halves):
                tt(temporal[:, cols], traces[:, cols], traces_v[:, cols], ALU.add).then_inc(temporal_ready, 1)
            dve.wait_ge(tg_ready, 2)
            for h, cols in enumerate(halves):
                tt(soma[:, cols], soma[:, cols], tgate[:, cols], ALU.mult).then_inc(sg_ready, 1)
            dve.wait_ge(out2_ready, 2)
            out2 = lambda t: psum[:, 2 + t // 4, (t % 4) * C:(t % 4 + 1) * C]
            layer_stats(out2)
            dve.wait_ge(std_ready, 2)
            chain(nc.vector.reciprocal(rstd[:, :], std[:, :]))
            for t in range(TILES):
                last = ts(ynorm[:, t, :], out2(t), bn_m[:, t, 0:1], rstd[:, t:t + 1], ALU.subtract, ALU.mult)
                if t % 4 == 3:
                    last.then_inc(ynorm_ready, 1)
            for h, cols in enumerate(halves):
                dve.wait_ge(low_pre, h + 1)
                chain(nc.vector.tensor_copy(low_hi[:, cols], psum[:, 6 + h, :]))
                stt(low_w[:, cols], low_hi[:, cols].bitcast(F32), field("consts", "lo_x"), psum[:, 6 + h, :], ALU.mult,
                    ALU.subtract).then_inc(low_ready, 1)
            for h, cols in enumerate(halves):
                dve.wait_ge(y2_ready, h + 1)
                stt(x_ch[:, cols], psum[:, 6 + h, :], field("l2_all", "b2"), x_ch[:, cols], ALU.add, ALU.add
                    ).then_inc(x3_ready, 1)

            dve.wait_ge(z_ready, 1)
            chain(nc.vector.tensor_copy(subj_bias[:, :], psum[:, 2, 0:B]))
            for h, cols in enumerate(halves):
                dve.wait_ge(z_ready, h + 1)
                tt(z_ch[:, cols].rearrange("p (b s) -> p b s", s=S), psum[:, h, :].rearrange("p (b s) -> p b s", s=S),
                   bc(subj_bias[:, 16 * h:16 * (h + 1)], 2, S), ALU.add).then_inc(zch_ready, 1)
            for h, cols in enumerate(halves):
                dve.wait_ge(zhi_ready, h + 1)
                dve.wait_ge(zch_ready, h + 1)
                tt(x_lo[:, cols], z_ch[:, cols], x_hi[:, cols].bitcast(F32), ALU.subtract).then_inc(zlo_ready, 1)
            iota8 = field("consts", "iota8")
            n = E3

            def first3():
                dve.wait_ge(lg3_ready, 1)
                nc.vector.tensor_copy(lg[:, :, 0:n], psum[:, 3, 0:TILES * n].rearrange("p (t e) -> p t e", e=n)
                                      ).then_inc(lg3_used, 1)
                dve.wait_ge(lg3_used, 1)
                chain(first_best(lg, top1, oh1, iota8, n))

            def second3():
                chain(stt(rest[:, :, 0:n], oh1[:, :, 0:n], NEG, lg[:, :, 0:n], ALU.mult, ALU.add))
                chain(first_best(rest, top2, oh2, iota8, n))
                tt(rest[:, :, 0:n], lg[:, :, 0:n], bc(top1[:, :], 2, n), ALU.subtract).then_inc(rest3_ready, 1)

            def kept3():
                dve.wait_ge(exp3_ready, 1)
                red(exsum[:, :], ex[:, :, 0:n], X_AXIS, ALU.add)
                chain(tt(eqm[:, :, 0:n], oh1[:, :, 0:n], oh2[:, :, 0:n], ALU.add))
                nc.vector.reciprocal(rsum[:, :], exsum[:, :])
                chain(tt(prob[:, :, 0:n], ex[:, :, 0:n], eqm[:, :, 0:n], ALU.mult))
                chain(tt(prob[:, :, 0:n], prob[:, :, 0:n], bc(rsum[:, :], 2, n), ALU.mult))
                chain(red(exsum[:, :], prob[:, :, 0:n], X_AXIS, ALU.add))

            def gates3():
                chain(ts(exsum[:, :], exsum[:, :], 1e-9, None, ALU.add))
                chain(nc.vector.reciprocal(rsum[:, :], exsum[:, :]))
                tt(gate3[:, :, :], prob[:, :, 0:n], bc(rsum[:, :], 2, n), ALU.mult).then_inc(gate3_ready, 1)
                dve.wait_ge(gate3_ready, 1)

            units3 = [(e, k, h) for e in range(E3) for k in range(FCH3) for h in range(HALVES)]
            UNITS3 = FCH3 * HALVES

            def hidden3(u):
                e, k, h = units3[u]
                dve.wait_ge(silu3_ready, u + 1)
                dve.wait_ge(u3_ready, u + 1)
                if e >= 2 and u % UNITS3 == 0:
                    dve.wait_ge(y3_ready, 2 * (e - 2) + 2)
                stt(hid[:, 0, (e % 2) * 2 + k, halves[h]], psum[:, 2 + u % 2, :],
                    field("l3_small", "up_b")[:, e * FCH3 + k:e * FCH3 + k + 1], silu3[:, u % 2, :],
                    ALU.add, ALU.mult).then_inc(hid3_ready, 1)

            def output3(g):
                e, h = g // 2, g % 2
                dve.wait_ge(y3_ready, g + 1)
                if g >= 2:
                    dve.wait_ge(y3_used, g - 1)
                for t in range(4 * h, 4 * h + 4):
                    last = stt(x_tok[:, t, :], psum[:, 4 + h, (t % 4) * C:(t % 4 + 1) * C], gate3[:, t, e:e + 1],
                               x_tok[:, t, :], ALU.mult, ALU.add)
                last.then_inc(y3_used, 1)

            first3()
            hidden3(0)
            second3()
            hidden3(1)
            kept3()
            hidden3(2)
            gates3()
            hidden3(3)
            dve.wait_ge(x3tok_ready, 2)
            for e in range(E3):
                if e >= 1:
                    for u in range(e * UNITS3, (e + 1) * UNITS3):
                        hidden3(u)
                if e >= 1:
                    output3(2 * (e - 1))
                    output3(2 * (e - 1) + 1)
            output3(2 * (E3 - 1))
            output3(2 * (E3 - 1) + 1)
            for h in range(HALVES):
                dve.wait_ge(y3_ready, 2 * E3 + h + 1)
                dve.wait_ge(y3_used, 2 * E3 + h - 1)
                tt(x_tok[:, 4 * h:4 * h + 4, :], psum[:, 4 + h, :].rearrange("p (t c) -> p t c", c=C),
                   x_tok[:, 4 * h:4 * h + 4, :], ALU.add).then_inc(y3_used, 1)


def layouts(inputs):
    import numpy as np

    f = {k: np.asarray(v) for k, v in inputs.items()}

    def rows(a, n=P):
        a = np.asarray(a)
        return np.concatenate([a, np.zeros((n - a.shape[0],) + a.shape[1:], a.dtype)]) if a.shape[0] < n else a

    def col(a):
        return rows(np.asarray(a).reshape(-1, 1))

    def cols(a):
        return np.asarray(a).reshape(-1, P).T

    def kmajor(a):
        return a.transpose(1, 0, 2).reshape(a.shape[1], -1)

    def chunked(a):
        return a.reshape(-1, P, a.shape[-1]).transpose(1, 0, 2).reshape(P, -1)

    p = np.arange(P)
    j, l = p[:, None] % S, np.arange(S)[None, :]
    own = np.repeat(np.eye(LANGS, dtype=bool), ADIM, axis=1)
    lang_ff = f["L0_cond_W1"].shape[0] * ADIM
    w2 = rows(f["L0_cond_W2"].reshape(lang_ff, C), 3 * P)
    fields = {
        "early": {"far": rows(np.where(own, 0.0, FAR)), "pidx": p[:, None], "eps": np.full((P, 1), EPS)},
        "l0_w1": {"w1": kmajor(f["L0_cond_W1"]), "b1": cols(rows(f["L0_cond_b1"].reshape(-1), 3 * P))},
        "consts": {
            "ident": np.eye(P), "eye32": j == l, "tri_batch": (p[:, None] // S == p // S) & (p[:, None] <= p),
            "ones_batch": p[:, None] // S == p // S, "tri_all": p[:, None] <= p,
            "same_expert": (p[:, None] % E1 == p % E1) & (p[:, None] >= E1),
            "mask_pre": np.where(l <= j, 0.0, NEG), "mask_post": np.where(l >= j, 0.0, NEG),
            "mask_cloze": np.where(l != j, 0.0, NEG),
            "counts": np.concatenate([j + 1, S - j, 0 * j + S - 1], 1),
            "iota16": np.tile(np.arange(E0) - E0, (P, 1)), "iota8": np.tile(np.arange(E3) - E3, (P, 1)),
            "steps": (p[:, None] // E1) * (2 * BOUND / 16.0 ** (1 + np.arange(ROUNDS)))[None, :],
            "eye8": rows(np.eye(8)),
            "batch_in_tile": p[:, None] // S == np.arange(BPT), "parity": p[:, None] // S % 2 == np.arange(2),
            "lo_w": p[:, None] // D2 % 2 == 1, "lo_x": p[:, None] // D2 >= 2,
        },
        "l0_small": {
            "table": rows(np.concatenate([f["L0_cond_b2"], f["L0_cond_gamma"], f["L0_cond_beta"]], 1)),
            "w2": chunked(w2), "router": f["L0_ffn_w_router"],
        },
        "l0_gatefc": {"gatefc": kmajor(np.concatenate([f["L0_ffn_w_gate"], f["L0_ffn_w_fc"]], 2))},
        "l0_proj": {"proj": rows(kmajor(f["L0_ffn_w_proj"]))},
        "l1_small": {
            "w1c": f["L1_cond_W1"], "b1c": col(f["L1_cond_b1"]), "v": col(f["L1_cond_v"]),
            "router": np.tile(f["L1_ffn_Wg"], (1, RANK_PARTS)), "b1": cols(f["L1_ffn_b1"]),
            "b2": rows(f["L1_ffn_b2"]),
        },
        "l1_w1": {"w1": kmajor(f["L1_ffn_W1"])},
        "l1_w2": {"w2": chunked(f["L1_ffn_W2"])},
        "l2_decay": {
            "blend": np.tile(f["cond_1024"].T, (1, 4)), "taus": col(np.tile(f["condB_tauraws"].reshape(-1), 4)),
            "tau_ctx": np.tile(f["L2_cond_tau_ctx"].reshape(1, 1), (P, 1)),
        },
        "l2_all": {
            "wg_x": f["L2_cond_Wg"][:, 0:C].T, "wg_ctx": f["L2_cond_Wg"][:, C:2 * C].T, "bg": col(f["L2_cond_bg"]),
            "wn1": f["L2_cond_Wn1"].T, "bn1": col(f["L2_cond_bn1"]), "wn2": rows(np.tile(f["cond_256"].T, (1, 4))),
            "bn2": col(np.tile(f["condB_bn2"].reshape(-1), 4)), "wtemp": f["L2_cond_Wtemp"].T,
            "btemp": col(f["L2_cond_btemp"]), "wsoma": f["L2_cond_Wsoma"].T, "bsoma": col(f["L2_cond_bsoma"]),
            "wout": f["L2_cond_Wout"].T, "gamma": col(f["L2_cond_gamma"]), "beta": col(f["L2_cond_beta"]),
            "u1": np.tile(f["L2_ffn_U1"], (1, 4)), "v1": np.tile(f["L2_ffn_V1"], (4, 1)), "b1": cols(f["L2_ffn_b1"]),
            "u2": chunked(f["L2_ffn_U2"]), "v2": np.tile(f["L2_ffn_V2"], (4, 1)), "b2": col(f["L2_ffn_b2"]),
        },
        "l3_small": {
            "cbias": rows(f["L3_cond_bias"]), "router": f["L3_ffn_router_w"].T, "gate_b": cols(f["L3_ffn_gate_b"]),
            "up_b": cols(f["L3_ffn_up_b"]), "down_b": rows(f["L3_ffn_down_b"]),
        },
        "l3_gate": {"gate": kmajor(f["L3_ffn_gate_w"])},
        "l3_up": {"up": kmajor(f["L3_ffn_up_w"])},
        "l3_down": {"down": chunked(f["L3_ffn_down_w"])},
    }
    arrays = {}
    for pack, names in PACKS.items():
        parts = [np.asarray(fields[pack][name]) for name, _ in names]
        for (name, width), part in zip(names, parts):
            assert part.shape == (P, width), (pack, name, part.shape)
        if pack in ("early", "consts"):
            parts = [np.asarray(part, np.float32) for part in parts]
        arrays[pack] = np.ascontiguousarray(np.concatenate(parts, 1))
    ids = np.concatenate([f["itok_B_0_8"], f["itok_B_0_2"], f["itok_B_0_7"]])
    arrays["ids"] = np.ascontiguousarray(np.tile(ids[None, :], (P, 1)))
    arrays["types"] = np.ascontiguousarray(np.repeat(f["itok_B_0_2"].reshape(TILES, BPT), S, axis=1).T)
    arrays["x"] = np.ascontiguousarray(f["x"].reshape(N, C))
    arrays["x_ch"] = np.ascontiguousarray(f["x"].reshape(N, C).T)
    arrays["subj_w"] = np.ascontiguousarray(f["L3_cond_weight"].transpose(0, 2, 1))
    return arrays


def kernel(**inputs):
    import concourse.bacc as bacc
    from concourse.bass_utils import run_bass_kernel_spmd

    arrays = layouts(inputs)
    nc = bacc.Bacc("TRN2", target_bir_lowering=False, num_devices=1)
    dram = {name: nc.dram_tensor("in_" + name, a.shape, mybir.dt.from_np(a.dtype), kind="ExternalInput").ap()
            for name, a in arrays.items()}
    out = nc.dram_tensor("out", (B, S, C), F32, kind="ExternalOutput").ap()
    program(nc, dram, out)
    r = run_bass_kernel_spmd(nc, [{"in_" + name: a for name, a in arrays.items()}], core_ids=[0])
    return r.results[0]["out"]
```

```python
from contextlib import ExitStack

import concourse.bass as bass
from concourse import mybir

F32 = mybir.dt.float32
F32R = mybir.dt.float32r
BF16 = mybir.dt.bfloat16
I32 = mybir.dt.int32
ALU = mybir.AluOpType
ACT = mybir.ActivationFunctionType
X_AXIS = mybir.AxisListType.X

P = 128
B, S, C = 32, 32, 128
N = B * S
TILES = N // P
BPT = P // S
HALF = 512
HALVES = N // HALF
LANGS, ADIM = 10, 32
LCH = (P, P, 64)
E0, H0, CAP = 16, 64, 4
SLOTS = E0 * CAP
E1, FF1 = 8, 512
FCH1 = FF1 // P
TOP1 = N * 2 // E1
RANK_PARTS = P // E1
DENSE1 = 2
SLOT_TILES = TOP1 // P
BOUND = 128.0
ROUNDS = 8
D2 = 32
HN2 = 32
FF2, RK2 = 512, 32
FCH2 = FF2 // P
SUBJ = 8
E3, FF3 = 8, 256
FCH3 = FF3 // P
LAG_ORDER = list(range(1, 26)) + [0] + list(range(26, S))
TENSOR_LAGS = (0, 1, 4, 6, 9, 11, 14, 16, 19, 21, 23, 25)
TENSOR_STEPS = [i for i, lag in enumerate(LAG_ORDER) if lag in TENSOR_LAGS]
POOL_STEPS = [i for i in range(S) if i not in TENSOR_STEPS]
LAG_GROUP = 4
FILLERS = {"first inputs": 36, "layer 0 norm": 25, "expert choice": 70, "dispatch": 80, "softmax": 70,
           "sum over lags": 19, "layer 2 norm": 50}
NEG = -1.0e30
FAR = -(2.0 ** 100)
EPS = 1e-5

PACKS = {
    "early": [("far", LANGS * ADIM), ("pidx", 1), ("eps", 1)],
    "l0_w1": [("w1", LANGS * ADIM), ("b1", 3)],
    "consts": [("ident", P), ("eye32", 32), ("tri_batch", P), ("ones_batch", P), ("tri_all", P),
               ("same_expert", P), ("mask_pre", 32), ("mask_post", 32),
               ("mask_cloze", 32), ("counts", 3), ("iota16", E0), ("iota8", E3),
               ("steps", ROUNDS), ("eye8", 8), ("batch_in_tile", BPT), ("parity", 2), ("lo_w", 1), ("lo_x", 1),
               ("slot_row", 2)],
    "l0_small": [("table", 3 * C), ("w2", 3 * C), ("router", E0)],
    "l0_gatefc": [("gatefc", E0 * 2 * H0)],
    "l0_proj": [("proj", E0 * C)],
    "l1_small": [("w1c", ADIM), ("b1c", 1), ("v", 1), ("router", P), ("b1", E1 * FCH1), ("b2", C)],
    "l1_w1": [("w1", E1 * FF1)],
    "l1_w2": [("w2", E1 * FCH1 * C)],
    "l2_decay": [("blend", P), ("taus", 1), ("tau_ctx", 1)],
    "l2_all": [("wg_x", C), ("wg_ctx", C), ("bg", 1), ("wn1", HN2), ("bn1", 1), ("wn2", P), ("bn2", 1),
               ("wtemp", C), ("btemp", 1), ("wsoma", C),
               ("bsoma", 1), ("wout", C), ("gamma", 1), ("beta", 1), ("u1", P), ("v1", FF2),
               ("b1", FCH2), ("u2", FCH2 * RK2), ("v2", C), ("b2", 1)],
    "l3_small": [("cbias", C), ("router", E3), ("gate_b", E3 * FCH3), ("up_b", E3 * FCH3), ("down_b", C)],
    "l3_gate": [("gate", E3 * FF3)],
    "l3_up": [("up", E3 * FF3)],
    "l3_down": [("down", E3 * FCH3 * C)],
}
WIDTH = {pack: sum(w for _, w in fields) for pack, fields in PACKS.items()}


def bc(ap, axis, n):
    shape = list(ap.shape)
    shape.insert(axis, n)
    return ap.unsqueeze(axis).to_broadcast(shape)


def program(nc, dram, out):
    ctx = ExitStack()
    with ctx:
        def sb(name, shape, dt=F32):
            return ctx.enter_context(nc.sbuf_tensor(name, shape, dt))

        def sem(name):
            return ctx.enter_context(nc.semaphore(name))

        psum = ctx.enter_context(nc.psum_tensor("psum", [P, 8, HALF], F32))

        shares = {"l3_gate": "l0_gatefc", "l3_up": "l0_proj"}
        packs = {name: sb("sb_" + name, [P, w]) for name, w in WIDTH.items()
                 if name not in shares and name not in shares.values()}
        with nc.sbuf_tensor("sb_l0_gatefc", [P, WIDTH["l0_gatefc"]], F32) as packs["l0_gatefc"], \
                nc.sbuf_tensor("sb_l0_proj", [P, WIDTH["l0_proj"]], F32) as packs["l0_proj"]:
            pass
        pick1 = [sb("pick1_%d" % k, [P, TILES, TOP1], F32R) for k in range(2)]
        packs.update({name: packs[old] for name, old in shares.items()})

        def field(pack, name):
            at = 0
            for f, w in PACKS[pack]:
                if f == name:
                    return packs[pack][:, at:at + w]
                at += w
            raise KeyError(name)

        ident, eye32, pidx = field("consts", "ident"), field("consts", "eye32"), field("early", "pidx")
        x_tok = sb("x_tok", [P, TILES, C])
        x_ch = sb("x_ch", [P, N])
        ids_i = sb("ids_i", [P, 3 * B], I32)
        types_i = sb("types_i", [P, TILES], I32)
        subj_w = packs["l1_w1"][:, 0:B * C].rearrange("p (b c) -> p b c", c=C)

        loaded = {name: sem("loaded_" + name) for name in list(WIDTH) + ["ids", "types", "x_ch", "x_ch2", "x_tok", "slot_no"]}
        subj_loaded = sem("subj_loaded")

        far_h = sb("far_h", [LANGS, LANGS * ADIM], BF16)
        tri_batch_h = sb("tri_batch_h", [P, P], BF16)
        ones_batch_h = sb("ones_batch_h", [P, P], BF16)
        tri_all_h = sb("tri_all_h", [P, P], BF16)
        same_expert_h = sb("same_expert_h", [P, P], BF16)
        ones_h = sb("ones_h", [P, P], BF16)
        ones_f = sb("ones_f", [P, P])
        ids_f = sb("ids_f", [P, 3 * B])
        types_f = sb("types_f", [P, TILES])
        lang_b = sb("lang_b", [LANGS, B])
        lang_h = sb("lang_h", [LANGS, N], BF16)
        lang_f_rows = sb("lang_f_rows", [P, N])
        lang_f = lang_f_rows[0:LANGS, :]
        subj_b = sb("subj_b", [SUBJ, B])
        type_sel = sb("type_sel", [P, 3, TILES])
        mask_add = sb("mask_add", [P, TILES, S])
        mask_tmp = sb("mask_tmp", [P, TILES, S])
        seen = sb("seen", [P, TILES])
        seen_tmp = sb("seen_tmp", [P, TILES])
        pool_step = sem("pool_step")
        far_ready = sem("far_ready")
        lang_ready = sem("lang_ready")
        langf_ready = sem("langf_ready")
        consts_ready = sem("consts_ready")

        with nc.sbuf_tensor("big", [P, 8 * N], F32) as big:
            pass
        with nc.sbuf_tensor("put_0", [P, SLOT_TILES, N], F32R) as put_0, \
                nc.sbuf_tensor("put_1", [P, SLOT_TILES, N], F32R) as put_1, \
                nc.sbuf_tensor("hid_s", [P, FCH1, TOP1], F32) as hid_s, \
                nc.sbuf_tensor("x_s", [P, 2, TOP1], F32R) as x_s, \
                nc.sbuf_tensor("y_hi", [P, SLOT_TILES, C], F32R) as y_hi, \
                nc.sbuf_tensor("y_lo", [P, SLOT_TILES, C], F32R) as y_lo:
            pass
        put1 = (put_0, put_1)
        SLOT_BANKS = (2, 5)
        OUT1 = HALF - C
        mod_hi = sb("mod_hi", [P, N], F32R)
        mod_w = sb("mod_w", [P, N], F32R)
        prod_t = sb("prod_t", [P, 2, N])
        gated_s = sb("gated_s", [P, N])
        v1_w = sb("v1_w", [P, FF2], F32R)
        under_big = sb("under_big", [P, 5 * HALF])
        quarter = [big[:, 2 * N * k:2 * N * (k + 1)] for k in range(4)]
        with nc.sbuf_tensor("three", [P, 3 * N], F32) as three:
            pass
        w_hi = sb("w_hi", [P, 2, HALF], F32R)
        w_lo = sb("w_lo", [P, 2, HALF], F32R)
        x_lo = sb("x_lo", [P, N], F32R)
        ad_hid = three[:, :].rearrange("p (k n) -> p k n", k=3)
        with nc.sbuf_tensor("res0", [P, TILES, C], F32) as res0:
            pass
        x_hi = sb("x_hi", [P, N], F32R)
        bn_s = sb("bn_s", [P, TILES, 6])
        bn_m = sb("bn_m", [P, TILES, 2])
        std = sb("std", [P, TILES])
        rstd = sb("rstd", [P, TILES])
        with nc.sbuf_tensor("c0", [P, TILES, C], F32) as c0, \
                nc.sbuf_tensor("c0_ch", [P, N], F32) as c0_ch, \
                nc.sbuf_tensor("lg", [P, TILES, E0], F32) as lg:
            pass
        parts = sb("parts", [P, TILES, 2 * C + 2 * E1], F32R)
        eqm = sb("eqm", [P, TILES, E0])
        pick = sb("pick", [P, TILES])
        top1 = sb("top1", [P, TILES])
        top2 = sb("top2", [P, TILES])
        oh1 = sb("oh1", [P, TILES, E0])
        oh2 = sb("oh2", [P, TILES, E0])
        oh1_h = sb("oh1_h", [P, TILES * E0], BF16)
        oh2_h = sb("oh2_h", [P, TILES * E0], BF16)
        rest = sb("rest", [P, TILES, E0])
        ex = sb("ex", [P, TILES, E0])
        exsum = sb("exsum", [P, TILES])
        rsum = sb("rsum", [P, TILES])
        prob = sb("prob", [P, TILES, E0])
        posa = sb("posa", [P, TILES, E0])
        posb = sb("posb", [P, TILES, E0])
        comb = sb("comb", [P, TILES, 2, E0, CAP])
        comb_t = sb("comb_t", [P, TILES, P])
        slot_in = quarter[0].rearrange("p (e t i c) -> p e t i c", e=E0, t=TILES, i=BPT)
        silu0 = quarter[1][0:H0, :]
        hid0 = quarter[2][0:H0, :]
        disp = quarter[2].rearrange("p (t i e c) -> p t i e c", t=TILES, i=BPT, e=E0)
        place = quarter[1][:, 0:TILES * BPT * E0].rearrange("p (t i e) -> p t i e", t=TILES, i=BPT)
        prob_par = quarter[1][:, HALF:HALF + TILES * 2 * E0].rearrange("p (t a e) -> p t a e", t=TILES, a=2)
        slot_ch = quarter[3].rearrange("p (t i e c) -> p t i e c", t=TILES, i=BPT, e=E0)
        with nc.sbuf_tensor("slot_out", [P, B // 2, C], F32) as slot_out:
            pass
        under_lrow = sb("under_lrow", [P, N])
        sel_h = sb("sel_h", [P, E1, P], BF16)
        pos_t = sb("pos_t", [P, N], BF16)

        ad_ready = sem("ad_ready")
        adhid_ready = sem("adhid_ready")
        adapt_ready = sem("adapt_ready")
        affine_ready = sem("affine_ready")
        var_ready = sem("var_ready")
        std_ready = sem("std_ready")
        norm_ready = sem("norm_ready")
        normt_ready = sem("normt_ready")
        normch_ready = sem("normch_ready")
        lg_ready = sem("lg_ready")
        choice_ready = sem("choice_ready")
        rank_ready = sem("rank_ready")
        rest_ready = sem("rest_ready")
        exp_ready = sem("exp_ready")
        disp_ready = sem("disp_ready")
        comb_ready = sem("comb_ready")
        gather_ready = sem("gather_ready")
        slotin_act = sem("slotin_act")
        slotin_dve = sem("slotin_dve")
        combt_ready = sem("combt_ready")
        combt_used = sem("combt_used")
        gatefc_ready = sem("gatefc_ready")
        silu_ready = sem("silu_ready")
        hid0_ready = sem("hid0_ready")
        proj_ready = sem("proj_ready")
        slotch_act = sem("slotch_act")
        slotch_dve = sem("slotch_dve")
        slott_ready = sem("slott_ready")
        slotout_act = sem("slotout_act")
        slotout_dve = sem("slotout_dve")
        y0_ready = sem("y0_ready")
        x1_ready = sem("x1_ready")

        attn = c0_ch[0:ADIM, :]
        score_d = sb("score_d", [P, TILES, S])
        soft = mask_tmp
        with nc.sbuf_tensor("soft_e", [P, TILES, S], F32) as soft_e:
            pass
        sig1 = sb("sig1", [P, TILES, E1])
        gate1 = sb("gate1", [P, TILES, E1])
        chosen = sb("chosen", [P, TILES, E1])
        pos = sb("pos", [P, TILES, E1])
        soft_t = quarter[0][:, 0:N].rearrange("p (t i s) -> p t i s", t=TILES, i=BPT)
        rmax = sb("rmax", [P, TILES])
        rden = sb("rden", [P, TILES])
        pool_ch = sb("pool_ch", [P, N])

        xtok_pre = sem("xtok_pre")
        xtok_ready = sem("xtok_ready")
        attn_ready = sem("attn_ready")
        attn_done = sem("attn_done")
        score_ready = sem("score_ready")
        scored_ready = sem("scored_ready")
        spread_ready = sem("spread_ready")
        soft_ready = sem("soft_ready")
        softexp_ready = sem("softexp_ready")
        softt_ready = sem("softt_ready")
        pooled_ready = sem("pooled_ready")
        poolch_act = sem("poolch_act")
        poolch_dve = sem("poolch_dve")

        lrow = slot_out[:, 0:TILES, :].rearrange("p q c -> p (q c)")
        above_row = slot_out[:, TILES:2 * TILES, :].rearrange("p q c -> p (q c)")
        thr = sb("thr", [P, 1])
        best_thr = sb("best_thr", [P, 1])
        best_end = sb("best_end", [P, 1])
        hits = sb("hits", [P, 1])
        enough_h = sb("enough_h", [P, 1], BF16)
        thr_d = sb("thr_d", [E1, 2, E1])
        ltok = sb("ltok", [P, TILES, E1])
        sure = sb("sure", [P, TILES, E1])
        sure_h = sb("sure_h", [P, TILES, E1], BF16)
        tied = sb("tied", [P, TILES, E1])
        tied_h = sb("tied_h", [P, TILES * E1], BF16)
        chosen_h = tied_h
        room = sb("room", [P, E1])
        gate1_t = sb("gate1_t", [E1, N])
        x_slots = comb_t[:, :, :].rearrange("p (s a) c -> p s (a c)", s=SLOT_TILES)[:, :, 0:2 * C + 2 * E1]
        slot_gate = sb("slot_gate", [P, 2, SLOT_TILES])
        hid = big[:, :].rearrange("p (a k n) -> p a k n", a=2, k=FCH1)

        lrow_ready = sem("lrow_ready")
        lrow_done = sem("lrow_done")
        ltok_ready = sem("ltok_ready")
        ltok_done = sem("ltok_done")
        enough_ready = sem("enough_ready")
        count_ready = sem("count_ready")
        tied_ready = sem("tied_ready")
        sig1_ready = sem("sig1_ready")
        gate1_ready = sem("gate1_ready")
        slot_no = score_d[:, :, :].rearrange("p t s -> p (t s)")
        ptok = pool_ch[:, :].rearrange("p (t c) -> p t c", c=C)
        ptokt_ready = sem("ptokt_ready")
        ptokhi_ready = sem("ptokhi_ready")
        parts_ready = sem("parts_ready")
        gates_read = sem("gates_read")
        xslots_ready = sem("xslots_ready")
        xst_ready = sem("xst_ready")
        chosen_ready = sem("chosen_ready")
        rank1_ready = sem("rank1_ready")
        pos_ready = sem("pos_ready")
        experts_t = sem("experts_t")
        experts_done = sem("experts_done")
        posrow_ready = sem("posrow_ready")
        put_ready = sem("put_ready")
        put_used = sem("put_used")
        pick_ready = sem("pick_ready")
        xs_gathered = sem("xs_gathered")
        xs_ready = sem("xs_ready")
        ups_ready = sem("ups_ready")
        hids_ready = sem("hids_ready")
        ys_ready = sem("ys_ready")
        ysplit_ready = sem("ysplit_ready")
        w_split = sem("w_split")
        xhi_ready = sem("xhi_ready")
        xlo_ready = sem("xlo_ready")
        up1_ready = sem("up1_ready")
        hid1_ready = sem("hid1_ready")
        y1_ready = sem("y1_ready")
        y1_used = sem("y1_used")

        decay = sb("decay", [P, N])
        tau_e = sb("tau_e", [P, 2])
        alpha_group = sb("alpha_group", [P, 1])
        alpha = sb("alpha", [P, 2])
        bl_max = sb("bl_max", [P, 1])
        bl = sb("bl", [P, 4 * D2])
        bl_e = sb("bl_e", [P, 4 * D2])
        bl_sum = sb("bl_sum", [P, 1])
        lag_f = sb("lag_f", [P, LAG_GROUP, C])
        lag_w = sb("lag_w", [P, S, C], F32R)
        ctx_ch = comb_t[:, :, :].rearrange("p t q -> p (t q)")
        soma = slot_out[:, 0:TILES, :].rearrange("p q c -> p (q c)")
        gated = slot_out[:, TILES:2 * TILES, :].rearrange("p q c -> p (q c)")
        net = lang_f_rows[0:HN2, :]
        mod = c0_ch
        prod = three[:, :].rearrange("p (k n) -> p k n", k=3)
        traces = pool_ch
        temporal = traces

        def batch_half(ap, h):
            return ap[:, :].rearrange("p (s b) -> p s b", b=B)[:, :, h * B // 2:(h + 1) * B // 2]

        tgate = res0[:, :, :].rearrange("p t c -> p (t c)")
        ynorm = c0
        y_ch = c0_ch
        low_hi = x_hi
        low_w = x_lo
        low2 = lang_f_rows

        blend_ready = sem("blend_ready")
        exps2_ready = sem("exps2_ready")
        blw_ready = sem("blw_ready")
        blt_ready = sem("blt_ready")
        lag0_ready = sem("lag0_ready")
        alpha_ready = sem("alpha_ready")
        lagw_ready = sem("lagw_ready")
        decay_ready = sem("decay_ready")
        x2t_ready = sem("x2t_ready")
        x2ch_ready = sem("x2ch_ready")
        ctx_ready = sem("ctx_ready")
        soma_pre = sem("soma_pre")
        soma_ready = sem("soma_ready")
        net_pre = sem("net_pre")
        net_ready = sem("net_ready")
        wg_pre = sem("wg_pre")
        wg_ready = sem("wg_ready")
        mod_pre = sem("mod_pre")
        mod_sig = sem("mod_sig")
        mod_ready = sem("mod_ready")
        lag_ready = sem("lag_ready")
        prod_ready = sem("prod_ready")
        summed = sem("summed")
        added = sem("added")
        temporal_ready = sem("temporal_ready")
        sg_ready = sem("sg_ready")
        out2_ready = sem("out2_ready")
        low_pre = sem("low_pre")
        low_ready = sem("low_ready")
        ff2_pre = sem("ff2_pre")
        ff2_ready = sem("ff2_ready")
        low2_ready = sem("low2_ready")
        y2_ready = sem("y2_ready")
        x3_ready = sem("x3_ready")

        subj_bias = sb("subj_bias", [P, B])
        z_ch = decay
        z_tok = pool_ch[:, :].rearrange("p (t c) -> p t c", c=C)
        gate3 = sb("gate3", [P, TILES, E3])
        gate3_t = gate1_t
        silu3 = hid[:, 1, 0, :].rearrange("p (k n) -> p k n", k=2)

        z_ready = sem("z_ready")
        ztok_ready = sem("ztok_ready")
        zch_ready = sem("zch_ready")
        lg3_used = sem("lg3_used")
        gate3_ready = sem("gate3_ready")
        g3_ready = sem("g3_ready")
        silu3_ready = sem("silu3_ready")
        u3_ready = sem("u3_ready")
        hid3_ready = sem("hid3_ready")
        y3_ready = sem("y3_ready")
        y3_used = sem("y3_used")

        dve_step = sem("dve_step")
        stored = sem("stored")

        block = ctx.enter_context(nc.Block())

        @block.sync
        def _(sp):
            sp.dma_start(ids_i[:, :], dram["ids"]).then_inc(loaded["ids"], 16)
            for name in ("early", "l0_w1"):
                sp.dma_start(packs[name][:, :], dram[name]).then_inc(loaded[name], 16)
            sp.dma_start(x_ch[:, 0:HALF], dram["x_ch"][:, 0:HALF]).then_inc(loaded["x_ch"], 16)
            sp.dma_start(x_ch[:, HALF:N], dram["x_ch"][:, HALF:N]).then_inc(loaded["x_ch2"], 16)
            sp.dma_start(packs["l0_small"][:, :], dram["l0_small"]).then_inc(loaded["l0_small"], 16)
            sp.dma_start(x_tok[:, :, :], dram["x"].rearrange("(t p) c -> p t c", p=P)).then_inc(loaded["x_tok"], 16)
            sp.dma_start(packs["consts"][:, :], dram["consts"]).then_inc(loaded["consts"], 16)
            sp.dma_start(types_i[:, :], dram["types"]).then_inc(loaded["types"], 16)
            for name in ("l2_decay", "l0_gatefc", "l0_proj", "l1_small"):
                sp.dma_start(packs[name][:, :], dram[name]).then_inc(loaded[name], 16)
            for name in ("l1_w1", "l1_w2", "l2_all", "l3_small", "l3_down"):
                sp.dma_start(packs[name][:, :], dram[name]).then_inc(loaded[name], 16)
            sp.wait_ge(spread_ready, 1)
            sp.dma_start(slot_no, dram["slot_no"]).then_inc(loaded["slot_no"], 16)
            sp.wait_ge(loaded["ids"], 16)
            sp.wait_ge(ups_ready, 2 * (E1 - DENSE1))
            for b in range(B):
                subject = sp.value_load(ids_i[0:1, 2 * B + b:2 * B + b + 1], min_val=0, max_val=SUBJ - 1)
                sp.dma_start(subj_w[:, b, :], dram["subj_w"][bass.ds(subject, 1), :, :].rearrange("a h o -> (a h) o")
                             ).then_inc(subj_loaded, 16)
            sp.wait_ge(ys_ready, E1 - DENSE1)
            for name in ("l3_gate", "l3_up"):
                sp.dma_start(packs[name][:, :], dram[name]).then_inc(loaded[name], 16)
            out_v = out.rearrange("b s c -> (b s) c").rearrange("(t p) c -> p t c", p=P)
            for h in range(HALVES):
                sp.wait_ge(y3_used, 2 * E3 + h + 1)
                sp.dma_start(out_v[:, 4 * h:4 * h + 4, :], x_tok[:, 4 * h:4 * h + 4, :]).then_inc(stored, 16)
            sp.wait_ge(stored, 32)

        @block.gpsimd
        def _(pool):
            steps = [0]

            def chain(ins):
                steps[0] += 1
                ins.then_inc(pool_step, 1)
                pool.wait_ge(pool_step, steps[0])

            pool.wait_ge(loaded["early"], 16)
            nc.gpsimd.tensor_copy(far_h[:, :], field("early", "far")[0:LANGS, :]).then_inc(far_ready, 1)
            nc.gpsimd.memset(ones_f[:, :], 1.0)
            pool.wait_ge(lang_ready, 2)
            nc.gpsimd.tensor_copy(lang_f[:, :].rearrange("l (b s) -> l b s", s=S), bc(lang_b[:, :], 2, S)
                                  ).then_inc(langf_ready, 1)
            pool.wait_ge(loaded["consts"], 16)
            pool.wait_ge(loaded["types"], 16)
            for dst, name in ((tri_batch_h, "tri_batch"), (ones_batch_h, "ones_batch"), (tri_all_h, "tri_all"),
                              (same_expert_h, "same_expert")):
                nc.gpsimd.tensor_copy(dst[:, :], field("consts", name))
            nc.gpsimd.tensor_scalar(subj_b[:, :], ids_f[0:SUBJ, 2 * B:3 * B], pidx[0:SUBJ, :], None, ALU.is_equal)
            chain(nc.gpsimd.tensor_copy(types_f[:, :], types_i[:, :]))
            chain(nc.gpsimd.tensor_scalar(type_sel[:, 0, :], types_f[:, :], 0.0, None, ALU.is_equal))
            chain(nc.gpsimd.tensor_scalar(type_sel[:, 1, :], types_f[:, :], 1.0, None, ALU.is_equal))
            chain(nc.gpsimd.tensor_tensor(type_sel[:, 2, :], type_sel[:, 0, :], type_sel[:, 1, :], ALU.add))
            chain(nc.gpsimd.tensor_scalar(type_sel[:, 2, :], type_sel[:, 2, :], -1.0, 1.0, ALU.mult, ALU.add))
            for k, name in enumerate(("mask_pre", "mask_post", "mask_cloze")):
                sel = bc(type_sel[:, k, :], 2, S)
                mask = bc(field("consts", name), 1, TILES)
                count = field("consts", "counts")[:, k:k + 1]
                if k == 0:
                    nc.gpsimd.tensor_tensor(mask_add[:, :, :], mask, sel, ALU.mult)
                    chain(nc.gpsimd.tensor_scalar(seen[:, :], type_sel[:, k, :], count, None, ALU.mult))
                    continue
                nc.gpsimd.tensor_tensor(mask_tmp[:, :, :], mask, sel, ALU.mult)
                chain(nc.gpsimd.tensor_scalar(seen_tmp[:, :], type_sel[:, k, :], count, None, ALU.mult))
                nc.gpsimd.tensor_tensor(mask_add[:, :, :], mask_add[:, :, :], mask_tmp[:, :, :], ALU.add)
                chain(nc.gpsimd.tensor_tensor(seen[:, :], seen[:, :], seen_tmp[:, :], ALU.add))
            nc.gpsimd.memset(mask_tmp[:, :, :], 0.0).then_inc(consts_ready, 1)
            chain(nc.gpsimd.memset(decay[:, :], 1.0))
            chain(nc.gpsimd.memset(decay[:, :].rearrange("p (b s) -> p b s", s=S)[:, :, 0:1], 0.0))
            pool.wait_ge(alpha_ready, 1)
            nc.gpsimd.tensor_scalar(decay[:, :], decay[:, :], alpha[:, 1:2], None, ALU.mult).then_inc(decay_ready, 1)

            def split(buf, at, weights):
                n = weights.shape[-1]
                chain(nc.gpsimd.tensor_copy(w_hi[:, buf, at:at + n], weights))
                return nc.gpsimd.tensor_tensor(w_lo[:, buf, at:at + n], weights,
                                               w_hi[:, buf, at:at + n].bitcast(F32), ALU.subtract)

            def split1(e):
                if e == 0:
                    pool.wait_ge(loaded["l1_w1"], 16)
                    pool.wait_ge(adapt_ready, 2)
                if 2 <= e < 2 + DENSE1:
                    pool.wait_ge(up1_ready, (e - 1) * FCH1 * HALVES)
                elif e >= 2:
                    pool.wait_ge(ups_ready, 2 * (e - 1 - DENSE1))
                split(e % 2, 0, field("l1_w1", "w1")[:, e * FF1:(e + 1) * FF1]).then_inc(w_split, 1)

            def negated_split(dst, part, mask):
                chain(nc.gpsimd.tensor_copy(dst, part))
                chain(nc.gpsimd.tensor_scalar(dst, dst.bitcast(F32), mask, None, ALU.mult))
                return nc.gpsimd.tensor_tensor(dst, dst.bitcast(F32), part, ALU.subtract)

            def lags(g):
                if g == 0:
                    pool.wait_ge(lag0_ready, 1)
                    for k in range(1, LAG_GROUP):
                        chain(nc.gpsimd.tensor_scalar(lag_f[:, k, :], lag_f[:, k - 1, :], alpha[:, 0:1], None, ALU.mult))
                else:
                    chain(nc.gpsimd.tensor_scalar(lag_f[:, :, :], lag_f[:, :, :], alpha_group[:, :], None, ALU.mult))
                negated_split(lag_w[:, g * LAG_GROUP:(g + 1) * LAG_GROUP, :], lag_f[:, :, :],
                              field("consts", "lo_w")).then_inc(lagw_ready, 1)
                pool.wait_ge(lagw_ready, g + 1)

            split1(0)
            split1(1)
            for g in range(S // LAG_GROUP):
                lags(g)
            split1(2)
            for h in range(HALVES):
                tiles = slice(4 * h, 4 * h + 4)
                pool.wait_ge(ptokhi_ready, 2 * (h + 1))
                nc.gpsimd.tensor_tensor(parts[:, tiles, C:2 * C], ptok[:, tiles, :], parts[:, tiles, 0:C].bitcast(F32),
                                        ALU.subtract).then_inc(parts_ready, 1)
            pool.wait_ge(sig1_ready, 1)
            gate_hi = parts[:, :, 2 * C:2 * C + E1]
            chain(nc.gpsimd.tensor_copy(gate_hi, sig1[:, :, :]))
            nc.gpsimd.tensor_tensor(parts[:, :, 2 * C + E1:], sig1[:, :, :], gate_hi.bitcast(F32),
                                    ALU.subtract).then_inc(parts_ready, 1)
            pool.wait_ge(enough_ready, 9)
            nc.gpsimd.tensor_copy(sel_h[0:E1, :, :], bc(ident[0:E1, 0:E1], 2, P)).then_inc(parts_ready, 1)
            split1(3)
            for e in range(2 + DENSE1, E1):
                split1(e)
            pool.wait_ge(loaded["l2_all"], 16)
            pool.wait_ge(ysplit_ready, E1 - DENSE1)
            negated_split(v1_w[:, :], field("l2_all", "v1"), field("consts", "lo_w")).then_inc(lagw_ready, 1)
            for turn, i in enumerate(POOL_STEPS):
                if turn == 0:
                    continue
                lag = LAG_ORDER[i]
                pool.wait_ge(prod_ready, i + 1)
                if turn > 1:
                    pool.wait_ge(summed, turn - 1)
                nc.gpsimd.tensor_tensor(traces[:, lag * B:N], traces[:, lag * B:N], prod[:, turn % 3, 0:(S - lag) * B],
                                        ALU.add).then_inc(summed, 1)
            pool.wait_ge(summed, len(POOL_STEPS) - 1)
            pool.wait_ge(loaded["l3_gate"], 16)
            pool.wait_ge(loaded["l3_up"], 16)
            for e in range(E3):
                if e >= 2:
                    pool.wait_ge(u3_ready, (e - 1) * FCH3 * HALVES)
                split(e % 2, 0, field("l3_gate", "gate")[:, e * FF3:(e + 1) * FF3])
                split(e % 2, FF3, field("l3_up", "up")[:, e * FF3:(e + 1) * FF3]).then_inc(w_split, 1)

        @block.tensor
        def _(pe):
            mm, tr = nc.tensor.matmul, nc.tensor.transpose

            def mm_split(dst, buf, at, cols):
                w = slice(at, at + P)
                mm(dst, w_hi[:, buf, w], x_hi[:, cols], start=True, stop=False)
                mm(dst, w_hi[:, buf, w], x_lo[:, cols], start=False, stop=False)
                return mm(dst, w_lo[:, buf, w], x_hi[:, cols], start=False, stop=True)

            def keep_warm(reason, bank):
                for _ in range(FILLERS[reason]):
                    mm(psum[:, bank, 0:P], ones_h[:, :], ones_h[:, :], start=True, stop=True)

            pe.wait_ge(lang_ready, 1)
            keep_warm("first inputs", 7)
            pe.wait_ge(loaded["l0_w1"], 16)
            pe.wait_ge(far_ready, 1)
            w1, w2 = field("l0_w1", "w1"), field("l0_small", "w2")
            table = field("l0_small", "table")
            for h in range(HALVES):
                cols = slice(h * HALF, (h + 1) * HALF)
                pe.wait_ge(loaded[("x_ch", "x_ch2")[h]], 16)
                for k, rows in enumerate(LCH):
                    dst = psum[0:rows, 3 * h + k, :]
                    mm(dst, w1[:, k * P:k * P + rows], x_ch[:, cols], start=True, stop=False)
                    if h == 0 and k == 0:
                        pe.wait_ge(lang_ready, 3)
                    mm(dst, far_h[:, k * P:k * P + rows], lang_h[:, cols], start=False, stop=True).then_inc(ad_ready, 1)
            pe.wait_ge(loaded["l0_small"], 16)
            pe.wait_ge(langf_ready, 1)
            for h in range(HALVES):
                pe.wait_ge(adhid_ready, 3 * (h + 1))
                for t in range(4 * h, 4 * h + 4):
                    dst = psum[:, 6 + h, (t % 4) * C:(t % 4 + 1) * C]
                    tok = slice(t * P, (t + 1) * P)
                    for k, rows in enumerate(LCH):
                        mm(dst, ad_hid[0:rows, k, tok], w2[0:rows, k * C:(k + 1) * C], start=(k == 0), stop=False)
                    last = mm(dst, lang_f[:, tok], table[0:LANGS, 0:C], start=False, stop=True)
                last.then_inc(adapt_ready, 1)
            for t in range(TILES):
                last = mm(psum[:, t // 2, (t % 2) * 2 * C:(t % 2 + 1) * 2 * C], lang_f[:, t * P:(t + 1) * P],
                          table[0:LANGS, C:3 * C], start=True, stop=True)
                if t % 4 == 3:
                    last.then_inc(affine_ready, 1)
            pe.wait_ge(loaded["consts"], 16)
            pe.wait_ge(blw_ready, 1)
            tr(psum[:, 5, 0:C], bl[:, :], ident).then_inc(blt_ready, 1)
            keep_warm("layer 0 norm", 4)
            for h in range(HALVES):
                pe.wait_ge(norm_ready, h + 1)
                if h == 1:
                    pe.wait_ge(lag0_ready, 1)
                for t in range(4 * h, 4 * h + 4):
                    last = tr(psum[:, 4 + h, (t % 4) * P:(t % 4 + 1) * P], c0[:, t, :], ident)
                last.then_inc(normt_ready, 1)
            for t in range(TILES):
                if t % 4 == 0:
                    pe.wait_ge(normch_ready, t // 4 + 1)
                last = mm(psum[:, 6, t * E0:(t + 1) * E0], c0_ch[:, t * P:(t + 1) * P], field("l0_small", "router"),
                          start=True, stop=True)
            last.then_inc(lg_ready, 1)
            keep_warm("expert choice", 0)
            pe.wait_ge(consts_ready, 1)
            pe.wait_ge(choice_ready, 2)
            mm(psum[:, 7, 0:P], tri_batch_h[:, :], oh1_h[:, :], start=True, stop=True)
            mm(psum[:, 7, P:2 * P], ones_batch_h[:, :], oh1_h[:, :], start=True, stop=False)
            mm(psum[:, 7, P:2 * P], tri_batch_h[:, :], oh2_h[:, :], start=False, stop=True).then_inc(rank_ready, 1)
            keep_warm("dispatch", 0)
            pe.wait_ge(disp_ready, 1)
            for t in range(TILES):
                last = mm(psum[:, t // 2, (t % 2) * BPT * SLOTS:(t % 2 + 1) * BPT * SLOTS], c0[:, t, :],
                          disp[:, t, :, :, :].rearrange("p i e c -> p (i e c)"), start=True, stop=True)
                if t % 2 == 1:
                    last.then_inc(gather_ready, 1)
            pe.wait_ge(comb_ready, 1)
            for t in range(TILES):
                last = tr(psum[:, 4 + t // 4, (t % 4) * P:(t % 4 + 1) * P],
                          comb[:, t, :, :, :].rearrange("p a e c -> p (a e c)"), ident)
                if t % 4 == 3:
                    last.then_inc(combt_ready, 1)
            pe.wait_ge(loaded["l0_gatefc"], 16)
            pe.wait_ge(slotin_act, 2)
            pe.wait_ge(slotin_dve, 2)
            for e in range(E0):
                bank = (6, 7, 4, 5)[e // 4]
                if e == 8:
                    pe.wait_ge(combt_used, 2)
                last = mm(psum[:, bank, (e % 4) * P:(e % 4 + 1) * P],
                          field("l0_gatefc", "gatefc")[:, e * P:(e + 1) * P],
                          slot_in[:, e, :, :, :].rearrange("p t i c -> p (t i c)"), start=True, stop=True)
                if e % 4 == 3:
                    last.then_inc(gatefc_ready, 1)
            pe.wait_ge(loaded["l0_proj"], 16)
            for e in range(E0):
                if e % 4 == 0:
                    pe.wait_ge(hid0_ready, e // 4 + 1)
                last = mm(psum[:, e // 4, (e % 4) * P:(e % 4 + 1) * P],
                          field("l0_proj", "proj")[0:H0, e * C:(e + 1) * C], hid0[:, e * P:(e + 1) * P],
                          start=True, stop=True)
                if e % 4 == 3:
                    last.then_inc(proj_ready, 1)
            pe.wait_ge(slotch_act, 2)
            pe.wait_ge(slotch_dve, 2)
            pairs = slot_ch[:, :, :, :, :].rearrange("p t (j a) e c -> p (t j) (a e c)", a=2)
            for q in range(B // 2):
                last = tr(psum[:, 4 + q // 4, (q % 4) * P:(q % 4 + 1) * P], pairs[:, q, :], ident)
                if q % 4 == 3:
                    last.then_inc(slott_ready, 1)
            pe.wait_ge(slotout_act, 2)
            pe.wait_ge(slotout_dve, 2)
            for q in range(B // 2):
                last = mm(psum[:, q // 8, (q % 8) * 2 * S:(q % 8 + 1) * 2 * S], slot_out[:, q, :],
                          comb_t[:, q // 2, (q % 2) * 2 * S:(q % 2 + 1) * 2 * S], start=True, stop=True)
                if q % 8 == 7:
                    last.then_inc(y0_ready, 1)

            for t in range(TILES):
                if t % 4 == 0:
                    pe.wait_ge(x1_ready, t // 4 + 1)
                last = tr(psum[:, 2 + t // 4, (t % 4) * C:(t % 4 + 1) * C], x_ch[:, t * P:(t + 1) * P], ident)
                if t % 4 == 3:
                    last.then_inc(xtok_pre, 1)
            pe.wait_ge(loaded["l1_small"], 16)
            for h in range(HALVES):
                mm(psum[0:ADIM, 4 + h, :], field("l1_small", "w1c"), x_ch[:, h * HALF:(h + 1) * HALF],
                   start=True, stop=True).then_inc(attn_ready, 1)
            for t in range(TILES):
                if t % 4 == 0:
                    pe.wait_ge(attn_done, t // 4 + 1)
                last = mm(psum[:, 6, t:t + 1], attn[:, t * P:(t + 1) * P], field("l1_small", "v")[0:ADIM, :],
                          start=True, stop=True)
            last.then_inc(score_ready, 1)
            pe.wait_ge(scored_ready, 1)
            mm(psum[:, 7, 0:TILES * S], field("consts", "ones_batch"), score_d[:, :, :].rearrange("p t s -> p (t s)"),
               start=True, stop=True).then_inc(spread_ready, 1)
            keep_warm("softmax", 0)
            pe.wait_ge(xtok_ready, 2)
            for t in range(TILES):
                if t % 4 == 0:
                    pe.wait_ge(softt_ready, t // 4 + 1)
                last = mm(psum[:, t // 4, (t % 4) * P:(t % 4 + 1) * P], x_tok[:, t, :],
                          soft_t[:, t, :, :].rearrange("p i s -> p (i s)"), start=True, stop=True)
                if t % 4 == 3:
                    last.then_inc(pooled_ready, 1)

            for h in range(HALVES):
                pe.wait_ge((poolch_act, poolch_dve)[h], 1)
                mm(psum[:, 4 + h, :], field("l1_small", "router"), pool_ch[:, h * HALF:(h + 1) * HALF],
                   start=True, stop=True).then_inc(lrow_ready, 1)

            units = [(e, k, h) for e in range(DENSE1) for k in range(FCH1) for h in range(HALVES)]
            UNITS = FCH1 * HALVES

            def up1(u):
                e, k, h = units[u]
                if u >= 3:
                    pe.wait_ge(hid1_ready, u - 2)
                if k == 0 and h == 0:
                    pe.wait_ge(w_split, e + 1)
                mm_split(psum[:, u % 3, :], e % 2, k * P, slice(h * HALF, (h + 1) * HALF)).then_inc(up1_ready, 1)

            def down1(e, h, pair):
                bank = (3 if e == 0 else 0) + h
                if pair == 0:
                    pe.wait_ge(hid1_ready, (e + 1) * UNITS)
                for t in range(4 * h + 2 * pair, 4 * h + 2 * pair + 2):
                    for k in range(FCH1):
                        at = (e * FCH1 + k) * C
                        last = mm(psum[:, bank, (t % 4) * C:(t % 4 + 1) * C], hid[:, e, k, t * P:(t + 1) * P],
                                  field("l1_w2", "w2")[:, at:at + C], start=(k == 0), stop=(k == FCH1 - 1))
                if pair == 1:
                    last.then_inc(y1_ready, 1)

            pe.wait_ge(xhi_ready, 2)
            pe.wait_ge(xlo_ready, 2)
            up1(0)
            pe.wait_ge(lrow_done, 2)
            for t in range(TILES):
                last = tr(psum[:, 6, t * E1:(t + 1) * E1], lrow[0:E1, t * P:(t + 1) * P], ident[0:E1, 0:E1])
            last.then_inc(ltok_ready, 1)
            up1(1)
            pe.wait_ge(ltok_done, 1)
            for r in range(ROUNDS):
                pe.wait_ge(enough_ready, r + 1)
                mm(psum[:, 6, 0:1], same_expert_h[:, :], enough_h[:, :], start=True, stop=True).then_inc(count_ready, 1)
                if r < 4:
                    for u in range(3 * r + 2, 3 * r + 5):
                        up1(u)
                elif r == 4:
                    up1(14)
                    up1(15)
                    pe.wait_ge(loaded["l1_w2"], 16)
                else:
                    if r == 5:
                        for t in range(TILES):
                            last = tr(psum[:, (5, 7)[t // 4], (t % 4) * P:(t % 4 + 1) * P],
                                      pool_ch[:, t * P:(t + 1) * P], ident)
                            if t % 4 == 3:
                                last.then_inc(ptokt_ready, 1)
                    down1(0, (r - 5) // 2, (r - 5) % 2)
            pe.wait_ge(enough_ready, 9)
            mm(psum[:, 6, 0:2 * E1], ones_f[0:E1, :], thr_d[:, :, :].rearrange("p a e -> p (a e)"), start=True,
               stop=True).then_inc(count_ready, 1)
            down1(0, 1, 1)
            def ranks(bank, flags_h):
                mm(psum[:, bank, 0:TILES * E1], tri_all_h[:, :], flags_h[:, :], start=True, stop=False)
                for t in range(TILES - 1):
                    last = mm(psum[:, bank, (t + 1) * E1:TILES * E1].rearrange("p (a e) -> p a e", e=E1),
                              ones_h[:, :], bc(flags_h[:, t * E1:(t + 1) * E1], 1, TILES - 1 - t), start=False,
                              stop=(t == TILES - 2))
                return last

            pe.wait_ge(tied_ready, 1)
            pe.wait_ge(ptokhi_ready, 4)
            ranks(7, tied_h)
            for t in range(TILES):
                last = mm(psum[:, 7, HALF - E1:HALF], ones_h[:, :], sure_h[:, t, :], start=(t == 0),
                          stop=(t == TILES - 1))
            last.then_inc(rank1_ready, 1)
            down1(1, 0, 0)
            pe.wait_ge(chosen_ready, 1)
            ranks(6, chosen_h).then_inc(rank1_ready, 1)
            down1(1, 0, 1)
            pe.wait_ge(pos_ready, 1)
            for t in range(TILES):
                last = tr(psum[0:E1, 5 + t // 4, (t % 4) * P:(t % 4 + 1) * P], pos[:, t, :], ident)
                if t % 4 == 3:
                    last.then_inc(experts_t, 1)
            down1(1, 1, 0)
            down1(1, 1, 1)
            pe.wait_ge(gate1_ready, 1)
            for t in range(TILES):
                if t == 4:
                    pe.wait_ge(experts_done, 1)
                last = tr(psum[0:E1, (7, 5)[t // 4], (t % 4) * P:(t % 4 + 1) * P], gate1[:, t, :], ident)
                if t % 4 == 3:
                    last.then_inc(experts_t, 1)

            def spread_slots(n):
                e = DENSE1 + n
                if n == 0:
                    pe.wait_ge(parts_ready, 4)
                    pe.wait_ge(experts_done, 2)
                else:
                    pe.wait_ge(put_ready, 2 * n)
                for h in range(HALVES):
                    if n == 0 and h == 1:
                        pe.wait_ge(experts_done, 3)
                    mm(psum[:, 6 + h, :], sel_h[0:E1, e, :], pos_t[0:E1, h * HALF:(h + 1) * HALF], start=True,
                       stop=True).then_inc(posrow_ready, 1)

            def gather1(n):
                pe.wait_ge(pick_ready, n + 1)
                if n == 0:
                    pe.wait_ge(parts_ready, 3)
                else:
                    pe.wait_ge(xslots_ready, SLOT_TILES * n)
                    if n >= 2:
                        pe.wait_ge(ysplit_ready, n - 1)
                for s in range(SLOT_TILES):
                    if n == 0 and s == 1:
                        pe.wait_ge(experts_done, 4)
                    for t in range(TILES):
                        last = mm(psum[:, SLOT_BANKS[s], 0:2 * C + 2 * E1], pick1[n % 2][:, t, s * P:(s + 1) * P],
                                  parts[:, t, :], start=(t == 0), stop=(t == TILES - 1))
                    last.then_inc(xs_gathered, 1)

            def turn_slots(n):
                if n == 0:
                    pe.wait_ge(y1_used, 2)
                else:
                    pe.wait_ge(hids_ready, FCH1 * n)
                for part in range(2):
                    for s in range(SLOT_TILES):
                        if part == 0:
                            pe.wait_ge(xslots_ready, SLOT_TILES * n + s + 1)
                        last = tr(psum[:, 3 + part, s * P:(s + 1) * P], x_slots[:, s, part * C:(part + 1) * C], ident)
                    last.then_inc(xst_ready, 1)

            def ups1(n):
                e = DENSE1 + n
                pe.wait_ge(w_split, e + 1)
                pe.wait_ge(xs_ready, 2 * n + 1)
                if n == 0:
                    pe.wait_ge(y1_used, 2)
                for k in range(FCH1):
                    if k % 2 == 0 and n >= 1:
                        pe.wait_ge(hids_ready, FCH1 * (n - 1) + k + 2)
                    dst = psum[:, 3 + k // 2, (k % 2) * TOP1:(k % 2 + 1) * TOP1]
                    w = slice(k * P, (k + 1) * P)
                    mm(dst, w_lo[:, e % 2, w], x_s[:, 0, :], start=True, stop=False)
                    mm(dst, w_hi[:, e % 2, w], x_s[:, 0, :], start=False, stop=False)
                    if k == 0:
                        pe.wait_ge(xs_ready, 2 * n + 2)
                    last = mm(dst, w_hi[:, e % 2, w], x_s[:, 1, :], start=False, stop=True)
                    if k % 2 == 1:
                        last.then_inc(ups_ready, 1)

            def downs1(n):
                e = DENSE1 + n
                if n >= 1:
                    pe.wait_ge(ysplit_ready, n)
                pe.wait_ge(hids_ready, FCH1 * (n + 1))
                for s in range(SLOT_TILES):
                    if n + 1 < E1 - DENSE1:
                        pe.wait_ge(xslots_ready, SLOT_TILES * (n + 1) + s + 1)
                    for k in range(FCH1):
                        at = (e * FCH1 + k) * C
                        last = mm(psum[:, SLOT_BANKS[s], OUT1:OUT1 + C], hid_s[:, k, s * P:(s + 1) * P],
                                  field("l1_w2", "w2")[:, at:at + C], start=(k == 0), stop=(k == FCH1 - 1))
                last.then_inc(ys_ready, 1)

            def scatter1(n, h):
                if h == 0:
                    pe.wait_ge(ysplit_ready, n + 1)
                    pe.wait_ge(put_ready, 2 * (n + 1))
                for s in range(SLOT_TILES):
                    for part, y in enumerate((y_hi, y_lo)):
                        last = mm(psum[:, h, :], y[:, s, :], put1[n % 2][:, s, h * HALF:(h + 1) * HALF],
                                  start=(n == 0 and h == 1 and s == 0 and part == 0),
                                  stop=(n == E1 - DENSE1 - 1 and s == SLOT_TILES - 1 and part == 1))
                if n == E1 - DENSE1 - 1:
                    last.then_inc(x2t_ready, 1)
                elif h == 1:
                    last.then_inc(put_used, 1)

            pe.wait_ge(loaded["l2_all"], 16)
            def others1(h):
                if h == 0:
                    pe.wait_ge(y1_used, 4)
                mm(psum[:, h, :], field("l1_small", "b2")[0:E1, :], gate1_t[:, h * HALF:(h + 1) * HALF],
                   start=(h == 0), stop=False)
                for t in range(4 * h, 4 * h + 4):
                    mm(psum[:, h, (t % 4) * P:(t % 4 + 1) * P], x_tok[:, t, :], ident, start=False, stop=False)

            SPARSE1 = E1 - DENSE1
            spread_slots(0)
            for n in range(SPARSE1):
                gather1(n)
                if n == 1:
                    others1(0)
                if n >= 1:
                    downs1(n - 1)
                turn_slots(n)
                if n + 1 < SPARSE1:
                    spread_slots(n + 1)
                ups1(n)
                if n >= 1:
                    scatter1(n - 1, 0)
                    scatter1(n - 1, 1)
            downs1(SPARSE1 - 1)
            others1(1)
            for h in range(HALVES):
                scatter1(SPARSE1 - 1, h)

            l2 = lambda name: field("l2_all", name)
            halves = [slice(h * HALF, (h + 1) * HALF) for h in range(HALVES)]
            for h, cols in enumerate(halves):
                pe.wait_ge(x2ch_ready, h + 1)
                mm(psum[0:HN2, 4 + h, :], l2("wn1"), x_ch[:, cols], start=True, stop=True).then_inc(net_pre, 1)
            for h, cols in enumerate(halves):
                mm(psum[:, 2 + h, :], l2("wsoma"), x_ch[:, cols], start=True, stop=True).then_inc(soma_pre, 1)
            for h, cols in enumerate(halves):
                pe.wait_ge(net_ready, h + 1)
                mm(psum[:, 6 + h, :], l2("wn2")[0:HN2, :], net[:, cols], start=True, stop=True).then_inc(mod_pre, 1)
            pe.wait_ge(ctx_ready, 1)
            for h, cols in enumerate(halves):
                mm(psum[:, h, :], l2("wg_x"), x_ch[:, cols], start=True, stop=False)
                mm(psum[:, h, :], l2("wg_ctx"), ctx_ch[:, cols], start=False, stop=True).then_inc(wg_pre, 1)
            pe.wait_ge(mod_ready, 2)
            pe.wait_ge(wg_ready, 2)
            pe.wait_ge(soma_ready, 2)
            pe.wait_ge(lagw_ready, S // LAG_GROUP)
            def add_step(i):
                turn = TENSOR_STEPS.index(i)
                first, final = turn == 0, i == TENSOR_STEPS[-1]
                start = 0 if first else LAG_ORDER[i] * B
                pe.wait_ge(prod_ready, i + 1)
                for h in range(HALVES):
                    at = max(start, h * HALF)
                    if at < (h + 1) * HALF:
                        last = mm(psum[:, 6 + h, at - h * HALF:HALF], ident,
                                  prod_t[:, turn % 2, at - start:(h + 1) * HALF - start], start=first, stop=final)
                last.then_inc(added, 1)

            for i, lag in enumerate(LAG_ORDER):
                n = (S - lag) * B
                if i >= 3:
                    pe.wait_ge(prod_ready, i - 2)
                for at in range(0, n, HALF):
                    end = min(n, at + HALF)
                    last = mm(psum[:, 2 * (i % 3) + at // HALF, 0:end - at], lag_w[:, lag, :], mod_w[:, at:end],
                              start=True, stop=True)
                last.then_inc(lag_ready, 1)
                if i - 2 in TENSOR_STEPS:
                    add_step(i - 2)
            pe.wait_ge(prod_ready, S)
            keep_warm("sum over lags", 0)
            for h, cols in enumerate(halves):
                pe.wait_ge(temporal_ready, h + 1)
                mm(psum[:, h, :].rearrange("p (s b) -> p s b", s=S), l2("wtemp"), batch_half(temporal, h),
                   start=True, stop=True).then_inc(wg_pre, 1)
            for h in range(HALVES):
                pe.wait_ge(sg_ready, h + 1)
                for t in range(4 * h, 4 * h + 4):
                    last = mm(psum[:, 2 + h, (t % 4) * C:(t % 4 + 1) * C], soma[:, t * P:(t + 1) * P], l2("wout"),
                              start=True, stop=True)
                last.then_inc(out2_ready, 1)
            keep_warm("layer 2 norm", 0)
            for h in range(HALVES):
                if h == 0:
                    pe.wait_ge(norm_ready, 3)
                else:
                    pe.wait_ge(std_ready, 5)
                for t in range(4 * h, 4 * h + 4):
                    last = tr(psum[:, 4 + h, (t % 4) * P:(t % 4 + 1) * P], ynorm[:, t, :], ident)
                last.then_inc(normt_ready, 1)
            for h, cols in enumerate(halves):
                pe.wait_ge(normch_ready, h + 3)
                mm(psum[:, 6 + h, :], l2("u1"), y_ch[:, cols], start=True, stop=True).then_inc(low_pre, 1)
            pe.wait_ge(lagw_ready, S // LAG_GROUP + 1)
            for u in range(HALVES * FCH2):
                h, k = u // FCH2, u % FCH2
                if u % FCH2 == 0:
                    pe.wait_ge(low_ready, h + 1)
                if u >= 4:
                    pe.wait_ge(ff2_ready, u - 3)
                mm(psum[:, u % 4, :], v1_w[:, k * P:(k + 1) * P], low_w[:, halves[h]], start=True, stop=True
                   ).then_inc(ff2_pre, 1)
            for h, cols in enumerate(halves):
                for k in range(FCH2):
                    pe.wait_ge(ff2_ready, h * FCH2 + k + 1)
                    last = mm(psum[k * RK2:(k + 1) * RK2, 4 + h, :], l2("u2")[:, k * RK2:(k + 1) * RK2],
                              hid[:, 0, k, cols], start=True, stop=True, tile_position=(0, k * RK2))
                last.then_inc(low_pre, 1)
            for h, cols in enumerate(halves):
                pe.wait_ge(low2_ready, h + 1)
                mm(psum[:, 6 + h, :], l2("v2"), low2[:, cols], start=True, stop=True).then_inc(y2_ready, 1)

            pe.wait_ge(subj_loaded, 16 * B)
            pe.wait_ge(loaded["l3_small"], 16)
            mm(psum[:, 2, 0:B], field("l3_small", "cbias")[0:SUBJ, :], subj_b[:, :], start=True, stop=True)
            for b in range(B):
                if b % 16 == 0:
                    pe.wait_ge(x3_ready, b // 16 + 1)
                rows = slice((b % BPT) * S, (b % BPT + 1) * S)
                t = b // BPT
                last = mm(psum[rows, b // 16, (t % 4) * C:(t % 4 + 1) * C], x_ch[:, b * S:(b + 1) * S],
                          subj_w[:, b, :], start=True, stop=True, tile_position=(0, (b % BPT) * S))
                if b % 16 == 15:
                    last.then_inc(z_ready, 1)
            for h in range(HALVES):
                for t in range(4 * h, 4 * h + 4):
                    last = tr(psum[:, 6 + h, (t % 4) * P:(t % 4 + 1) * P], x_ch[:, t * P:(t + 1) * P], ident)
                last.then_inc(xtok_pre, 1)
            for h in range(HALVES):
                pe.wait_ge(ztok_ready, h + 1)
                for t in range(4 * h, 4 * h + 4):
                    last = tr(psum[:, 4 + h, (t % 4) * P:(t % 4 + 1) * P], z_tok[:, t, :], ident)
                last.then_inc(normt_ready, 1)
            for t in range(TILES):
                if t % 4 == 0:
                    pe.wait_ge(zch_ready, t // 4 + 1)
                last = mm(psum[:, 3, t * E3:(t + 1) * E3], z_ch[:, t * P:(t + 1) * P], field("l3_small", "router"),
                          start=True, stop=True)
            last.then_inc(lg_ready, 1)
            pe.wait_ge(loaded["l3_down"], 16)
            pe.wait_ge(xhi_ready, 4)
            pe.wait_ge(xlo_ready, 4)

            units3 = [(e, k, h) for e in range(E3) for k in range(FCH3) for h in range(HALVES)]
            UNITS3 = FCH3 * HALVES

            def up3(u):
                e, k, h = units3[u]
                if k == 0 and h == 0:
                    pe.wait_ge(w_split, e + 9)
                if u == 1:
                    pe.wait_ge(lg3_used, 1)
                if u >= 2:
                    pe.wait_ge(silu3_ready, u - 1)
                mm_split(psum[:, u % 2, :], e % 2, k * P, halves[h]).then_inc(g3_ready, 1)
                if u >= 2:
                    pe.wait_ge(hid3_ready, u - 1)
                mm_split(psum[:, 2 + u % 2, :], e % 2, FF3 + k * P, halves[h]).then_inc(u3_ready, 1)

            def down3(e, h):
                pe.wait_ge(hid3_ready, (e + 1) * UNITS3 - 1 + h)
                turn = e if e <= 1 else e + 1
                if turn >= 1:
                    pe.wait_ge(y3_used, 2 * (turn - 1) + h + 1)
                for t in range(4 * h, 4 * h + 4):
                    for k in range(FCH3):
                        at = (e * FCH3 + k) * C
                        last = mm(psum[:, 4 + h, (t % 4) * C:(t % 4 + 1) * C], hid[:, 0, (e % 2) * 2 + k, t * P:(t + 1) * P],
                                  field("l3_down", "down")[:, at:at + C], start=(k == 0), stop=(k == FCH3 - 1))
                last.then_inc(y3_ready, 1)

            for e in range(E3):
                for u in range(e * UNITS3, (e + 1) * UNITS3):
                    up3(u)
                if e == 1:
                    pe.wait_ge(gate3_ready, 1)
                    for t in range(TILES):
                        last = tr(psum[0:E3, 6 + t // 4, (t % 4) * P:(t % 4 + 1) * P], gate3[:, t, :], ident)
                        if t % 4 == 3:
                            last.then_inc(experts_t, 1)
                if e >= 1:
                    down3(e - 1, 0)
                    down3(e - 1, 1)
                if e == 2:
                    pe.wait_ge(experts_done, 6)
                    for h in range(HALVES):
                        pe.wait_ge(y3_used, 2 + h + 1)
                        for t in range(4 * h, 4 * h + 4):
                            last = mm(psum[:, 4 + h, (t % 4) * C:(t % 4 + 1) * C], gate3_t[:, t * P:(t + 1) * P],
                                      field("l3_small", "down_b")[0:E3, :], start=True, stop=True)
                        last.then_inc(y3_ready, 1)
            down3(E3 - 1, 0)
            down3(E3 - 1, 1)

        @block.scalar
        def _(act):
            act.wait_ge(loaded["l2_decay"], 16)
            nc.scalar.activation(tau_e[:, 0:1], field("l2_decay", "taus"), ACT.Exp)
            nc.scalar.activation(tau_e[:, 1:2], field("l2_decay", "tau_ctx"), ACT.Exp).then_inc(exps2_ready, 1)
            act.wait_ge(blend_ready, 1)
            nc.scalar.activation(bl_e[:, :], bl[:, :], ACT.Exp).then_inc(exps2_ready, 1)
            for h in range(HALVES):
                for k, rows in enumerate(LCH):
                    act.wait_ge(ad_ready, 3 * h + k + 1)
                    nc.scalar.activation(ad_hid[0:rows, k, h * HALF:(h + 1) * HALF], psum[0:rows, 3 * h + k, :],
                                         ACT.Relu, bias=field("l0_w1", "b1")[0:rows, k:k + 1]
                                         ).then_inc(adhid_ready, 1)
            for h in range(HALVES):
                tiles = slice(4 * h, 4 * h + 4)
                act.wait_ge(var_ready, h + 1)
                nc.scalar.activation(std[:, tiles], bn_m[:, tiles, 1], ACT.Sqrt, bias=field("early", "eps")
                                     ).then_inc(std_ready, 1)
            act.wait_ge(blt_ready, 1)
            nc.scalar.activation(lag_f[:, 0, :], psum[:, 5, 0:C], ACT.Copy).then_inc(lag0_ready, 1)
            for h in range(HALVES):
                act.wait_ge(normt_ready, h + 1)
                nc.scalar.activation(c0_ch[:, h * HALF:(h + 1) * HALF], psum[:, 4 + h, :], ACT.Copy
                                     ).then_inc(normch_ready, 1)
            act.wait_ge(rest_ready, 1)
            nc.scalar.activation(ex[:, :, :], rest[:, :, :], ACT.Exp).then_inc(exp_ready, 1)
            for g in (0, 1):
                act.wait_ge(gather_ready, g + 1)
                nc.scalar.activation(slot_in[:, :, 2 * g:2 * g + 2, :, :].rearrange("p e t i c -> p e (t i) c"),
                                     psum[:, g, :].rearrange("p (b e c) -> p e b c", e=E0, c=CAP), ACT.Copy
                                     ).then_inc(slotin_act, 1)
            for h in range(HALVES):
                act.wait_ge(combt_ready, h + 1)
                nc.scalar.activation(comb_t[:, 4 * h:4 * h + 4, :],
                                     psum[:, 4 + h, :].rearrange("p (t q) -> p t q", q=P), ACT.Copy
                                     ).then_inc(combt_used, 1)
            for g in range(4):
                act.wait_ge(gatefc_ready, g + 1)
                nc.scalar.activation(silu0[:, g * HALF:(g + 1) * HALF], psum[0:H0, (6, 7, 4, 5)[g], :], ACT.Silu
                                     ).then_inc(silu_ready, 1)
            for g in (0, 1):
                act.wait_ge(proj_ready, g + 1)
                nc.scalar.activation(slot_ch[:, :, :, 4 * g:4 * g + 4, :].rearrange("p t i e c -> p (t i) e c"),
                                     psum[:, g, :].rearrange("p (e b c) -> p b e c", e=4, c=CAP), ACT.Copy
                                     ).then_inc(slotch_act, 1)
            for g in (0, 1):
                act.wait_ge(slott_ready, g + 1)
                nc.scalar.activation(slot_out[:, 4 * g:4 * g + 4, :],
                                     psum[:, 4 + g, :].rearrange("p (q c) -> p q c", c=C), ACT.Copy
                                     ).then_inc(slotout_act, 1)

            halves = [slice(h * HALF, (h + 1) * HALF) for h in range(HALVES)]
            for h in range(HALVES):
                act.wait_ge(xtok_pre, h + 1)
                nc.scalar.activation(x_tok[:, 4 * h:4 * h + 4, :], psum[:, 2 + h, :].rearrange("p (t c) -> p t c", c=C),
                                     ACT.Copy).then_inc(xtok_ready, 1)
            for h, cols in enumerate(halves):
                act.wait_ge(attn_ready, h + 1)
                nc.scalar.activation(attn[:, cols], psum[0:ADIM, 4 + h, :], ACT.Tanh,
                                     bias=field("l1_small", "b1c")[0:ADIM, :]).then_inc(attn_done, 1)
            act.wait_ge(soft_ready, 1)
            nc.scalar.activation(soft_e[:, :, :], soft[:, :, :], ACT.Exp).then_inc(softexp_ready, 1)
            act.wait_ge(pooled_ready, 1)
            nc.scalar.activation(pool_ch[:, halves[0]], psum[:, 0, :], ACT.Copy).then_inc(poolch_act, 1)
            for h, cols in enumerate(halves):
                act.wait_ge((poolch_act, poolch_dve)[h], 1)
                nc.scalar.activation(x_hi[:, cols], pool_ch[:, cols], ACT.Copy).then_inc(xhi_ready, 1)

            units = [(e, k, h) for e in range(DENSE1) for k in range(FCH1) for h in range(HALVES)]
            UNITS = FCH1 * HALVES
            act.wait_ge(ltok_done, 1)
            nc.scalar.activation(sig1[:, :, :], ltok[:, :, :], ACT.Sigmoid).then_inc(sig1_ready, 1)
            for u, (e, k, h) in enumerate(units):
                act.wait_ge(up1_ready, u + 1)
                nc.scalar.activation(hid[:, e, k, halves[h]], psum[:, u % 3, :], ACT.Gelu,
                                     bias=field("l1_small", "b1")[:, e * FCH1 + k:e * FCH1 + k + 1]
                                     ).then_inc(hid1_ready, 1)
            for h in range(HALVES):
                tiles = slice(4 * h, 4 * h + 4)
                src = psum[:, (5, 7)[h], :].rearrange("p (t c) -> p t c", c=C)
                act.wait_ge(ptokt_ready, h + 1)
                nc.scalar.activation(ptok[:, tiles, :], src, ACT.Copy).then_inc(ptokhi_ready, 1)
                nc.scalar.activation(parts[:, tiles, 0:C], src, ACT.Copy).then_inc(ptokhi_ready, 1)
            for h, cols in enumerate(halves):
                act.wait_ge(experts_t, h + 1)
                nc.scalar.activation(pos_t[0:E1, cols], psum[0:E1, 5 + h, :], ACT.Copy).then_inc(experts_done, 1)
            for h, cols in enumerate(halves):
                act.wait_ge(experts_t, h + 3)
                nc.scalar.activation(gate1_t[:, cols], psum[0:E1, (7, 5)[h], :], ACT.Copy).then_inc(experts_done, 1)
            for n in range(E1 - DENSE1):
                for s in range(SLOT_TILES):
                    act.wait_ge(xs_gathered, SLOT_TILES * n + s + 1)
                    if n >= 1:
                        act.wait_ge(xst_ready, 2 * n)
                        act.wait_ge(gates_read, n)
                    nc.scalar.activation(x_slots[:, s, :], psum[:, SLOT_BANKS[s], 0:2 * C + 2 * E1], ACT.Copy
                                         ).then_inc(xslots_ready, 1)
                if n >= 1:
                    act.wait_ge(ups_ready, 2 * n)
                else:
                    act.wait_ge(y1_ready, 2 * DENSE1)
                for part in range(2):
                    act.wait_ge(xst_ready, 2 * n + part + 1)
                    nc.scalar.activation(x_s[:, part, :], psum[:, 3 + part, 0:TOP1], ACT.Copy).then_inc(xs_ready, 1)
                for k in range(FCH1):
                    act.wait_ge(ups_ready, 2 * n + k // 2 + 1)
                    if k == 0 and n >= 1:
                        act.wait_ge(ys_ready, n)
                    at = (DENSE1 + n) * FCH1 + k
                    nc.scalar.activation(hid_s[:, k, :], psum[:, 3 + k // 2, (k % 2) * TOP1:(k % 2 + 1) * TOP1],
                                         ACT.Gelu, bias=field("l1_small", "b1")[:, at:at + 1]).then_inc(hids_ready, 1)

            l2 = lambda name: field("l2_all", name)
            for h, cols in enumerate(halves):
                act.wait_ge(x2t_ready, h + 1)
                nc.scalar.activation(x_ch[:, cols], psum[:, h, :], ACT.Copy).then_inc(x2ch_ready, 1)
            for h, cols in enumerate(halves):
                act.wait_ge(net_pre, h + 1)
                nc.scalar.activation(net[:, cols], psum[0:HN2, 4 + h, :], ACT.Gelu, bias=l2("bn1")[0:HN2, :]
                                     ).then_inc(net_ready, 1)
            for h, cols in enumerate(halves):
                act.wait_ge(soma_pre, h + 1)
                nc.scalar.activation(soma[:, cols], psum[:, 2 + h, :], ACT.Gelu, bias=l2("bsoma")
                                     ).then_inc(soma_ready, 1)
            for h, cols in enumerate(halves):
                act.wait_ge(mod_pre, h + 1)
                nc.scalar.activation(mod[:, cols], psum[:, 6 + h, :], ACT.Sigmoid, bias=l2("bn2")).then_inc(mod_sig, 1)
            for h, cols in enumerate(halves):
                act.wait_ge(wg_pre, h + 1)
                nc.scalar.activation(gated[:, cols], psum[:, h, :], ACT.Sigmoid, bias=l2("bg")).then_inc(wg_ready, 1)
            for h, cols in enumerate(halves):
                act.wait_ge(wg_pre, h + 3)
                nc.scalar.activation(tgate[:, cols].rearrange("p (b s) -> p s b", s=S),
                                     psum[:, h, :].rearrange("p (s b) -> p s b", s=S), ACT.Sigmoid, bias=l2("btemp")
                                     ).then_inc(wg_ready, 1)
            for h in range(HALVES):
                tiles = slice(4 * h, 4 * h + 4)
                act.wait_ge(var_ready, h + 3)
                nc.scalar.activation(std[:, tiles], bn_m[:, tiles, 1], ACT.Sqrt, bias=field("early", "eps")
                                     ).then_inc(std_ready, 1)
            act.wait_ge(affine_ready, 3)
            for t in range(4, TILES):
                last = nc.scalar.activation(ynorm[:, t, :], psum[:, 3, (t % 4) * C:(t % 4 + 1) * C], ACT.Identity,
                                            bias=bn_m[:, t, 0:1], scale=rstd[:, t:t + 1])
            last.then_inc(std_ready, 1)
            for h, cols in enumerate(halves):
                act.wait_ge(normt_ready, h + 3)
                nc.scalar.activation(y_ch[:, cols], psum[:, 4 + h, :], ACT.Identity, bias=l2("beta"), scale=l2("gamma")
                                     ).then_inc(normch_ready, 1)
            for u in range(HALVES * FCH2):
                h, k = u // FCH2, u % FCH2
                act.wait_ge(ff2_pre, u + 1)
                nc.scalar.activation(hid[:, 0, k, halves[h]], psum[:, u % 4, :], ACT.Gelu_apprx_tanh,
                                     bias=l2("b1")[:, k:k + 1]).then_inc(ff2_ready, 1)
            for h, cols in enumerate(halves):
                act.wait_ge(low_pre, h + 3)
                nc.scalar.activation(low2[:, cols], psum[:, 4 + h, :], ACT.Copy).then_inc(low2_ready, 1)

            for h in range(HALVES):
                act.wait_ge(z_ready, h + 1)
                nc.scalar.activation(z_tok[:, 4 * h:4 * h + 4, :], psum[:, h, :].rearrange("p (t c) -> p t c", c=C),
                                     ACT.Copy).then_inc(ztok_ready, 1)
            for h in range(HALVES):
                act.wait_ge(xtok_pre, h + 3)
                nc.scalar.activation(x_tok[:, 4 * h:4 * h + 4, :], psum[:, 6 + h, :].rearrange("p (t c) -> p t c", c=C),
                                     ACT.Copy).then_inc(xtok_ready, 1)
            for h, cols in enumerate(halves):
                act.wait_ge(zch_ready, h + 1)
                nc.scalar.activation(x_hi[:, cols], z_ch[:, cols], ACT.Copy).then_inc(xhi_ready, 1)
            units3 = [(e, k, h) for e in range(E3) for k in range(FCH3) for h in range(HALVES)]
            for u, (e, k, h) in enumerate(units3):
                act.wait_ge(g3_ready, u + 1)
                if u >= 2:
                    act.wait_ge(hid3_ready, u - 1)
                nc.scalar.activation(silu3[:, u % 2, :], psum[:, u % 2, :], ACT.Silu,
                                     bias=field("l3_small", "gate_b")[:, e * FCH3 + k:e * FCH3 + k + 1]
                                     ).then_inc(silu3_ready, 1)
                if u == 1:
                    act.wait_ge(rest_ready, 2)
                    nc.scalar.activation(ex[:, :, 0:E3], rest[:, :, 0:E3], ACT.Exp).then_inc(exp_ready, 1)
                if u == 2 * FCH3 * HALVES - 1:
                    for a in range(2):
                        act.wait_ge(experts_t, a + 5)
                        nc.scalar.activation(gate3_t[:, halves[a]], psum[0:E3, 6 + a, :], ACT.Copy
                                             ).then_inc(experts_done, 1)

        @block.vector
        def _(dve):
            steps = [0]
            ts, tt = nc.vector.tensor_scalar, nc.vector.tensor_tensor
            stt, red = nc.vector.scalar_tensor_tensor, nc.vector.tensor_reduce

            def chain(ins):
                steps[0] += 1
                ins.then_inc(dve_step, 1)
                dve.wait_ge(dve_step, steps[0])

            def layer_stats(src, tiles=range(TILES)):
                for t in tiles:
                    last = nc.vector.bn_stats(bn_s[:, t, :], src(t))
                chain(last)
                for t in tiles:
                    last = nc.vector.bn_aggr(bn_m[:, t, :], bn_s[:, t, :])
                last.then_inc(var_ready, 1)

            nc.vector.memset(ones_h[:, :], 1.0).then_inc(lang_ready, 1)
            dve.wait_ge(loaded["ids"], 16)
            dve.wait_ge(loaded["early"], 16)
            chain(nc.vector.tensor_copy(ids_f[:, :], ids_i[:, :]))
            ts(lang_b[:, :], ids_f[0:LANGS, 0:B], pidx[0:LANGS, :], None, ALU.is_equal).then_inc(lang_ready, 1)
            dve.wait_ge(lang_ready, 2)
            nc.vector.tensor_copy(lang_h[:, :].rearrange("l (b s) -> l b s", s=S), bc(lang_b[:, :], 2, S)
                                  ).then_inc(lang_ready, 1)

            dve.wait_ge(loaded["l2_decay"], 16)
            blend = field("l2_decay", "blend")
            chain(red(bl_max[:, :], blend, X_AXIS, ALU.max))
            ts(bl[:, :], blend, bl_max[:, :], None, ALU.subtract).then_inc(blend_ready, 1)
            dve.wait_ge(exps2_ready, 1)
            chain(ts(tau_e[:, :], tau_e[:, :], 1.0, None, ALU.add))
            chain(nc.vector.reciprocal(alpha[:, :], tau_e[:, :]))
            chain(tt(alpha_group[:, :], alpha[:, 0:1], alpha[:, 0:1], ALU.mult))
            tt(alpha_group[:, :], alpha_group[:, :], alpha_group[:, :], ALU.mult).then_inc(alpha_ready, 1)
            dve.wait_ge(exps2_ready, 2)
            chain(red(bl_sum[:, :], bl_e[:, 0:D2], X_AXIS, ALU.add))
            chain(nc.vector.reciprocal(bl_sum[:, :], bl_sum[:, :]))
            ts(bl[:, :], bl_e[:, :], bl_sum[:, :], None, ALU.mult).then_inc(blw_ready, 1)

            def affine0(h):
                tiles = slice(4 * h, 4 * h + 4)
                dve.wait_ge(affine_ready, h + 1)
                affine = psum[:, 2 * h:2 * h + 2, :].rearrange("p b (t a c) -> p (b t) a c", a=2, c=C)
                chain(tt(res0[:, tiles, :], affine[:, :, 0, :], res0[:, tiles, :], ALU.mult))
                tt(c0[:, tiles, :], affine[:, :, 1, :], res0[:, tiles, :], ALU.add).then_inc(norm_ready, 1)

            dve.wait_ge(loaded["x_tok"], 16)
            for h in range(HALVES):
                tiles = slice(4 * h, 4 * h + 4)
                dve.wait_ge(adapt_ready, h + 1)
                chain(tt(res0[:, tiles, :], psum[:, 6 + h, :].rearrange("p (t c) -> p t c", c=C), x_tok[:, tiles, :],
                         ALU.add))
                layer_stats(lambda t: res0[:, t, :], range(4 * h, 4 * h + 4))
                if h == 1:
                    affine0(0)
                dve.wait_ge(std_ready, h + 1)
                chain(nc.vector.reciprocal(rstd[:, tiles], std[:, tiles]))
                for t in range(4 * h, 4 * h + 4):
                    last = ts(res0[:, t, :], res0[:, t, :], bn_m[:, t, 0:1], rstd[:, t:t + 1], ALU.subtract, ALU.mult)
            chain(last)
            affine0(1)

            def first_best(src, best, onehot, iota, n):
                chain(red(best[:, :], src[:, :, 0:n], X_AXIS, ALU.max))
                chain(tt(eqm[:, :, 0:n], src[:, :, 0:n], bc(best[:, :], 2, n), ALU.is_equal))
                chain(tt(eqm[:, :, 0:n], eqm[:, :, 0:n], bc(iota, 1, TILES), ALU.mult))
                chain(red(pick[:, :], eqm[:, :, 0:n], X_AXIS, ALU.min))
                return tt(onehot[:, :, 0:n], bc(iota, 1, TILES), bc(pick[:, :], 2, n), ALU.is_equal)

            flat = "p t e -> p (t e)"
            iota16 = field("consts", "iota16")
            dve.wait_ge(lg_ready, 1)
            chain(nc.vector.tensor_copy(lg[:, :, :].rearrange(flat), psum[:, 6, 0:TILES * E0]))
            chain(first_best(lg, top1, oh1, iota16, E0))
            nc.vector.tensor_copy(oh1_h[:, :], oh1[:, :, :].rearrange(flat)).then_inc(choice_ready, 1)
            chain(stt(rest[:, :, :].rearrange(flat), oh1[:, :, :].rearrange(flat), NEG, lg[:, :, :].rearrange(flat),
                      ALU.mult, ALU.add))
            chain(first_best(rest, top2, oh2, iota16, E0))
            nc.vector.tensor_copy(oh2_h[:, :], oh2[:, :, :].rearrange(flat)).then_inc(choice_ready, 1)
            tt(rest[:, :, :], lg[:, :, :], bc(top1[:, :], 2, E0), ALU.subtract).then_inc(rest_ready, 1)
            dve.wait_ge(rank_ready, 1)
            rank = psum[:, 7, 0:2 * P].rearrange("p (a q) -> p a q", a=2)
            tt(posa[:, :, :].rearrange(flat), rank[:, 0, :], oh1[:, :, :].rearrange(flat), ALU.mult)
            chain(tt(posb[:, :, :].rearrange(flat), rank[:, 1, :], oh2[:, :, :].rearrange(flat), ALU.mult))
            chain(tt(posa[:, :, :], posa[:, :, :], posb[:, :, :], ALU.add))
            for i in range(BPT):
                last = ts(place[:, :, i, :], posa[:, :, :], field("consts", "batch_in_tile")[:, i:i + 1], None, ALU.mult)
            chain(last)
            for c in range(CAP):
                last = ts(disp[:, :, :, :, c].rearrange("p t i e -> p (t i e)"),
                          place[:, :, :, :].rearrange("p t i e -> p (t i e)"), float(c + 1), None, ALU.is_equal)
            last.then_inc(disp_ready, 1)
            dve.wait_ge(exp_ready, 1)
            chain(red(exsum[:, :], ex[:, :, :], X_AXIS, ALU.add))
            nc.vector.reciprocal(rsum[:, :], exsum[:, :])
            chain(tt(eqm[:, :, :], oh1[:, :, :], oh2[:, :, :], ALU.add))
            chain(tt(prob[:, :, :], ex[:, :, :], eqm[:, :, :], ALU.mult))
            chain(tt(prob[:, :, :], prob[:, :, :], bc(rsum[:, :], 2, E0), ALU.mult))
            for a in range(2):
                ts(prob_par[:, :, a, :], prob[:, :, :], field("consts", "parity")[:, a:a + 1], None, ALU.mult)
            chain(ts(posb[:, :, :], posa[:, :, :], float(CAP), None, ALU.min))
            for a in range(2):
                for c in range(CAP):
                    last = stt(comb[:, :, a, :, c], posb[:, :, :], float(c + 1), prob_par[:, :, a, :],
                               ALU.is_equal, ALU.mult)
            last.then_inc(comb_ready, 1)
            for g in (2, 3):
                dve.wait_ge(gather_ready, g + 1)
                nc.vector.tensor_copy(slot_in[:, :, 2 * g:2 * g + 2, :, :].rearrange("p e t i c -> p e (t i) c"),
                                      psum[:, g, :].rearrange("p (b e c) -> p e b c", e=E0, c=CAP)
                                      ).then_inc(slotin_dve, 1)
            for g in range(4):
                dve.wait_ge(silu_ready, g + 1)
                cols = slice(g * HALF, (g + 1) * HALF)
                tt(hid0[:, cols], psum[H0:2 * H0, (6, 7, 4, 5)[g], :], silu0[:, cols], ALU.mult).then_inc(hid0_ready, 1)
            for g in (2, 3):
                dve.wait_ge(proj_ready, g + 1)
                nc.vector.tensor_copy(slot_ch[:, :, :, 4 * g:4 * g + 4, :].rearrange("p t i e c -> p (t i) e c"),
                                      psum[:, g, :].rearrange("p (e b c) -> p b e c", e=4, c=CAP)
                                      ).then_inc(slotch_dve, 1)
            for g in (2, 3):
                dve.wait_ge(slott_ready, g + 1)
                nc.vector.tensor_copy(slot_out[:, 4 * g:4 * g + 4, :],
                                      psum[:, 4 + g, :].rearrange("p (q c) -> p q c", c=C)).then_inc(slotout_dve, 1)
            for h in range(HALVES):
                cols = slice(h * HALF, (h + 1) * HALF)
                dve.wait_ge(y0_ready, h + 1)
                tt(x_ch[:, cols], psum[:, h, :], x_ch[:, cols], ALU.add).then_inc(x1_ready, 1)

            dve.wait_ge(score_ready, 1)
            tt(score_d[:, :, :], bc(eye32, 1, TILES), bc(psum[:, 6, 0:TILES], 2, S), ALU.mult).then_inc(scored_ready, 1)
            dve.wait_ge(spread_ready, 1)
            chain(tt(soft[:, :, :], psum[:, 7, 0:TILES * S].rearrange("p (t s) -> p t s", s=S), mask_add[:, :, :],
                     ALU.add))
            chain(red(rmax[:, :], soft[:, :, :], X_AXIS, ALU.max))
            tt(soft[:, :, :], soft[:, :, :], bc(rmax[:, :], 2, S), ALU.subtract).then_inc(soft_ready, 1)
            dve.wait_ge(softexp_ready, 1)
            chain(red(rden[:, :], soft_e[:, :, :], X_AXIS, ALU.add))
            chain(tt(rden[:, :], rden[:, :], seen[:, :], ALU.mult))
            chain(nc.vector.reciprocal(rden[:, :], rden[:, :]))
            chain(tt(soft_e[:, :, :], soft_e[:, :, :], bc(rden[:, :], 2, S), ALU.mult))
            chain(nc.vector.transpose(soft[:, :, :].rearrange("p t s -> p (t s)"),
                                      soft_e[:, :, :].rearrange("p t s -> p (t s)")))
            for h in range(HALVES):
                tiles = slice(4 * h, 4 * h + 4)
                tt(soft_t[:, tiles, :, :], bc(soft[:, tiles, :], 2, BPT),
                   bc(bc(field("consts", "batch_in_tile"), 1, 4), 3, S), ALU.mult).then_inc(softt_ready, 1)
            dve.wait_ge(pooled_ready, 2)
            nc.vector.tensor_copy(pool_ch[:, HALF:2 * HALF], psum[:, 1, :]).then_inc(poolch_dve, 1)

            for h in range(HALVES):
                cols = slice(h * HALF, (h + 1) * HALF)
                dve.wait_ge(xhi_ready, h + 1)
                tt(x_lo[:, cols], pool_ch[:, cols], x_hi[:, cols].bitcast(F32), ALU.subtract).then_inc(xlo_ready, 1)
            nc.vector.memset(best_thr[:, :], -BOUND)
            for h in range(HALVES):
                dve.wait_ge(lrow_ready, h + 1)
                ts(lrow[:, h * HALF:(h + 1) * HALF], psum[:, 4 + h, :], -BOUND, None, ALU.max).then_inc(lrow_done, 1)
            dve.wait_ge(ltok_ready, 1)
            nc.vector.tensor_copy(ltok[:, :, :].rearrange(flat), psum[:, 6, 0:TILES * E1]).then_inc(ltok_done, 1)
            for r in range(ROUNDS):
                width = 2 * BOUND / 16.0 ** (r + 1)
                chain(tt(thr[:, :], best_thr[:, :], field("consts", "steps")[:, r:r + 1], ALU.add))
                chain(ts(above_row[:, :], lrow[:, :], thr[:, :], None, ALU.is_ge, ALU.add, accum_out=hits[:, :]))
                ts(enough_h[:, :], hits[:, :], float(TOP1), None, ALU.is_ge).then_inc(enough_ready, 1)
                dve.wait_ge(count_ready, r + 1)
                chain(stt(best_thr[:, :], psum[:, 6, 0:1], width, best_thr[:, :], ALU.mult, ALU.add))
            chain(ts(best_end[:, :], best_thr[:, :], width, None, ALU.add))
            eye8 = field("consts", "eye8")[0:E1, :]
            ts(thr_d[:, 0, :], eye8, best_thr[0:E1, :], None, ALU.mult)
            ts(thr_d[:, 1, :], eye8, best_end[0:E1, :], None, ALU.mult).then_inc(enough_ready, 1)
            dve.wait_ge(count_ready, 9)
            low_end = bc(psum[:, 6, 0:E1], 1, TILES)
            tt(sure[:, :, :], ltok[:, :, :], bc(psum[:, 6, E1:2 * E1], 1, TILES), ALU.is_ge)
            chain(tt(tied[:, :, :], ltok[:, :, :], low_end, ALU.is_gt))
            chain(tt(sure[:, :, :], sure[:, :, :], tied[:, :, :], ALU.mult))
            chain(tt(tied[:, :, :], ltok[:, :, :], low_end, ALU.is_ge))
            nc.vector.tensor_copy(sure_h[:, :, :], sure[:, :, :])
            chain(tt(tied[:, :, :], tied[:, :, :], sure[:, :, :], ALU.subtract))
            nc.vector.tensor_copy(tied_h[:, :], tied[:, :, :].rearrange(flat)).then_inc(tied_ready, 1)
            dve.wait_ge(rank1_ready, 1)
            chain(ts(room[:, :], psum[:, 7, HALF - E1:HALF], -1.0, float(TOP1), ALU.mult, ALU.add))
            chain(tt(chosen[:, :, :], psum[:, 7, 0:TILES * E1].rearrange("p (t e) -> p t e", e=E1),
                     bc(room[:, :], 1, TILES), ALU.is_le))
            chain(tt(chosen[:, :, :], chosen[:, :, :], tied[:, :, :], ALU.mult))
            chain(tt(chosen[:, :, :], chosen[:, :, :], sure[:, :, :], ALU.add))
            nc.vector.tensor_copy(chosen_h[:, :], chosen[:, :, :].rearrange(flat)).then_inc(chosen_ready, 1)
            dve.wait_ge(sig1_ready, 1)
            tt(gate1[:, :, :], chosen[:, :, :], sig1[:, :, :], ALU.mult).then_inc(gate1_ready, 1)
            dve.wait_ge(rank1_ready, 2)
            tt(pos[:, :, :].rearrange(flat), psum[:, 6, 0:TILES * E1], chosen[:, :, :].rearrange(flat), ALU.mult
               ).then_inc(pos_ready, 1)
            dve.wait_ge(pos_ready, 1)
            dve.wait_ge(gate1_ready, 1)

            def output1(e):
                for h in range(HALVES):
                    dve.wait_ge(y1_ready, 2 * e + h + 1)
                    if e >= 1:
                        dve.wait_ge(y1_used, 2 * (e - 1) + h + 1)
                    bank = (3 if e == 0 else 0) + h
                    for t in range(4 * h, 4 * h + 4):
                        last = stt(x_tok[:, t, :], psum[:, bank, (t % 4) * C:(t % 4 + 1) * C], gate1[:, t, e:e + 1],
                                   x_tok[:, t, :], ALU.mult, ALU.add)
                    last.then_inc(y1_used, 1)

            def make_pick(n):
                if n >= 2:
                    dve.wait_ge(xs_gathered, SLOT_TILES * (n - 1))
                for t in range(TILES):
                    last = ts(pick1[n % 2][:, t, :], slot_no, pos[:, t, DENSE1 + n:DENSE1 + n + 1], None, ALU.is_equal)
                last.then_inc(pick_ready, 1)

            def make_put(n):
                if n >= 2:
                    dve.wait_ge(put_used, n - 1)
                for h in range(HALVES):
                    dve.wait_ge(posrow_ready, 2 * n + h + 1)
                    for s in range(SLOT_TILES):
                        last = ts(put1[n % 2][:, s, h * HALF:(h + 1) * HALF], psum[:, 6 + h, :],
                                  field("consts", "slot_row")[:, s:s + 1], None, ALU.is_equal)
                    last.then_inc(put_ready, 1)

            def read_gates(n):
                dve.wait_ge(xslots_ready, SLOT_TILES * (n + 1))
                at = 2 * C + DENSE1 + n
                red(slot_gate[:, n % 2, :], x_slots[:, :, at:at + E1 + 1:E1], X_AXIS, ALU.add
                    ).then_inc(gates_read, 1)

            def gated_output(n):
                dve.wait_ge(ys_ready, n + 1)
                dve.wait_ge(gates_read, n + 1)
                if n >= 1:
                    dve.wait_ge(put_used, n)
                out1 = lambda s: psum[:, SLOT_BANKS[s], OUT1:OUT1 + C]
                gate = lambda s: slot_gate[:, n % 2, s:s + 1]
                for s in range(SLOT_TILES):
                    last = ts(y_hi[:, s, :], out1(s), gate(s), None, ALU.mult)
                chain(last)
                for s in range(SLOT_TILES):
                    last = stt(y_lo[:, s, :], out1(s), gate(s), y_hi[:, s, :].bitcast(F32), ALU.mult, ALU.subtract)
                last.then_inc(ysplit_ready, 1)

            dve.wait_ge(loaded["slot_no"], 16)
            make_pick(0)
            output1(0)
            make_pick(1)
            output1(1)
            make_put(0)
            read_gates(0)
            make_put(1)
            for n in range(E1 - DENSE1):
                if n + 1 < E1 - DENSE1:
                    read_gates(n + 1)
                gated_output(n)
                if n + 2 < E1 - DENSE1:
                    make_pick(n + 2)
                    make_put(n + 2)

            halves = [slice(h * HALF, (h + 1) * HALF) for h in range(HALVES)]
            dve.wait_ge(decay_ready, 1)
            dve.wait_ge(x2ch_ready, 2)
            nc.vector.tensor_tensor_scan(ctx_ch[:, :], decay[:, :], x_ch[:, :], 0.0, ALU.mult, ALU.add
                                         ).then_inc(ctx_ready, 1)
            by_step = lambda a: a[:, :].rearrange("p (s b) -> p b s", b=B)
            for h, cols in enumerate(halves):
                dve.wait_ge(mod_sig, h + 1)
                chain(ts(mod[:, cols], mod[:, cols], 0.5, None, ALU.add))
                chain(nc.vector.tensor_copy(mod_hi[:, cols], mod[:, cols]))
                stt(by_step(mod_w)[:, 16 * h:16 * (h + 1), :],
                    mod_hi[:, cols].bitcast(F32).rearrange("p (b s) -> p b s", s=S), field("consts", "lo_x"),
                    mod[:, cols].rearrange("p (b s) -> p b s", s=S), ALU.mult, ALU.subtract).then_inc(mod_ready, 1)
            dve.wait_ge(wg_ready, 2)
            chain(tt(by_step(gated_s), gated[:, :].rearrange("p (b s) -> p b s", s=S),
                     x_ch[:, :].rearrange("p (b s) -> p b s", s=S), ALU.mult))
            nc.vector.memset(prod_t[:, 0, 0:B], 0.0)
            nc.vector.memset(traces[:, 0:2 * B], 0.0)
            for i, lag in enumerate(LAG_ORDER):
                n = (S - lag) * B
                bank = 2 * (i % 3)
                dve.wait_ge(lag_ready, i + 1)
                if i in TENSOR_STEPS:
                    turn = TENSOR_STEPS.index(i)
                    dst = prod_t[:, turn % 2, B:N] if turn == 0 else prod_t[:, turn % 2, 0:n]
                    if turn >= 2:
                        dve.wait_ge(added, turn - 1)
                elif i == POOL_STEPS[0]:
                    dst = traces[:, lag * B:N]
                else:
                    turn = POOL_STEPS.index(i)
                    dst = prod[:, turn % 3, 0:n]
                    if turn >= 4:
                        dve.wait_ge(summed, turn - 3)
                tt(dst, psum[:, bank:bank + 2, :].rearrange("p a n -> p (a n)")[:, 0:n], gated_s[:, 0:n],
                   ALU.mult).then_inc(prod_ready, 1)
            dve.wait_ge(summed, len(POOL_STEPS) - 1)
            dve.wait_ge(added, len(TENSOR_STEPS))
            tensor_sum = psum[:, 6:8, :].rearrange("p a n -> p (a n)")
            for h in range(HALVES):
                tt(batch_half(temporal, h), batch_half(traces, h), batch_half(tensor_sum, h), ALU.add
                   ).then_inc(temporal_ready, 1)
            for h, cols in enumerate(halves):
                dve.wait_ge(wg_ready, h + 3)
                tt(soma[:, cols], soma[:, cols], tgate[:, cols], ALU.mult).then_inc(sg_ready, 1)
            out2 = lambda t: psum[:, 2 + t // 4, (t % 4) * C:(t % 4 + 1) * C]
            for h in range(HALVES):
                dve.wait_ge(out2_ready, h + 1)
                layer_stats(out2, range(4 * h, 4 * h + 4))
            dve.wait_ge(std_ready, 4)
            chain(nc.vector.reciprocal(rstd[:, :], std[:, :]))
            stt(bn_m[:, 4:TILES, 0], bn_m[:, 4:TILES, 0], -1.0, rstd[:, 4:TILES], ALU.mult, ALU.mult
                ).then_inc(affine_ready, 1)
            for t in range(4):
                last = ts(ynorm[:, t, :], out2(t), bn_m[:, t, 0:1], rstd[:, t:t + 1], ALU.subtract, ALU.mult)
            last.then_inc(norm_ready, 1)
            for h, cols in enumerate(halves):
                dve.wait_ge(low_pre, h + 1)
                chain(nc.vector.tensor_copy(low_hi[:, cols], psum[:, 6 + h, :]))
                stt(low_w[:, cols], low_hi[:, cols].bitcast(F32), field("consts", "lo_x"), psum[:, 6 + h, :], ALU.mult,
                    ALU.subtract).then_inc(low_ready, 1)
            for h, cols in enumerate(halves):
                dve.wait_ge(y2_ready, h + 1)
                stt(x_ch[:, cols], psum[:, 6 + h, :], field("l2_all", "b2"), x_ch[:, cols], ALU.add, ALU.add
                    ).then_inc(x3_ready, 1)

            dve.wait_ge(z_ready, 1)
            chain(nc.vector.tensor_copy(subj_bias[:, :], psum[:, 2, 0:B]))
            for h, cols in enumerate(halves):
                dve.wait_ge(normt_ready, h + 5)
                tt(z_ch[:, cols].rearrange("p (b s) -> p b s", s=S), psum[:, 4 + h, :].rearrange("p (b s) -> p b s", s=S),
                   bc(subj_bias[:, 16 * h:16 * (h + 1)], 2, S), ALU.add).then_inc(zch_ready, 1)
            for h, cols in enumerate(halves):
                dve.wait_ge(xhi_ready, h + 3)
                dve.wait_ge(zch_ready, h + 1)
                tt(x_lo[:, cols], z_ch[:, cols], x_hi[:, cols].bitcast(F32), ALU.subtract).then_inc(xlo_ready, 1)
            iota8 = field("consts", "iota8")
            n = E3

            def first3():
                dve.wait_ge(lg_ready, 2)
                nc.vector.tensor_copy(lg[:, :, 0:n], psum[:, 3, 0:TILES * n].rearrange("p (t e) -> p t e", e=n)
                                      ).then_inc(lg3_used, 1)
                dve.wait_ge(lg3_used, 1)
                chain(first_best(lg, top1, oh1, iota8, n))

            def second3():
                chain(stt(rest[:, :, 0:n], oh1[:, :, 0:n], NEG, lg[:, :, 0:n], ALU.mult, ALU.add))
                chain(first_best(rest, top2, oh2, iota8, n))
                tt(rest[:, :, 0:n], lg[:, :, 0:n], bc(top1[:, :], 2, n), ALU.subtract).then_inc(rest_ready, 1)

            def kept3():
                dve.wait_ge(exp_ready, 2)
                red(exsum[:, :], ex[:, :, 0:n], X_AXIS, ALU.add)
                chain(tt(eqm[:, :, 0:n], oh1[:, :, 0:n], oh2[:, :, 0:n], ALU.add))
                nc.vector.reciprocal(rsum[:, :], exsum[:, :])
                chain(tt(prob[:, :, 0:n], ex[:, :, 0:n], eqm[:, :, 0:n], ALU.mult))
                chain(tt(prob[:, :, 0:n], prob[:, :, 0:n], bc(rsum[:, :], 2, n), ALU.mult))
                chain(red(exsum[:, :], prob[:, :, 0:n], X_AXIS, ALU.add))

            def gates3():
                chain(ts(exsum[:, :], exsum[:, :], 1e-9, None, ALU.add))
                chain(nc.vector.reciprocal(rsum[:, :], exsum[:, :]))
                tt(gate3[:, :, :], prob[:, :, 0:n], bc(rsum[:, :], 2, n), ALU.mult).then_inc(gate3_ready, 1)
                dve.wait_ge(gate3_ready, 1)

            units3 = [(e, k, h) for e in range(E3) for k in range(FCH3) for h in range(HALVES)]
            UNITS3 = FCH3 * HALVES

            def hidden3(u):
                e, k, h = units3[u]
                dve.wait_ge(silu3_ready, u + 1)
                dve.wait_ge(u3_ready, u + 1)
                if e >= 2 and u % UNITS3 == 0:
                    dve.wait_ge(y3_ready, 2 * (e - 2) + 2 + (2 if e >= 4 else 0))
                stt(hid[:, 0, (e % 2) * 2 + k, halves[h]], psum[:, 2 + u % 2, :],
                    field("l3_small", "up_b")[:, e * FCH3 + k:e * FCH3 + k + 1], silu3[:, u % 2, :],
                    ALU.add, ALU.mult).then_inc(hid3_ready, 1)

            def bias3(h):
                dve.wait_ge(y3_ready, 4 + h + 1)
                dve.wait_ge(y3_used, 2 + h + 1)
                tt(x_tok[:, 4 * h:4 * h + 4, :], psum[:, 4 + h, :].rearrange("p (t c) -> p t c", c=C),
                   x_tok[:, 4 * h:4 * h + 4, :], ALU.add).then_inc(y3_used, 1)

            def output3(g):
                e, h = g // 2, g % 2
                turn = e if e <= 1 else e + 1
                dve.wait_ge(y3_ready, 2 * turn + h + 1)
                if turn >= 1:
                    dve.wait_ge(y3_used, 2 * (turn - 1) + h + 1)
                for t in range(4 * h, 4 * h + 4):
                    last = stt(x_tok[:, t, :], psum[:, 4 + h, (t % 4) * C:(t % 4 + 1) * C], gate3[:, t, e:e + 1],
                               x_tok[:, t, :], ALU.mult, ALU.add)
                last.then_inc(y3_used, 1)

            first3()
            hidden3(0)
            second3()
            hidden3(1)
            kept3()
            hidden3(2)
            gates3()
            hidden3(3)
            dve.wait_ge(xtok_ready, 4)
            for e in range(E3):
                if e >= 1:
                    for u in range(e * UNITS3, (e + 1) * UNITS3):
                        hidden3(u)
                if e >= 1:
                    output3(2 * (e - 1))
                    output3(2 * (e - 1) + 1)
                if e == 2:
                    bias3(0)
                    bias3(1)
            output3(2 * (E3 - 1))
            output3(2 * (E3 - 1) + 1)


def layouts(inputs):
    import numpy as np

    f = {k: np.asarray(v) for k, v in inputs.items()}

    def rows(a, n=P):
        a = np.asarray(a)
        return np.concatenate([a, np.zeros((n - a.shape[0],) + a.shape[1:], a.dtype)]) if a.shape[0] < n else a

    def col(a):
        return rows(np.asarray(a).reshape(-1, 1))

    def cols(a):
        return np.asarray(a).reshape(-1, P).T

    def kmajor(a):
        return a.transpose(1, 0, 2).reshape(a.shape[1], -1)

    def chunked(a):
        return a.reshape(-1, P, a.shape[-1]).transpose(1, 0, 2).reshape(P, -1)

    p = np.arange(P)
    j, l = p[:, None] % S, np.arange(S)[None, :]
    own = np.repeat(np.eye(LANGS, dtype=bool), ADIM, axis=1)
    lang_ff = f["L0_cond_W1"].shape[0] * ADIM
    w2 = rows(f["L0_cond_W2"].reshape(lang_ff, C), 3 * P)
    fields = {
        "early": {"far": rows(np.where(own, 0.0, FAR)), "pidx": p[:, None], "eps": np.full((P, 1), EPS)},
        "l0_w1": {"w1": kmajor(f["L0_cond_W1"]), "b1": cols(rows(f["L0_cond_b1"].reshape(-1), 3 * P))},
        "consts": {
            "ident": np.eye(P), "eye32": j == l, "tri_batch": (p[:, None] // S == p // S) & (p[:, None] <= p),
            "ones_batch": p[:, None] // S == p // S, "tri_all": p[:, None] <= p,
            "same_expert": (p[:, None] % E1 == p % E1) & (p[:, None] >= E1),
            "mask_pre": np.where(l <= j, 0.0, NEG), "mask_post": np.where(l >= j, 0.0, NEG),
            "mask_cloze": np.where(l != j, 0.0, NEG),
            "counts": np.concatenate([j + 1, S - j, 0 * j + S - 1], 1),
            "iota16": np.tile(np.arange(E0) - E0, (P, 1)), "iota8": np.tile(np.arange(E3) - E3, (P, 1)),
            "steps": (p[:, None] // E1) * (2 * BOUND / 16.0 ** (1 + np.arange(ROUNDS)))[None, :],
            "eye8": rows(np.eye(8)),
            "batch_in_tile": p[:, None] // S == np.arange(BPT), "parity": p[:, None] // S % 2 == np.arange(2),
            "lo_w": p[:, None] // D2 % 2 == 1, "lo_x": p[:, None] // D2 >= 2,
            "slot_row": p[:, None] + 1 + P * np.arange(2),
        },
        "l0_small": {
            "table": rows(np.concatenate([f["L0_cond_b2"], f["L0_cond_gamma"], f["L0_cond_beta"]], 1)),
            "w2": chunked(w2), "router": f["L0_ffn_w_router"],
        },
        "l0_gatefc": {"gatefc": kmajor(np.concatenate([f["L0_ffn_w_gate"], f["L0_ffn_w_fc"]], 2))},
        "l0_proj": {"proj": rows(kmajor(f["L0_ffn_w_proj"]))},
        "l1_small": {
            "w1c": f["L1_cond_W1"], "b1c": col(f["L1_cond_b1"]), "v": col(f["L1_cond_v"]),
            "router": np.tile(f["L1_ffn_Wg"], (1, RANK_PARTS)), "b1": cols(f["L1_ffn_b1"]),
            "b2": rows(f["L1_ffn_b2"]),
        },
        "l1_w1": {"w1": kmajor(f["L1_ffn_W1"])},
        "l1_w2": {"w2": chunked(f["L1_ffn_W2"])},
        "l2_decay": {
            "blend": np.tile(f["cond_1024"].T, (1, 4)), "taus": col(np.tile(f["condB_tauraws"].reshape(-1), 4)),
            "tau_ctx": np.tile(f["L2_cond_tau_ctx"].reshape(1, 1), (P, 1)),
        },
        "l2_all": {
            "wg_x": f["L2_cond_Wg"][:, 0:C].T, "wg_ctx": f["L2_cond_Wg"][:, C:2 * C].T, "bg": col(f["L2_cond_bg"]),
            "wn1": f["L2_cond_Wn1"].T, "bn1": col(f["L2_cond_bn1"]), "wn2": rows(np.tile(f["cond_256"].T, (1, 4))),
            "bn2": col(np.tile(f["condB_bn2"].reshape(-1), 4)), "wtemp": f["L2_cond_Wtemp"].T,
            "btemp": col(f["L2_cond_btemp"]), "wsoma": f["L2_cond_Wsoma"].T, "bsoma": col(f["L2_cond_bsoma"]),
            "wout": f["L2_cond_Wout"].T, "gamma": col(f["L2_cond_gamma"]), "beta": col(f["L2_cond_beta"]),
            "u1": np.tile(f["L2_ffn_U1"], (1, 4)), "v1": np.tile(f["L2_ffn_V1"], (4, 1)), "b1": cols(f["L2_ffn_b1"]),
            "u2": chunked(f["L2_ffn_U2"]), "v2": np.tile(f["L2_ffn_V2"], (4, 1)), "b2": col(f["L2_ffn_b2"]),
        },
        "l3_small": {
            "cbias": rows(f["L3_cond_bias"]), "router": f["L3_ffn_router_w"].T, "gate_b": cols(f["L3_ffn_gate_b"]),
            "up_b": cols(f["L3_ffn_up_b"]), "down_b": rows(f["L3_ffn_down_b"]),
        },
        "l3_gate": {"gate": kmajor(f["L3_ffn_gate_w"])},
        "l3_up": {"up": kmajor(f["L3_ffn_up_w"])},
        "l3_down": {"down": chunked(f["L3_ffn_down_w"])},
    }
    arrays = {}
    for pack, names in PACKS.items():
        parts = [np.asarray(fields[pack][name]) for name, _ in names]
        for (name, width), part in zip(names, parts):
            assert part.shape == (P, width), (pack, name, part.shape)
        if pack in ("early", "consts"):
            parts = [np.asarray(part, np.float32) for part in parts]
        arrays[pack] = np.ascontiguousarray(np.concatenate(parts, 1))
    ids = np.concatenate([f["itok_B_0_8"], f["itok_B_0_2"], f["itok_B_0_7"]])
    arrays["ids"] = np.ascontiguousarray(np.tile(ids[None, :], (P, 1)))
    arrays["slot_no"] = np.tile(1 + np.arange(TOP1, dtype=np.float32), (P, 1))
    arrays["types"] = np.ascontiguousarray(np.repeat(f["itok_B_0_2"].reshape(TILES, BPT), S, axis=1).T)
    arrays["x"] = np.ascontiguousarray(f["x"].reshape(N, C))
    arrays["x_ch"] = np.ascontiguousarray(f["x"].reshape(N, C).T)
    arrays["subj_w"] = np.ascontiguousarray(f["L3_cond_weight"].transpose(0, 2, 1))
    return arrays


def kernel(**inputs):
    import concourse.bacc as bacc
    from concourse.bass_utils import run_bass_kernel_spmd

    arrays = layouts(inputs)
    nc = bacc.Bacc("TRN2", target_bir_lowering=False, num_devices=1)
    dram = {name: nc.dram_tensor("in_" + name, a.shape, mybir.dt.from_np(a.dtype), kind="ExternalInput").ap()
            for name, a in arrays.items()}
    out = nc.dram_tensor("out", (B, S, C), F32, kind="ExternalOutput").ap()
    program(nc, dram, out)
    r = run_bass_kernel_spmd(nc, [{"in_" + name: a for name, a in arrays.items()}], core_ids=[0])
    return r.results[0]["out"]
```
